# Optimizing a Trainium2 kernel written in Bass

```python
import numpy as np
import jax
import jax.numpy as jnp

def _softmax(x, axis=-1):
    return jax.nn.softmax(x, axis=axis)

def _gelu(x):
    return jax.nn.gelu(x, approximate=True)

def _silu(x):
    return jax.nn.silu(x)

def _sigmoid(x):
    return jax.nn.sigmoid(x)

def _layernorm(x, axis=-1, eps=1e-05):
    m = jnp.mean(x, axis=axis, keepdims=True)
    v = jnp.var(x, axis=axis, keepdims=True)
    return (x - m) / jnp.sqrt(v + eps)

def _scatter_add(tgt, idx, src, axis=0):
    return tgt.at[idx].add(src)

def _segment_sum(src, seg, n):
    return jax.ops.segment_sum(src, seg, n)
kernel_name = 'mk_gnn_resnorm_d4_gnn_r8_d339b7'

def setup_inputs(seed: int=0):
    np.random.seed(seed)
    _w = jnp.asarray

    def _rec_inputs():
        import jax
        import jax.numpy as jnp
        _gk = jax.random.key(seed)
        x = -0.0003713 + 1 * jax.random.normal(jax.random.fold_in(_gk, 1), (6250, 128), jnp.float32)
        _s = jax.random.randint(jax.random.fold_in(_gk, 2), (50000,), 0, 6250, jnp.int32)
        _d = jax.random.randint(jax.random.fold_in(_gk, 3), (50000,), 0, 6250, jnp.int32)
        _loop = jnp.arange(6250, dtype=jnp.int32)
        src = jnp.concatenate([_s, _d, _loop])
        dst = jnp.concatenate([_d, _s, _loop])
        _o = jnp.argsort(dst, stable=True)
        src = src[_o]
        dst = dst[_o]
        edge_type_4 = jax.random.randint(jax.random.fold_in(_gk, 12), (106250,), 0, 4, jnp.int32)
        edge_weight1 = 0.000452788 + 0.999756 * jax.random.normal(jax.random.fold_in(_gk, 13), (106250, 1), jnp.float32)
        node_type_3 = jax.random.randint(jax.random.fold_in(_gk, 14), (6250,), 0, 3, jnp.int32)
        return (x, src, dst, edge_type_4, edge_weight1, node_type_3)
    x, src, dst, edge_type_4, edge_weight1, node_type_3 = _rec_inputs()

    def _L0_gnn_setup():
        import jax, jax.numpy as jnp
        import numpy as np
        N = 12500
        E = 200000
        IN_DIM = 128
        OUT_DIM = 128
        H = 4
        HD = OUT_DIM // H
        NEG_SLOPE = 0.2
        EPS_SOFTMAX = 1e-08
        EPS_LN = 1e-05

        def _attention_aggregate(h_proj, sender, receiver, attn_vec, num_nodes):
            h_sender = h_proj[sender]
            h_receiver = h_proj[receiver]
            e = jnp.einsum('ehd,hd->eh', h_sender, attn_vec[:, :HD]) + jnp.einsum('ehd,hd->eh', h_receiver, attn_vec[:, HD:])
            e = jax.nn.leaky_relu(e, NEG_SLOPE)
            e_max = jax.ops.segment_max(e, receiver, num_segments=num_nodes)
            alpha = jnp.exp(e - e_max[receiver])
            alpha_sum = jax.ops.segment_sum(alpha, receiver, num_segments=num_nodes)
            alpha = alpha / (alpha_sum[receiver] + EPS_SOFTMAX)
            msg = h_sender * alpha[..., None]
            return jax.ops.segment_sum(msg, receiver, num_segments=num_nodes)
        key = jax.random.key(seed)
        ks = jax.random.split(key, 6)
        h = jax.random.normal(ks[0], (N, IN_DIM), dtype=jnp.float32)
        edge_index = jax.random.randint(ks[1], (2, E), 0, N, dtype=jnp.int32)
        W = jax.random.normal(ks[2], (IN_DIM, OUT_DIM), dtype=jnp.float32) / np.sqrt(IN_DIM)
        W_self = jax.random.normal(ks[3], (IN_DIM, OUT_DIM), dtype=jnp.float32) / np.sqrt(IN_DIM)
        a_in = jax.random.normal(ks[4], (H, 2 * HD), dtype=jnp.float32) * 0.01
        a_out = jax.random.normal(ks[5], (H, 2 * HD), dtype=jnp.float32) * 0.01
        bias = jnp.zeros((OUT_DIM,), dtype=jnp.float32)
        ln_gamma = jnp.ones((OUT_DIM,), dtype=jnp.float32)
        ln_beta = jnp.zeros((OUT_DIM,), dtype=jnp.float32)
        return {'h': h, 'edge_index': edge_index, 'W': W, 'W_self': W_self, 'a_in': a_in, 'a_out': a_out, 'bias': bias, 'ln_gamma': ln_gamma, 'ln_beta': ln_beta}
    _L0_gnn_all = _L0_gnn_setup()
    _L0_gnn_in = {k: v for k, v in _L0_gnn_all.items() if k in ('W', 'W_self', 'a_in', 'a_out', 'bias', 'ln_gamma', 'ln_beta')}
    del _L0_gnn_all

    def _L1_gnn_setup():
        import jax, jax.numpy as jnp
        import numpy as np
        N, E, IN, HID, H, DH, L, T, R = (6250, 100000, 128, 128, 4, 32, 2, 3, 4)

        def _typed_linear(x, W, b, node_type):
            out = jnp.zeros((x.shape[0], W.shape[-1]), x.dtype)
            for t in range(W.shape[0]):
                m = (node_type == t)[:, None]
                out = out + jnp.where(m, x @ W[t] + b[t], jnp.zeros((), x.dtype))
            return out

        def _segment_softmax(logits, seg, num_segments):
            mx = jax.ops.segment_max(logits, seg, num_segments=num_segments)
            ex = jnp.exp(logits - mx[seg])
            den = jax.ops.segment_sum(ex, seg, num_segments=num_segments)
            return ex / (den[seg] + 1e-16)

        def _hgt_layer(x, Wk, bk, Wq, bq, Wv, bv, Wa, ba, a_rel, m_rel, mu, skip, node_type, src, dst, edge_type):
            n = x.shape[0]
            k = _typed_linear(x, Wk, bk, node_type).reshape(n, H, DH)
            q = _typed_linear(x, Wq, bq, node_type).reshape(n, H, DH)
            v = _typed_linear(x, Wv, bv, node_type).reshape(n, H, DH)
            kt = jnp.einsum('nhd,rhde->rnhe', k, a_rel)
            vt = jnp.einsum('nhd,rhde->rnhe', v, m_rel)
            k_e = kt[edge_type, src]
            v_e = vt[edge_type, src]
            att = (q[dst] * k_e).sum(-1) * mu[edge_type] / np.sqrt(DH)
            alpha = _segment_softmax(att, dst, n)
            agg = jax.ops.segment_sum(v_e * alpha[..., None], dst, num_segments=n).reshape(n, H * DH)
            out = _typed_linear(jax.nn.gelu(agg), Wa, ba, node_type)
            a = jax.nn.sigmoid(skip)[node_type][:, None]
            return a * out + (1.0 - a) * x
        key = jax.random.key(seed)
        k = jax.random.split(key, 16)
        s = 0.05
        return {'x': jax.random.normal(k[0], (N, IN), jnp.float32), 'W_in': jax.random.normal(k[1], (T, IN, HID)) * s, 'b_in': jnp.zeros((T, HID), jnp.float32), 'Wk': jax.random.normal(k[2], (L, T, HID, HID)) * s, 'bk': jnp.zeros((L, T, HID), jnp.float32), 'Wq': jax.random.normal(k[3], (L, T, HID, HID)) * s, 'bq': jnp.zeros((L, T, HID), jnp.float32), 'Wv': jax.random.normal(k[4], (L, T, HID, HID)) * s, 'bv': jnp.zeros((L, T, HID), jnp.float32), 'Wa': jax.random.normal(k[5], (L, T, HID, HID)) * s, 'ba': jnp.zeros((L, T, HID), jnp.float32), 'a_rel': jax.random.normal(k[6], (L, R, H, DH, DH)) * 0.1, 'm_rel': jax.random.normal(k[7], (L, R, H, DH, DH)) * 0.1, 'mu': jnp.ones((L, R, H), jnp.float32), 'skip': jnp.ones((L, T), jnp.float32), 'node_type': jax.random.randint(k[8], (N,), 0, T), 'edge_index': jax.random.randint(k[9], (2, E), 0, N), 'edge_type': jax.random.randint(k[10], (E,), 0, R)}
    _L1_gnn_all = _L1_gnn_setup()
    _L1_gnn_in = {k: v for k, v in _L1_gnn_all.items() if k in ('W_in', 'b_in', 'Wk', 'bk', 'Wq', 'bq', 'Wv', 'bv', 'Wa', 'ba', 'a_rel', 'm_rel', 'mu', 'skip')}
    del _L1_gnn_all

    def _L2_gnn_setup():
        import jax, jax.numpy as jnp
        import numpy as np
        N = 12500
        E = 200000
        D = 128
        NEG_SLOPE = 0.1
        key = jax.random.key(seed)
        k1, k2, k3 = jax.random.split(key, 3)
        x = jax.random.normal(k1, (N, D), dtype=jnp.float32)
        edge_index = jax.random.randint(k2, (2, E), 0, N, dtype=jnp.int32)
        W = jax.random.normal(k3, (D, D), dtype=jnp.float32) / np.sqrt(D).astype(np.float32)
        b = jnp.zeros((D,), dtype=jnp.float32)
        return {'x': x, 'edge_index': edge_index, 'W': W, 'b': b}
    _L2_gnn_all = _L2_gnn_setup()
    _L2_gnn_in = {k: v for k, v in _L2_gnn_all.items() if k in ('W', 'b')}
    del _L2_gnn_all

    def _L3_gnn_setup():
        import jax, jax.numpy as jnp
        import numpy as np
        N, E, C = (6250, 200000, 128)
        BN_EPS = 1e-05
        key = jax.random.key(seed)
        ks = jax.random.split(key, 12)
        x = jax.random.normal(ks[0], (N, C), dtype=jnp.float32)
        edge_index = jax.random.randint(ks[1], (2, E), 0, N, dtype=jnp.int64)
        edge_attr = jax.random.normal(ks[2], (E, 1), dtype=jnp.float32)
        s = 1.0 / np.sqrt(C)
        edge_w = jax.random.uniform(ks[3], (1, C), jnp.float32, -1.0, 1.0)
        edge_b = jax.random.uniform(ks[4], (C,), jnp.float32, -1.0, 1.0)
        w1 = jax.random.uniform(ks[5], (C, C), jnp.float32, -s, s)
        b1 = jax.random.uniform(ks[6], (C,), jnp.float32, -s, s)
        w2 = jax.random.uniform(ks[7], (C, C), jnp.float32, -s, s)
        b2 = jax.random.uniform(ks[8], (C,), jnp.float32, -s, s)
        res_w = jax.random.uniform(ks[9], (C, C), jnp.float32, -s, s)
        res_b = jax.random.uniform(ks[10], (C,), jnp.float32, -s, s)
        eps = jnp.zeros((1,), jnp.float32)
        gamma = jnp.ones((C,), jnp.float32)
        beta = jnp.zeros((C,), jnp.float32)
        return {'x': x, 'edge_index': edge_index, 'edge_attr': edge_attr, 'edge_w': edge_w, 'edge_b': edge_b, 'w1': w1, 'b1': b1, 'w2': w2, 'b2': b2, 'res_w': res_w, 'res_b': res_b, 'eps': eps, 'gamma': gamma, 'beta': beta}
    _L3_gnn_all = _L3_gnn_setup()
    _L3_gnn_in = {k: v for k, v in _L3_gnn_all.items() if k in ('edge_w', 'edge_b', 'w1', 'b1', 'w2', 'b2', 'res_w', 'res_b', 'eps', 'gamma', 'beta')}
    del _L3_gnn_all
    return {'x': x, 'src': src, 'dst': dst, 'edge_type_4': edge_type_4, 'edge_weight1': edge_weight1, 'node_type_3': node_type_3, 'L0_gnn_W': _L0_gnn_in['W'], 'L0_gnn_W_self': _L0_gnn_in['W_self'], 'L0_gnn_a_in': _L0_gnn_in['a_in'], 'L0_gnn_a_out': _L0_gnn_in['a_out'], 'L0_gnn_bias': _L0_gnn_in['bias'], 'L0_gnn_ln_gamma': _L0_gnn_in['ln_gamma'], 'L0_gnn_ln_beta': _L0_gnn_in['ln_beta'], 'L1_gnn_W_in': _L1_gnn_in['W_in'], 'L1_gnn_b_in': _L1_gnn_in['b_in'], 'L1_gnn_Wk': _L1_gnn_in['Wk'], 'L1_gnn_bk': _L1_gnn_in['bk'], 'L1_gnn_Wq': _L1_gnn_in['Wq'], 'L1_gnn_bq': _L1_gnn_in['bq'], 'L1_gnn_Wv': _L1_gnn_in['Wv'], 'L1_gnn_bv': _L1_gnn_in['bv'], 'L1_gnn_Wa': _L1_gnn_in['Wa'], 'L1_gnn_ba': _L1_gnn_in['ba'], 'L1_gnn_a_rel': _L1_gnn_in['a_rel'], 'L1_gnn_m_rel': _L1_gnn_in['m_rel'], 'L1_gnn_mu': _L1_gnn_in['mu'], 'L1_gnn_skip': _L1_gnn_in['skip'], 'L2_gnn_W': _L2_gnn_in['W'], 'L2_gnn_b': _L2_gnn_in['b'], 'L3_gnn_edge_w': _L3_gnn_in['edge_w'], 'L3_gnn_edge_b': _L3_gnn_in['edge_b'], 'L3_gnn_w1': _L3_gnn_in['w1'], 'L3_gnn_b1': _L3_gnn_in['b1'], 'L3_gnn_w2': _L3_gnn_in['w2'], 'L3_gnn_b2': _L3_gnn_in['b2'], 'L3_gnn_res_w': _L3_gnn_in['res_w'], 'L3_gnn_res_b': _L3_gnn_in['res_b'], 'L3_gnn_eps': _L3_gnn_in['eps'], 'L3_gnn_gamma': _L3_gnn_in['gamma'], 'L3_gnn_beta': _L3_gnn_in['beta']}

def reference(x, src, dst, edge_type_4, edge_weight1, node_type_3, L0_gnn_W, L0_gnn_W_self, L0_gnn_a_in, L0_gnn_a_out, L0_gnn_bias, L0_gnn_ln_gamma, L0_gnn_ln_beta, L1_gnn_W_in, L1_gnn_b_in, L1_gnn_Wk, L1_gnn_bk, L1_gnn_Wq, L1_gnn_bq, L1_gnn_Wv, L1_gnn_bv, L1_gnn_Wa, L1_gnn_ba, L1_gnn_a_rel, L1_gnn_m_rel, L1_gnn_mu, L1_gnn_skip, L2_gnn_W, L2_gnn_b, L3_gnn_edge_w, L3_gnn_edge_b, L3_gnn_w1, L3_gnn_b1, L3_gnn_w2, L3_gnn_b2, L3_gnn_res_w, L3_gnn_res_b, L3_gnn_eps, L3_gnn_gamma, L3_gnn_beta):
    import jax
    import jax.numpy as jnp

    def _L0_gnn_ref(h, edge_index, W, W_self, a_in, a_out, bias, ln_gamma, ln_beta):
        import jax, jax.numpy as jnp
        import numpy as np
        N = 12500
        E = 200000
        IN_DIM = 128
        OUT_DIM = 128
        H = 4
        HD = OUT_DIM // H
        NEG_SLOPE = 0.2
        EPS_SOFTMAX = 1e-08
        EPS_LN = 1e-05

        def _attention_aggregate(h_proj, sender, receiver, attn_vec, num_nodes):
            h_sender = h_proj[sender]
            h_receiver = h_proj[receiver]
            e = jnp.einsum('ehd,hd->eh', h_sender, attn_vec[:, :HD]) + jnp.einsum('ehd,hd->eh', h_receiver, attn_vec[:, HD:])
            e = jax.nn.leaky_relu(e, NEG_SLOPE)
            e_max = jax.ops.segment_max(e, receiver, num_segments=num_nodes)
            alpha = jnp.exp(e - e_max[receiver])
            alpha_sum = jax.ops.segment_sum(alpha, receiver, num_segments=num_nodes)
            alpha = alpha / (alpha_sum[receiver] + EPS_SOFTMAX)
            msg = h_sender * alpha[..., None]
            return jax.ops.segment_sum(msg, receiver, num_segments=num_nodes)
        n = h.shape[0]
        h_proj = (h @ W).reshape(n, H, HD)
        h_self = h @ W_self
        src, dst = (edge_index[0], edge_index[1])
        h_in = _attention_aggregate(h_proj, src, dst, a_in, n)
        h_out = _attention_aggregate(h_proj, dst, src, a_out, n)
        combined = h_self + h_in.reshape(n, -1) + h_out.reshape(n, -1) + bias
        mean = combined.mean(axis=-1, keepdims=True)
        var = combined.var(axis=-1, keepdims=True)
        normed = (combined - mean) * jax.lax.rsqrt(var + EPS_LN)
        return normed * ln_gamma + ln_beta

    def _L1_gnn_ref(x, W_in, b_in, Wk, bk, Wq, bq, Wv, bv, Wa, ba, a_rel, m_rel, mu, skip, node_type, edge_index, edge_type):
        import jax, jax.numpy as jnp
        import numpy as np
        N, E, IN, HID, H, DH, L, T, R = (6250, 100000, 128, 128, 4, 32, 2, 3, 4)

        def _typed_linear(x, W, b, node_type):
            out = jnp.zeros((x.shape[0], W.shape[-1]), x.dtype)
            for t in range(W.shape[0]):
                m = (node_type == t)[:, None]
                out = out + jnp.where(m, x @ W[t] + b[t], jnp.zeros((), x.dtype))
            return out

        def _segment_softmax(logits, seg, num_segments):
            mx = jax.ops.segment_max(logits, seg, num_segments=num_segments)
            ex = jnp.exp(logits - mx[seg])
            den = jax.ops.segment_sum(ex, seg, num_segments=num_segments)
            return ex / (den[seg] + 1e-16)

        def _hgt_layer(x, Wk, bk, Wq, bq, Wv, bv, Wa, ba, a_rel, m_rel, mu, skip, node_type, src, dst, edge_type):
            n = x.shape[0]
            k = _typed_linear(x, Wk, bk, node_type).reshape(n, H, DH)
            q = _typed_linear(x, Wq, bq, node_type).reshape(n, H, DH)
            v = _typed_linear(x, Wv, bv, node_type).reshape(n, H, DH)
            kt = jnp.einsum('nhd,rhde->rnhe', k, a_rel)
            vt = jnp.einsum('nhd,rhde->rnhe', v, m_rel)
            k_e = kt[edge_type, src]
            v_e = vt[edge_type, src]
            att = (q[dst] * k_e).sum(-1) * mu[edge_type] / np.sqrt(DH)
            alpha = _segment_softmax(att, dst, n)
            agg = jax.ops.segment_sum(v_e * alpha[..., None], dst, num_segments=n).reshape(n, H * DH)
            out = _typed_linear(jax.nn.gelu(agg), Wa, ba, node_type)
            a = jax.nn.sigmoid(skip)[node_type][:, None]
            return a * out + (1.0 - a) * x
        src, dst = (edge_index[0], edge_index[1])
        h = _typed_linear(x, W_in, b_in, node_type)
        for l in range(L):
            h = _hgt_layer(h, Wk[l], bk[l], Wq[l], bq[l], Wv[l], bv[l], Wa[l], ba[l], a_rel[l], m_rel[l], mu[l], skip[l], node_type, src, dst, edge_type)
        return h

    def _L2_gnn_ref(x, edge_index, W, b):
        import jax, jax.numpy as jnp
        import numpy as np
        N = 12500
        E = 200000
        D = 128
        NEG_SLOPE = 0.1
        n = x.shape[0]
        loops = jnp.arange(n, dtype=edge_index.dtype)
        src = jnp.concatenate([edge_index[0], loops])
        dst = jnp.concatenate([edge_index[1], loops])
        deg = jax.ops.segment_sum(jnp.ones_like(dst, dtype=x.dtype), dst, num_segments=n)
        dinv = jnp.where(deg > 0, jax.lax.rsqrt(deg), 0.0)
        norm = dinv[src] * dinv[dst]
        h = x @ W
        msgs = h[src] * norm[:, None]
        agg = jax.ops.segment_sum(msgs, dst, num_segments=n) + b
        act = jnp.where(agg >= 0, agg, NEG_SLOPE * agg)
        return act + x

    def _L3_gnn_ref(x, edge_index, edge_attr, edge_w, edge_b, w1, b1, w2, b2, res_w, res_b, eps, gamma, beta):
        import jax, jax.numpy as jnp
        import numpy as np
        N, E, C = (6250, 200000, 128)
        BN_EPS = 1e-05
        src, dst = (edge_index[0], edge_index[1])
        ea = edge_attr @ edge_w + edge_b
        message = x[src] + ea
        sums = jax.ops.segment_sum(message, dst, num_segments=x.shape[0])
        cnt = jax.ops.segment_sum(jnp.ones((message.shape[0],), x.dtype), dst, num_segments=x.shape[0])
        aggr = sums / jnp.maximum(cnt, 1.0)[:, None]
        h = (1.0 + eps[0]) * x + aggr
        out = jax.nn.relu(h @ w1 + b1) @ w2 + b2
        out = out + (x @ res_w + res_b)
        mean = jnp.mean(out, axis=0)
        var = jnp.var(out, axis=0)
        out = (out - mean) * jax.lax.rsqrt(var + BN_EPS) * gamma + beta
        return jax.nn.relu(out)
    edge_index = jnp.stack([src, dst])
    x = _layernorm(x + _L0_gnn_ref(x, edge_index, L0_gnn_W, L0_gnn_W_self, L0_gnn_a_in, L0_gnn_a_out, L0_gnn_bias, L0_gnn_ln_gamma, L0_gnn_ln_beta), axis=-1)
    x = _layernorm(x + _L1_gnn_ref(x, L1_gnn_W_in, L1_gnn_b_in, L1_gnn_Wk, L1_gnn_bk, L1_gnn_Wq, L1_gnn_bq, L1_gnn_Wv, L1_gnn_bv, L1_gnn_Wa, L1_gnn_ba, L1_gnn_a_rel, L1_gnn_m_rel, L1_gnn_mu, L1_gnn_skip, node_type_3, edge_index, edge_type_4), axis=-1)
    x = _layernorm(x + _L2_gnn_ref(x, edge_index, L2_gnn_W, L2_gnn_b), axis=-1)
    x = _layernorm(x + _L3_gnn_ref(x, edge_index, edge_weight1, L3_gnn_edge_w, L3_gnn_edge_b, L3_gnn_w1, L3_gnn_b1, L3_gnn_w2, L3_gnn_b2, L3_gnn_res_w, L3_gnn_res_b, L3_gnn_eps, L3_gnn_gamma, L3_gnn_beta), axis=-1)
    return x

_drawn_inputs = setup_inputs


def setup_inputs(seed=0):
    import zlib

    import numpy as np

    out = dict(_drawn_inputs(seed))
    spreads = {'L0_gnn_bias': (0.0, 0.1),
     'L0_gnn_ln_gamma': (1.0, 0.2),
     'L0_gnn_ln_beta': (0.0, 0.1),
     'L1_gnn_b_in': (0.0, 0.8),
     'L1_gnn_bk': (0.0, 0.8),
     'L1_gnn_bq': (0.0, 0.8),
     'L1_gnn_bv': (0.0, 0.8),
     'L1_gnn_ba': (0.0, 0.1),
     'L1_gnn_mu': (1.0, 0.6),
     'L1_gnn_skip': (1.0, 0.6),
     'L2_gnn_b': (0.0, 0.1),
     'L3_gnn_gamma': (1.0, 0.2),
     'L3_gnn_beta': (0.0, 0.1)}
    factors = {'L0_gnn_a_in': 7.143,
     'L0_gnn_a_out': 7.145,
     'L1_gnn_Wk': 8.0,
     'L1_gnn_Wq': 8.0,
     'L1_gnn_Wv': 8.0,
     'L1_gnn_Wa': 8.0,
     'L1_gnn_a_rel': 8.0,
     'L1_gnn_m_rel': 8.0,
     'L3_gnn_b1': 4.035,
     'L3_gnn_b2': 8.0,
     'L3_gnn_res_b': 8.0}
    for name, (base, spread) in spreads.items():
        noise = np.random.default_rng([zlib.crc32(name.encode()), seed]).standard_normal(out[name].shape)
        drawn = base * np.exp(spread * noise) if base else spread * noise
        out[name] = jnp.asarray(drawn.astype(out[name].dtype))
    for name, factor in factors.items():
        out[name] = (out[name] * factor).astype(out[name].dtype)
    return out
```

```python
from contextlib import ExitStack

import concourse.bass as bass
from concourse import mybir

P = 128
N = 6250
E = 106250
D = 128
H = 4
HD = D // H
R = 4
T = 3
NB = -(-N // P)
NP = NB * P
EC = -(-E // (P * 16)) * 16
NT = 880
assert (P * EC + NB * (P - 1)) // P <= NT and P * EC >= E
NTP = 896
TB = NTP // 32
CH = 8
NI = NT // CH // 2
EI = EC // CH // 2
BIG = 1.0e30
RW = 4
W0 = D + 2 * H

ALU = mybir.AluOpType
ACT = mybir.ActivationFunctionType
AX = mybir.AxisListType
F32 = mybir.dt.float32
BF16 = mybir.dt.bfloat16
I32 = mybir.dt.int32
U32 = mybir.dt.uint32
ds = bass.ds


class Space:

    def __init__(self, nc, tag):
        self.nc, self.tag, self.ctx, self.sems = nc, tag, ExitStack(), []

    def __enter__(self):
        self.ctx.__enter__()
        return self

    def __exit__(self, *a):
        self.ctx.__exit__(*a)
        if a[0] is None:
            self.nc.clear_and_free_semaphores(self.sems)
            self.nc.all_engine_barrier()

    def sb(self, name, shape, dt=F32):
        return self.ctx.enter_context(self.nc.sbuf_tensor(f"{self.tag}_{name}", shape, dt))

    def ps(self, name, shape, dt=F32):
        return self.ctx.enter_context(self.nc.psum_tensor(f"{self.tag}_{name}", shape, dt))

    def sem(self, name):
        self.sems.append(self.nc.alloc_semaphore(f"{self.tag}_{name}"))
        return self.sems[-1]

    def block(self):
        return self.ctx.enter_context(self.nc.Block())


class Passed:

    def __init__(self, pool, sem):
        self.pool, self.sem = pool, sem

    def __call__(self):
        self.pool.sem_inc(self.sem, 1)


class Chain:

    def __init__(self, eng, sem):
        self.eng, self.sem, self.n = eng, sem, 0

    def __call__(self, ins):
        self.n += 1
        ins.then_inc(self.sem, 1)
        self.eng.wait_ge(self.sem, self.n)


def pairs(eng, count, chunk):
    for b in (0, 1):
        chunk(b, 0, b, True)
    with eng.Fori(1, count) as i:
        for b in (0, 1):
            chunk(i * 2 + b, i, b, False)


def tiles(eng, count, tile):
    for b in (0, 1):
        tile(b, 0, b, True)
    with eng.Fori(1, count // 2) as i:
        for b in (0, 1):
            tile(i * 2 + b, i, b, False)
    if count % 2:
        tile(count - 1, count // 2, 0, False)


def old(c, by=2):
    return not isinstance(c, int) or c >= by


def pipeline(eng, n, *stages):
    leads = [lead for _, lead in stages]
    first, last = -max(leads), n - min(leads)
    begin = (2 - min(leads) + 1) // 2
    end = max((n - max(leads)) // 2, begin)

    def step(s, i, b):
        for stage, lead in stages:
            if not isinstance(s, int) or 0 <= s + lead < n:
                stage(s + lead, i + (b + lead) // 2, (b + lead) % 2)

    for t in range(first, 2 * begin):
        step(t, t // 2, t % 2)
    if end > begin:
        with eng.Fori(begin, end) as i:
            for b in (0, 1):
                step(i * 2 + b, i, b)
    for t in range(2 * end, last):
        step(t, t // 2, t % 2)


def rows(dram):
    return dram.rearrange("(n p) w -> p n w", p=P)


def move(v, out, in_):
    return v.tensor_scalar(out, in_, 1.0, None, ALU.mult)


def cols3(ap):
    return ap.rearrange("p (a b) -> p a b", b=1)



def load_inputs(nc, g, a):
    with Space(nc, "ld") as s:
        loaded, made, chain, cast = s.sem("loaded"), s.sem("made"), s.sem("chain"), s.sem("cast")
        keys = s.sb("keys", [P, 3, EC], I32)
        types = s.sb("types", [P, NB], I32)
        lo = s.sb("lo", [P, EC], I32)
        hi = s.sb("hi", [P, EC], I32)
        full = E // EC
        block = s.block()

        @block.sync
        def _(sp):
            sp.wait_ge(chain, 3)
            sp.dma_start(g.X[:, 0:NB - 1, :], a.x[0:(NB - 1) * P, :].rearrange("(n p) w -> p n w", p=P)).then_inc(loaded, 16)
            sp.dma_start(g.X[0:N - (NB - 1) * P, NB - 1, :], a.x[(NB - 1) * P:N, :]).then_inc(loaded, 16)
            for k, src in enumerate((a.src, a.dst, a.edge_type)):
                sp.dma_start(keys[0:full, k, :], src[0:full * EC].rearrange("(p c) -> p c", c=EC)).then_inc(loaded, 16)
                sp.dma_start(keys[full:full + 1, k, 0:E - full * EC],
                             src[full * EC:E].rearrange("(p c) -> p c", p=1)).then_inc(loaded, 16)
            w = a.edge_weight.rearrange("e o -> (e o)")
            sp.dma_start(g.EW[0:full, :], w[0:full * EC].rearrange("(p c) -> p c", c=EC)).then_inc(loaded, 16)
            sp.dma_start(g.EW[full:full + 1, 0:E - full * EC],
                         w[full * EC:E].rearrange("(p c) -> p c", p=1)).then_inc(loaded, 16)
            with nc.allow_non_contiguous_dma(reason="one word a node, once"):
                sp.dma_start(types[:, 0:NB - 1], a.node_type[0:(NB - 1) * P].rearrange("(n p) -> p n", p=P)).then_inc(loaded, 16)
                sp.dma_start(types[0:N - (NB - 1) * P, NB - 1:NB],
                             a.node_type[(NB - 1) * P:N].rearrange("(p o) -> p o", o=1)).then_inc(loaded, 16)
            sp.wait_ge(loaded, 12 * 16)

        @block.gpsimd
        def _(pool):
            pool.memset(g.ident[:, :], 0.0).then_inc(made, 1)
            pool.iota(g.iota[:, :], pattern=[[1, P]], base=0, channel_multiplier=0,
                      allow_small_or_imprecise_dtypes=True).then_inc(made, 1)
            pool.memset(g.before[:, :], 1.0).then_inc(made, 1)
            pool.wait_ge(made, 3)
            pool.affine_select(out=g.ident[:, :], in_=g.ident[:, :], compare_op=ALU.not_equal, fill=1.0,
                               base=0, pattern=[[-1, P]], channel_multiplier=1).then_inc(made, 1)
            pool.affine_select(out=g.before[:, :], in_=g.before[:, :], compare_op=ALU.is_gt, fill=0.0,
                               base=0, pattern=[[1, P]], channel_multiplier=-1).then_inc(made, 1)

        @block.vector
        def _(v):
            link = Chain(v, chain)
            link(v.memset(keys[:, :, :], 0))
            link(v.memset(types[:, :], 0))
            v.memset(g.EW[:, :], 0.0)
            v.memset(g.X[:, :, :], 0.0)
            v.memset(g.ones[:, :], 1.0)
            v.memset(g.zeros[:, :], 0.0)
            link(v.memset(keys[:, 0:2, :], NP - 1))
            v.wait_ge(made, 5)
            v.tensor_copy(g.iota_b[:, :], g.iota[:, :])
            v.tensor_copy(g.ident_b[:, :], g.ident[:, :])
            v.wait_ge(loaded, 12 * 16)
            for k in (0, 1):
                v.tensor_copy(g.NODE[:, k, :], keys[:, k, :])
                v.tensor_scalar(lo[:, :], keys[:, k, :], P - 1, None, ALU.bitwise_and)
                link(v.tensor_scalar(hi[:, :], keys[:, k, :], 7, None, ALU.arith_shift_right))
                v.tensor_copy(g.DIG[:, k, :, 0], lo[:, :])
                link(v.tensor_copy(g.DIG[:, k, :, 1], hi[:, :]))
            for t in range(T):
                v.tensor_scalar(g.TM[:, :, t], types[:, :], float(t), None, ALU.is_equal)
            link(v.tensor_copy(g.ET[:, :], keys[:, 2, :]))



def count_keys(nc, g, k, tag):
    with Space(nc, tag) as s:
        staged, hot, counted = s.sem("staged"), s.sem("hot"), s.sem("counted")
        chain, summed, made = s.sem("chain"), s.sem("summed"), s.sem("made")
        dig = s.sb("dig", [P, 2, CH, 2])
        olo = s.sb("olo", [P, 2, CH, P], BF16)
        ohi = s.sb("ohi", [P, 2, CH, NB], BF16)
        zero = s.sb("zero", [P, P], BF16)
        tot = s.sb("tot", [P, NB])
        toti = s.sb("toti", [P, NB], I32)
        end = s.sb("end", [P, NB])
        diag = s.sb("diag", [NB, NB])
        endc = s.sb("endc", [NB, 1])
        first = s.sb("first", [NB, NT])
        full = s.sb("full", [NB, NT])
        pc = s.ps("pc", [P, 512])
        pt = s.ps("pt", [P, 512])
        pu = s.ps("pu", [P, 512])
        pn = s.ps("pn", [P, 2, 512])
        block = s.block()
        HT = NT // 2

        @block.gpsimd
        def _(pool):
            pool.iota(first[:, :], pattern=[[P, NT]], base=0, channel_multiplier=0,
                      allow_small_or_imprecise_dtypes=True).then_inc(made, 1)

        @block.vector
        def _(v):
            v.memset(zero[:, :], 0.0).then_inc(hot, 1)

            def chunk(c, i, b, first):
                move(v, dig[:, b, :, :], g.DIG[:, k, ds(c * CH, CH), :]).then_inc(staged, 1)
                v.wait_ge(staged, c + 1)
                if not first:
                    v.wait_ge(counted, c - 1)
                for j in range(CH):
                    v.tensor_scalar(olo[:, b, j, :], g.iota_b[:, :], dig[:, b, j, 0:1], None, ALU.is_equal)
                    last = v.tensor_scalar(ohi[:, b, j, :], g.iota_b[:, 0:NB], dig[:, b, j, 1:2], None, ALU.is_equal)
                last.then_inc(hot, 1)

            pairs(v, EI, chunk)
            link = Chain(v, chain)
            v.wait_ge(counted, 2 * EI + 1)
            link(v.tensor_copy(g.CNT[:, k, :], pc[:, 0:NB]))
            v.wait_ge(summed, 2)
            link(v.tensor_scalar(tot[:, :], pt[:, 0:NB], float(P - 1), None, ALU.add))
            link(v.tensor_copy(toti[:, :], tot[:, :]))
            link(v.tensor_scalar(toti[:, :], toti[:, :], 7, 7, ALU.arith_shift_right, ALU.logical_shift_left))
            link(v.tensor_copy(tot[:, :], toti[:, :]))
            link(v.tensor_tensor_scan(end[:, :], tot[:, :], g.zeros[:, 0:NB], 0.0, ALU.add, ALU.add))
            link(v.tensor_tensor(tot[:, :], end[:, :], tot[:, :], ALU.subtract))
            link(v.tensor_tensor(g.START[:, k, :], pu[:, 0:NB], tot[:, :], ALU.add))
            link(v.tensor_tensor(diag[:, :], end[0:NB, :], g.ident[0:NB, 0:NB], ALU.mult))
            link(v.tensor_reduce(endc[:, :], diag[:, :], AX.X, ALU.add))
            v.wait_ge(made, 1)
            v.tensor_scalar(full[:, :], first[:, :], endc[:, 0:1], None, ALU.is_ge).then_inc(summed, 1)
            v.wait_ge(summed, 5)
            for q in (0, 1):
                link(v.tensor_scalar(g.BIN[:, k, q * HT:(q + 1) * HT], pn[:, q, 0:HT], float(NB - 1), None, ALU.min))
            link(v.tensor_copy(g.BINI[:, k, :], g.BIN[0:1, k, :]))
            v.tensor_tensor(g.TF[:, k, 0, 1:NT], g.BIN[:, k, 1:NT], g.BIN[:, k, 0:NT - 1], ALU.not_equal)
            link(v.memset(g.TF[:, k, 0, 0:1], 1.0))
            link(v.memset(g.TF[:, k, 1, NT - 1:NT], 1.0))
            link(v.tensor_copy(g.TF[:, k, 1, 0:NT - 1], g.TF[:, k, 0, 1:NT]))
            link(v.tensor_scalar(g.TF[:, k, :, :], g.TF[:, k, :, :], -BIG, None, ALU.mult))

        @block.tensor
        def _(pe):
            pe.wait_ge(hot, 1)
            pe.matmul(pc[:, 0:NB], zero[:, :], zero[:, 0:NB], start=True, stop=False, skip_group_check=True)

            def chunk(c, i, b, first):
                pe.wait_ge(hot, c + 2)
                for j in range(CH):
                    last = pe.matmul(pc[:, 0:NB], olo[:, b, j, :], ohi[:, b, j, :], start=False, stop=False,
                                     skip_group_check=True)
                last.then_inc(counted, 1)

            pairs(pe, EI, chunk)
            pe.matmul(pc[:, 0:NB], zero[:, :], zero[:, 0:NB], start=False, stop=True,
                      skip_group_check=True).then_inc(counted, 1)
            pe.wait_ge(chain, 1)
            pe.matmul(pt[:, 0:NB], g.ones[:, :], g.CNT[:, k, :], start=True, stop=True).then_inc(summed, 1)
            pe.matmul(pu[:, 0:NB], g.before[:, :], g.CNT[:, k, :], start=True, stop=True).then_inc(summed, 1)
            pe.wait_ge(summed, 3)
            for q in (0, 1):
                pe.matmul(pn[:, q, 0:HT], g.ones[0:NB, :], full[:, q * HT:(q + 1) * HT],
                          start=True, stop=True).then_inc(summed, 1)


def place_edges(nc, g, k, slots, tag):
    with Space(nc, tag) as s:
        staged, hot, turned, copied_b = s.sem("staged"), s.sem("hot"), s.sem("turned"), s.sem("copied_b")
        copied_f, equal, kept, tally = s.sem("copied_f"), s.sem("equal"), s.sem("kept"), s.sem("tally")
        tallied, carried, seen_ok, found = s.sem("tallied"), s.sem("carried"), s.sem("seen_ok"), s.sem("found")
        picked, ranked, index_ok, small = s.sem("picked"), s.sem("ranked"), s.sem("index_ok"), s.sem("small")
        sent = [s.sem(f"sent{q}") for q in range(4)]
        cleared, reset_ok, zeroed = s.sem("cleared"), s.sem("reset_ok"), s.sem("zeroed")
        dig = s.sb("dig", [P, 2, CH, 2])
        rec = s.sb("rec", [P, 2, CH, RW])
        olo = s.sb("olo", [P, 2, CH, P], BF16)
        ohi = s.sb("ohi", [P, 2, CH, NB], BF16)
        otb = s.sb("otb", [P, 2, CH, P], BF16)
        otf = s.sb("otf", [P, 2, CH, P])
        bm = s.sb("bm", [P, 2, CH, P], BF16)
        before = s.sb("before", [P, CH, P])
        reset = s.sb("reset", [P, NB, CH + 1])
        seq = s.sb("seq", [P, 2, NB, CH + 1])
        seen = s.sb("seen", [P, 2, NB, CH + 1])
        hits = s.sb("hits", [P, 2, CH, NB])
        pos = s.sb("pos", [P, 2, CH])
        posi = s.sb("posi", [P, 2, 3, CH], I32)
        idx = s.sb("idx", [P, 2, CH], U32)
        zrow = s.sb("zrow", [P, NT * RW])
        pt = s.ps("pt", [P, 1, CH, P], BF16)
        pe_q = s.ps("pe_q", [P, CH, P])
        pd = s.ps("pd", [P, 2, 512])
        pr = s.ps("pr", [P, 2, 512])
        waited = s.sem("waited")
        block = s.block()

        @block.sync
        def _(sp):
            sp.wait_ge(zeroed, 1)
            for q in range(4):
                sp.dma_start(slots[q].rearrange("(p c) w -> p (c w)", p=P), zrow[:, :]).then_inc(cleared, 16)
            sp.wait_ge(cleared, 64)

        @block.vector
        def _(v):
            v.memset(zrow[:, :], 0.0).then_inc(zeroed, 1)
            v.memset(reset[:, :, :], 1.0).then_inc(reset_ok, 1)
            v.wait_ge(reset_ok, 1)
            v.memset(reset[:, :, 0:1], 0.0)
            for j in range(CH):
                v.tensor_copy(before[:, j, :], g.before[:, :])
            v.tensor_copy(seen[:, 1, :, CH], g.START[:, k, :]).then_inc(seen_ok, 1)

            def stage(c, i, b):
                move(v, dig[:, b, :, :], g.DIG[:, k, ds(c * CH, CH), :]).then_inc(staged, 1)

            def one_hots(c, i, b):
                v.wait_ge(staged, c + 1)
                if old(c):
                    v.wait_ge(found, c - 1)
                for j in range(CH):
                    v.tensor_scalar(olo[:, b, j, :], g.iota_b[:, :], dig[:, b, j, 0:1], None, ALU.is_equal)
                    last = v.tensor_scalar(ohi[:, b, j, :], g.iota_b[:, 0:NB], dig[:, b, j, 1:2], None, ALU.is_equal)
                last.then_inc(hot, 1)

            def keep_earlier(c, i, b):
                v.wait_ge(equal, c + 1)
                v.tensor_tensor(bm[:, b, :, :], pe_q[:, :, :], before[:, :, :], ALU.mult).then_inc(kept, 1)

            def count_up(c, i, b):
                v.wait_ge(seen_ok, c + 1)
                v.tensor_copy(seq[:, b, :, 0], seen[:, 1 - b, :, CH])
                v.wait_ge(tally, c + 1)
                v.tensor_copy(seq[:, b, :, 1:CH + 1],
                              pd[:, b, 0:CH * NB].rearrange("p (j h) -> p h j", j=CH)).then_inc(carried, 1)
                v.wait_ge(carried, c + 1)
                v.tensor_tensor_scan(seen[:, b, :, :].rearrange("p h j -> p (h j)"),
                                     reset[:, :, :].rearrange("p h j -> p (h j)"),
                                     seq[:, b, :, :].rearrange("p h j -> p (h j)"), 0.0,
                                     ALU.mult, ALU.add).then_inc(seen_ok, 1)

            def finish(c, i, b):
                v.wait_ge(found, c + 1)
                v.tensor_tensor(hits[:, b, :, :], pr[:, b, 0:CH * NB].rearrange("p (j h) -> p j h", j=CH),
                                ohi[:, b, :, :], ALU.mult).then_inc(picked, 1)
                if old(c):
                    for q in range(4):
                        v.wait_ge(sent[q], (c - 1) * (CH // 4 * 16))
                move(v, rec[:, b, :, 0], g.NODE[:, 1 - k, ds(c * CH, CH)])
                v.wait_ge(picked, c + 1)
                v.tensor_reduce(pos[:, b, :], hits[:, b, :, :], AX.X, ALU.add).then_inc(ranked, 1)
                v.tensor_scalar(rec[:, b, :, 1], g.DIG[:, k, ds(c * CH, CH), 0], 1.0, None, ALU.add)
                v.wait_ge(ranked, c + 1)
                v.tensor_copy(posi[:, b, 0, :], pos[:, b, :]).then_inc(small, 1)
                move(v, rec[:, b, :, 2], g.ET[:, ds(c * CH, CH)])
                v.wait_ge(small, c * 2 + 1)
                v.tensor_scalar(posi[:, b, 1, :], posi[:, b, 0, :], P - 1, None, ALU.bitwise_and)
                v.tensor_scalar(posi[:, b, 2, :], posi[:, b, 0, :], 7, None, ALU.arith_shift_right).then_inc(small, 1)
                move(v, rec[:, b, :, 3], g.EW[:, ds(c * CH, CH)])
                v.wait_ge(small, c * 2 + 2)
                v.scalar_tensor_tensor(out=idx[:, b, :], in0=posi[:, b, 1, :], scalar=float(NT),
                                       in1=posi[:, b, 2, :], op0=ALU.mult, op1=ALU.add).then_inc(index_ok, 1)

            pipeline(v, 2 * EI, (finish, -1), (one_hots, 1), (keep_earlier, 0), (count_up, 0), (stage, 2))

        @block.tensor
        def _(pe):
            def turn_and_tally(c, i, b):
                pe.wait_ge(hot, c + 1)
                if old(c, 1):
                    pe.wait_ge(copied_f, c)
                    pe.wait_ge(copied_b, c)
                for j in range(CH):
                    last = pe.transpose(pt[:, 0, j, :], olo[:, b, j, :], g.ident_b[:, :])
                last.then_inc(turned, 1)
                if old(c):
                    pe.wait_ge(carried, c - 1)
                for j in range(CH):
                    last = pe.matmul(pd[:, b, j * NB:(j + 1) * NB], olo[:, b, j, :], ohi[:, b, j, :],
                                     start=True, stop=True)
                last.then_inc(tally, 1)

            def equal_digits(c, i, b):
                pe.wait_ge(copied_b, c + 1)
                if old(c, 1):
                    pe.wait_ge(kept, c)
                for j in range(CH):
                    last = pe.matmul(pe_q[:, j, :], otb[:, b, j, :], otb[:, b, j, :], start=True, stop=True)
                last.then_inc(equal, 1)

            def find(c, i, b):
                pe.wait_ge(copied_f, c + 1)
                pe.wait_ge(kept, c + 1)
                pe.wait_ge(seen_ok, c + 2)
                if old(c):
                    pe.wait_ge(picked, c - 1)
                for j in range(CH):
                    pe.matmul(pr[:, b, j * NB:(j + 1) * NB], otf[:, b, j, :], seen[:, b, :, j],
                              start=True, stop=False)
                    last = pe.matmul(pr[:, b, j * NB:(j + 1) * NB], bm[:, b, j, :], ohi[:, b, j, :],
                                     start=False, stop=True)
                last.then_inc(found, 1)

            pipeline(pe, 2 * EI, (turn_and_tally, 1), (find, 0), (equal_digits, 1))

        @block.scalar
        def _(act):
            def chunk(c, i, b, first):
                act.wait_ge(turned, c + 1)
                if not first:
                    act.wait_ge(found, c - 1)
                act.activation(otb[:, b, :, :], pt[:, 0, :, :], ACT.Copy).then_inc(copied_b, 1)
                act.activation(otf[:, b, :, :], pt[:, 0, :, :], ACT.Copy).then_inc(copied_f, 1)

            pairs(act, EI, chunk)

        @block.gpsimd
        def _(pool):
            pool.wait_ge(cleared, 64)
            passed = Passed(pool, waited)

            def chunk(c, i, b, first):
                pool.wait_ge(index_ok, c + 1)
                for j in range(CH):
                    q = j % 4
                    pool.wait_ge(sent[q], (c * 2 + j // 4) * 16)
                    passed()
                    pool.indirect_dma_start(
                        out=slots[q], out_offset=bass.IndirectOffsetOnAxis(ap=idx[:, b, j:j + 1], axis=0),
                        in_=rec[:, b, j, :], in_offset=None).then_inc(sent[q], 16)

            pairs(pool, EI, chunk)
            for q in range(4):
                pool.wait_ge(sent[q], EC // 4 * 16)


def slot_tables(nc, g, k, slots, flags, tag):
    with Space(nc, tag) as s:
        loaded, chain, turned, back, out = s.sem("loaded"), s.sem("chain"), s.sem("turned"), s.sem("back"), s.sem("out")
        copied = s.sem("copied")
        part = [s.sb(f"part{q}", [P, NTP * RW]) for q in range(4)]
        xl = s.sb("xl", [P, TB * P])
        fl = s.sb("fl", [P, TB, P])
        pt = s.ps("pt", [P, 2, 512])
        block = s.block()
        local4 = part[1]
        lastx = part[2][:, :].rearrange("p (t e) -> p t e", e=P)

        @block.sync
        def _(sp):
            for q in range(4):
                sp.dma_start(part[q][:, 0:NT * RW], slots[q].rearrange("(p c) w -> p (c w)", p=P)).then_inc(loaded, 16)
            sp.wait_ge(chain, 9)
            sp.dma_start(flags, fl[:, :, :].rearrange("p t e -> p (t e)")).then_inc(out, 16)
            sp.wait_ge(loaded, 64)
            sp.wait_ge(out, 16)

        @block.vector
        def _(v):
            link = Chain(v, chain)
            v.wait_ge(loaded, 64)
            w = NT * RW
            v.tensor_tensor(part[0][:, 0:w], part[0][:, 0:w], part[1][:, 0:w], ALU.add)
            link(v.tensor_tensor(part[2][:, 0:w], part[2][:, 0:w], part[3][:, 0:w], ALU.add))
            link(v.tensor_tensor(part[0][:, 0:w], part[0][:, 0:w], part[2][:, 0:w], ALU.add))
            r = part[0][:, 0:w].rearrange("p (t w) -> p t w", w=RW)
            v.tensor_copy(g.OTHER[:, k, 0:NT], r[:, :, 0])
            v.memset(g.LOCAL[:, k, NT:NTP], -1.0)
            link(v.tensor_scalar(g.LOCAL[:, k, 0:NT], r[:, :, 1], -1.0, None, ALU.add))
            if k == 1:
                v.scalar_tensor_tensor(out=g.KVROW[:, 0:NT], in0=r[:, :, 0], scalar=float(R), in1=r[:, :, 2],
                                       op0=ALU.mult, op1=ALU.add)
                link(v.tensor_copy(g.WEIGHT[:, 0:NT], r[:, :, 3]))
            else:
                link(v.memset(fl[:, :, 0:1], 0.0))
            link(v.tensor_copy(local4[:, :].rearrange("p (t h) -> p t h", h=H),
                               cols3(g.LOCAL[:, k, :]).to_broadcast([P, NTP, H])))
            v.wait_ge(copied, TB // 4)
            x3 = xl[:, :].rearrange("p (t e) -> p t e", e=P)
            v.tensor_tensor(fl[:, :, 1:P], x3[:, :, 1:P], x3[:, :, 0:P - 1], ALU.not_equal)
            v.memset(lastx[:, :, P - 1:P], 1.0)
            link(v.memset(fl[:, :, 0:1], 1.0))
            link(v.tensor_copy(lastx[:, :, 0:P - 1], fl[:, :, 1:P]))
            link(v.scalar_tensor_tensor(out=part[2][:, :], in0=xl[:, :], scalar=1.0, in1=part[2][:, :],
                                        op0=ALU.add, op1=ALU.mult))
            v.tensor_scalar(part[2][:, :], part[2][:, :], -1.0, None, ALU.add).then_inc(back, 1)
            v.wait_ge(back, 1)
            link(v.tensor_scalar(fl[:, :, :], fl[:, :, :], -BIG, None, ALU.mult))
            assert link.n == 9
            for m in range(TB // 4):
                v.wait_ge(back, 2 + m)
                o = pt[:, m % 2, :].rearrange("p (t h) -> p t h", h=H)
                v.tensor_copy(g.LAST[:, k, m * P:(m + 1) * P], o[:, :, 0]).then_inc(copied, 1)

        @block.scalar
        def _(act):
            for m in range(TB // 4):
                act.wait_ge(turned, m + 1)
                act.activation(xl[:, m * 512:(m + 1) * 512], pt[:, m % 2, :], ACT.Copy).then_inc(copied, 1)

        @block.tensor
        def _(pe):
            pe.wait_ge(chain, 5)
            for m in range(TB // 4):
                if m >= 2:
                    pe.wait_ge(copied, m - 1)
                for q in range(4):
                    last = pe.transpose(pt[:, m % 2, q * P:(q + 1) * P], local4[:, (4 * m + q) * P:(4 * m + q + 1) * P],
                                        g.ident[:, :])
                last.then_inc(turned, 1)
            pe.wait_ge(back, 1)
            for m in range(TB // 4):
                pe.wait_ge(copied, TB // 4 if m < 2 else TB // 4 + m - 1)
                for q in range(4):
                    last = pe.transpose(pt[:, m % 2, q * P:(q + 1) * P], part[2][:, (4 * m + q) * P:(4 * m + q + 1) * P],
                                        g.ident[:, :])
                last.then_inc(back, 1)



def edge_logits(nc, g, k, table, width, rowidx, node, nw, score, voff, stash, tag):
    with Space(nc, tag) as s:
        index_ok, gathered = s.sem("index_ok"), [s.sem(f"gathered{b}") for b in (0, 1)]
        stored = [s.sem(f"stored{b}") for b in (0, 1)]
        staged, hot, turned, copied, spread = (s.sem(x) for x in ("staged", "hot", "turned", "copied", "spread"))
        raw, kinked, logit = s.sem("raw"), s.sem("kinked"), s.sem("logit")
        G = s.sb("G", [P, 2, CH, width])
        idx = s.sb("idx", [P, 2, CH], U32)
        loc = s.sb("loc", [P, 2, CH])
        neg = s.sb("neg", [P, 2, CH])
        O = s.sb("O", [P, 2, CH, P], BF16)
        OT = s.sb("OT", [P, 2, CH, P])
        prod = s.sb("prod", [P, CH, nw])
        red = s.sb("red", [P, 2, CH, H])
        pt = s.ps("pt", [P, 2, CH, P], BF16)
        pe_b = s.ps("pe_x", [P, 2, max(CH * nw, 512)])
        pe_x = pe_b[:, :, 0:CH * nw].rearrange("p b (j w) -> p b j w", w=nw)
        waited = s.sem("waited")
        block = s.block()

        @block.gpsimd
        def _(pool):
            passed = Passed(pool, waited)

            def chunk(c, i, b, first):
                pool.wait_ge(index_ok, c + 1)
                if not first:
                    pool.wait_ge(logit, c - 1)
                    pool.wait_ge(stored[b], i * 16)
                passed()
                for j in range(CH):
                    pool.indirect_dma_start(
                        out=G[:, b, j, :], out_offset=None, in_=table,
                        in_offset=bass.IndirectOffsetOnAxis(ap=idx[:, b, j:j + 1], axis=0)).then_inc(gathered[b], 16)

            pairs(pool, NI, chunk)

        @block.sync
        def _(sp):
            def chunk(c, i, b, first):
                sp.wait_ge(gathered[b], i * (16 * CH) + 16 * CH)
                sp.dma_start(stash[ds(c, 1), :, :].rearrange("o p (j w) -> (o p) j w", j=CH),
                             G[:, b, :, voff:voff + D]).then_inc(stored[b], 16)

            pairs(sp, NI, chunk)
            for b in (0, 1):
                sp.wait_ge(stored[b], NI * 16)

        @block.scalar
        def _(act):
            def index(c, i, b):
                if old(c):
                    act.wait_ge(gathered[b], i * (16 * CH))
                act.activation(idx[:, b, :], rowidx[:, ds(c * CH, CH)], ACT.Copy).then_inc(index_ok, 1)

            def copy(c, i, b):
                act.wait_ge(turned, c + 1)
                if old(c):
                    act.wait_ge(spread, c - 1)
                act.activation(OT[:, b, :, :], pt[:, b, :, :], ACT.Copy).then_inc(copied, 1)

            pipeline(act, 2 * NI, (copy, 0), (index, 2))

        @block.vector
        def _(v):
            def stage(c, i, b):
                move(v, loc[:, b, :], g.LOCAL[:, k, ds(c * CH, CH)]).then_inc(staged, 1)

            def one_hots(c, i, b):
                v.wait_ge(staged, c + 1)
                if old(c):
                    v.wait_ge(turned, c - 1)
                v.tensor_scalar(neg[:, b, :], loc[:, b, :], 0.0, BIG, ALU.min, ALU.mult)
                for j in range(CH):
                    last = v.tensor_scalar(O[:, b, j, :], g.iota_b[:, :], loc[:, b, j:j + 1], None, ALU.is_equal)
                last.then_inc(hot, 1)

            def logits(c, i, b):
                v.wait_ge(spread, c + 1)
                v.wait_ge(gathered[b], i * (16 * CH) + 16 * CH)
                sc = G[:, b, :, score:score + nw]
                if nw == H:
                    v.tensor_tensor(prod[:, :, :], pe_x[:, b, :, :], sc, ALU.add).then_inc(raw, 1)
                    v.wait_ge(raw, c + 1)
                    v.scalar_tensor_tensor(out=red[:, b, :, :], in0=prod[:, :, :], scalar=0.2, in1=prod[:, :, :],
                                           op0=ALU.mult, op1=ALU.max).then_inc(kinked, 1)
                else:
                    v.tensor_tensor(prod[:, :, :], pe_x[:, b, :, :], sc, ALU.mult).then_inc(raw, 1)
                    v.wait_ge(raw, c + 1)
                    v.tensor_reduce(red[:, b, :, :], prod[:, :, :].rearrange("p j (h d) -> p j h d", h=H),
                                    AX.X, ALU.add).then_inc(kinked, 1)
                v.wait_ge(kinked, c + 1)
                v.tensor_tensor(g.LG[:, ds(c * CH, CH), :], red[:, b, :, :],
                                cols3(neg[:, b, :]).to_broadcast([P, CH, H]), ALU.add).then_inc(logit, 1)

            pipeline(v, 2 * NI, (one_hots, 1), (logits, 0), (stage, 2))

        @block.tensor
        def _(pe):
            def turn(c, i, b):
                pe.wait_ge(hot, c + 1)
                if old(c):
                    pe.wait_ge(copied, c - 1)
                for j in range(CH):
                    last = pe.transpose(pt[:, b, j, :], O[:, b, j, :], g.ident_b[:, :])
                last.then_inc(turned, 1)

            def to_edges(c, i, b):
                bins = nc.values_load_multi_w_load_instructions(
                    g.BINI[0:1, k, ds(c * CH, CH)], engines=[pe.engine], min_val=0, max_val=NB - 1,
                    skip_runtime_bounds_check_because="the table is cut at the last bin")[1]
                pe.wait_ge(copied, c + 1)
                if old(c):
                    pe.wait_ge(logit, c - 1)
                for j in range(CH):
                    last = pe.matmul(pe_x[:, b, j, :], OT[:, b, j, :], node[:, ds(bins[j], 1), :], start=True, stop=True)
                last.then_inc(spread, 1)

            pipeline(pe, 2 * NI, (turn, 1), (to_edges, 0))


def segment_max(nc, g, k, flags, tag):
    with Space(nc, tag) as s:
        loaded, turned, copied, scanned, back, taken = (s.sem(x) for x in ("loaded", "turned", "copied", "scanned", "back", "taken"))
        staged, hot, moved, kept, chain, init = (s.sem(x) for x in ("staged", "hot", "moved", "kept", "chain", "init"))
        fl = g.MX[:, :, :].rearrange("p t h -> p (t h)")
        mt = g.ACC[:, :, :].rearrange("p n w -> p (n w)")[:, 0:NT * (H + 1)].rearrange("p (t h) -> p t h", h=H + 1)
        xt = s.sb("xt", [P, TB * P])
        fw = s.sb("fw", [P, NTP, H + 1])
        loc = s.sb("loc", [P, 2, CH])
        OL = s.sb("OL", [P, 2, CH, P])
        fs = s.sb("fs", [P, 2, CH, H + 1])
        pt = s.ps("pt", [P, 2, 512])
        pm = s.ps("pm", [P, 2, 512])
        block = s.block()
        lg = g.LG[:, :, :].rearrange("p t h -> p (t h)")
        M4 = TB // 4

        @block.sync
        def _(sp):
            sp.dma_start(fl, flags).then_inc(loaded, 16)
            sp.wait_ge(loaded, 16)

        @block.scalar
        def _(act):
            for m in range(M4):
                act.wait_ge(turned, m + 1)
                act.activation(xt[:, m * 512:(m + 1) * 512], pt[:, m % 2, :], ACT.Copy).then_inc(copied, 1)
            for m in range(M4):
                act.wait_ge(back, m + 1)
                act.activation(fw[:, m * P:(m + 1) * P, 0:H],
                               pt[:, m % 2, :].rearrange("p (t h) -> p t h", h=H), ACT.Copy).then_inc(taken, 1)

        @block.vector
        def _(v):
            v.memset(fw[:, :, H:H + 1], 1.0).then_inc(init, 1)
            v.wait_ge(loaded, 16)
            v.wait_ge(copied, M4)
            v.tensor_tensor_scan(xt[:, :], fl, xt[:, :], -BIG, ALU.add, ALU.max).then_inc(scanned, 1)
            v.wait_ge(taken, M4)
            v.wait_ge(init, 1)

            def stage(c, i, b):
                move(v, loc[:, b, :], g.LAST[:, k, ds(c * CH, CH)]).then_inc(staged, 1)

            def one_hots(c, i, b):
                v.wait_ge(staged, c + 1)
                if old(c):
                    v.wait_ge(moved, c - 1)
                move(v, fs[:, b, :, :], fw[:, ds(c * CH, CH), :])
                for j in range(CH):
                    last = v.tensor_scalar(OL[:, b, j, :], g.iota[:, :], loc[:, b, j:j + 1], None, ALU.is_equal)
                last.then_inc(hot, 1)

            def keep(c, i, b):
                v.wait_ge(moved, c + 1)
                move(v, mt[:, ds(c * CH, CH), :],
                     pm[:, b, 0:CH * (H + 1)].rearrange("p (j h) -> p j h", j=CH)).then_inc(kept, 1)

            pipeline(v, 2 * NI, (one_hots, 1), (keep, 0), (stage, 2))
            link = Chain(v, chain)
            v.wait_ge(kept, 2 * NI)
            link(v.tensor_scalar(mt[:, :, H], mt[:, :, H], -1.0, BIG, ALU.add, ALU.mult))
            link(v.tensor_tensor(mt[:, :, 0:H], mt[:, :, 0:H],
                                 mt[:, :, H:H + 1].to_broadcast([P, NT, H]), ALU.add))
            for h in range(H):
                v.tensor_tensor_scan(g.MX[:, 0:NT, h], g.TF[:, k, 0, :], mt[:, :, h], -BIG, ALU.add, ALU.max)
            link(v.memset(loc[:, :, :], 0.0))
            for h in range(H):
                last = v.tensor_tensor_scan(mt[:, ::-1, h], g.TF[:, k, 1, ::-1], mt[:, ::-1, h], -BIG, ALU.add, ALU.max)
            link(last)
            link(v.tensor_tensor(g.MX[:, 0:NT, :], g.MX[:, 0:NT, :], mt[:, :, 0:H], ALU.max))

        @block.tensor
        def _(pe):
            for m in range(M4):
                if m >= 2:
                    pe.wait_ge(copied, m - 1)
                for q in range(4):
                    last = pe.transpose(pt[:, m % 2, q * P:(q + 1) * P], lg[:, (4 * m + q) * P:(4 * m + q + 1) * P],
                                        g.ident[:, :])
                last.then_inc(turned, 1)
            pe.wait_ge(scanned, 1)
            for m in range(M4):
                if m >= 2:
                    pe.wait_ge(taken, m - 1)
                for q in range(4):
                    last = pe.transpose(pt[:, m % 2, q * P:(q + 1) * P], xt[:, (4 * m + q) * P:(4 * m + q + 1) * P],
                                        g.ident[:, :])
                last.then_inc(back, 1)

            def chunk(c, i, b, first):
                pe.wait_ge(hot, c + 1)
                if not first:
                    pe.wait_ge(kept, c - 1)
                for j in range(CH):
                    last = pe.matmul(pm[:, b, j * (H + 1):(j + 1) * (H + 1)], OL[:, b, j, :], fs[:, b, j, :],
                                     start=True, stop=True)
                last.then_inc(moved, 1)

            pairs(pe, NI, chunk)


def agg_cell(pa, b, j):
    return pa[:, b, j // 3, (j % 3) * (D + H):(j % 3 + 1) * (D + H)]


def edge_sums(nc, g, k, stash, tag):
    with Space(nc, tag) as s:
        arrived = [s.sem(f"arrived{b}") for b in (0, 1)]
        staged, hot, turned, copied, spread, wide = (s.sem(x) for x in ("staged", "hot", "turned", "copied", "spread", "wide"))
        shifted, powered, weighted, summed, added, init = (s.sem(x) for x in ("shifted", "powered", "weighted", "summed", "added", "init"))
        mx_ok = s.sem("mx_ok")
        V = s.sb("V", [P, 2, CH, D])
        WV = s.sb("WV", [P, 2, CH, D + H])
        loc = s.sb("loc", [P, 2, CH])
        O = s.sb("O", [P, 2, CH, P])
        OB = s.sb("OB", [P, 2, CH, P], BF16)
        OT = s.sb("OT", [P, 2, CH, P])
        sh = s.sb("sh", [P, 2, CH, H])
        mx = s.sb("mx", [P, 2, CH, H])
        pt = s.ps("pt", [P, 1, CH, P], BF16)
        pe_x = s.ps("pe_x", [P, 512])
        pa = s.ps("pa", [P, 2, 3, 512])
        block = s.block()
        NC = 2 * NI

        @block.sync
        def _(sp):
            def load(c, i, b):
                if old(c):
                    sp.wait_ge(weighted, (c - 1) * CH)
                sp.dma_start(V[:, b, :, :].rearrange("p j w -> p (j w)"),
                             stash[ds(c, 1), :, :].rearrange("o p w -> (o p) w")).then_inc(arrived[b], 16)

            pipeline(sp, NC, (load, 0))

        @block.scalar
        def _(act):
            def copies(c, i, b):
                if old(c):
                    act.wait_ge(spread, c - 1)
                act.activation(mx[:, b, :, :], g.MX[:, ds(c * CH, CH), :], ACT.Copy).then_inc(mx_ok, 1)
                act.wait_ge(turned, c + 1)
                act.activation(OT[:, b, :, :], pt[:, 0, :, :], ACT.Copy).then_inc(copied, 1)
                if old(c):
                    act.wait_ge(summed, (c - 1) * CH)
                act.activation(O[:, b, :, :], OB[:, b, :, :], ACT.Copy).then_inc(wide, 1)

            def power(c, i, b):
                act.wait_ge(shifted, c + 1)
                act.activation(WV[:, b, :, D:D + H], sh[:, b, :, :], ACT.Exp).then_inc(powered, 1)

            pipeline(act, NC, (copies, 0), (power, 0))

        @block.vector
        def _(v):
            v.memset(g.ACC[:, :, :], 0.0).then_inc(init, 1)
            v.wait_ge(init, 1)

            def stage(c, i, b):
                move(v, loc[:, b, :], g.LOCAL[:, k, ds(c * CH, CH)]).then_inc(staged, 1)

            def one_hots(c, i, b):
                v.wait_ge(staged, c + 1)
                if old(c):
                    v.wait_ge(turned, c - 1)
                    v.wait_ge(wide, c - 1)
                for j in range(CH):
                    last = v.tensor_scalar(OB[:, b, j, :], g.iota_b[:, :], loc[:, b, j:j + 1], None, ALU.is_equal)
                last.then_inc(hot, 1)

            def shift(c, i, b):
                v.wait_ge(spread, c + 1)
                if old(c):
                    v.wait_ge(powered, c - 1)
                v.tensor_tensor(sh[:, b, :, :], g.LG[:, ds(c * CH, CH), :],
                                pe_x[:, 0:CH * H].rearrange("p (j h) -> p j h", j=CH), ALU.subtract).then_inc(shifted, 1)

            def weigh_and_add(c, i, b, weigh=True):
                if old(c, 1):
                    bins = nc.values_load_multi_w_load_instructions(
                        g.BINI[0:1, k, ds((c - 1) * CH, CH)], engines=[v.engine], min_val=0, max_val=NB - 1,
                        skip_runtime_bounds_check_because="the table is cut at the last bin")[1]
                if weigh:
                    v.wait_ge(arrived[b], i * 16 + 16)
                    v.wait_ge(powered, c + 1)
                    if old(c):
                        v.wait_ge(summed, (c - 1) * CH)
                for j in range(CH):
                    if weigh:
                        v.tensor_tensor(WV[:, b, j, 0:D].rearrange("p (h d) -> p h d", h=H),
                                        V[:, b, j, :].rearrange("p (h d) -> p h d", h=H),
                                        WV[:, b, j, D:D + H].rearrange("p (h o) -> p h o", o=1).to_broadcast([P, H, HD]),
                                        ALU.mult).then_inc(weighted, 1)
                    if old(c, 1):
                        if j % 3 == 0:
                            v.wait_ge(summed, (c - 1) * CH + min(j + 3, CH))
                        if old(c, 2) or j:
                            v.wait_ge(added, (c - 1) * CH + j)
                        a = g.ACC[:, ds(bins[j], 1), :]
                        v.tensor_tensor(a, a, agg_cell(pa, 1 - b, j), ALU.add).then_inc(added, 1)

            pipeline(v, NC, (weigh_and_add, 0), (shift, 1), (one_hots, 2), (stage, 3))
            weigh_and_add(NC, NI, 0, weigh=False)
            v.wait_ge(added, NT)

        @block.tensor
        def _(pe):
            def turn(c, i, b):
                pe.wait_ge(hot, c + 1)
                if old(c, 1):
                    pe.wait_ge(copied, c)
                for j in range(CH):
                    last = pe.transpose(pt[:, 0, j, :], OB[:, b, j, :], g.ident_b[:, :])
                last.then_inc(turned, 1)

            def to_edges(c, i, b):
                pe.wait_ge(copied, c + 1)
                pe.wait_ge(mx_ok, c + 1)
                if old(c, 1):
                    pe.wait_ge(shifted, c)
                for j in range(CH):
                    last = pe.matmul(pe_x[:, j * H:(j + 1) * H], OT[:, b, j, :], mx[:, b, j, :], start=True, stop=True)
                last.then_inc(spread, 1)

            def sums(c, i, b):
                pe.wait_ge(wide, c + 1)
                for j in range(CH):
                    if old(c) and j % 3 == 0:
                        pe.wait_ge(added, (c - 2) * CH + min(j + 3, CH))
                    pe.wait_ge(weighted, c * CH + j + 1)
                    pe.matmul(agg_cell(pa, b, j), O[:, b, j, :], WV[:, b, j, :], start=True, stop=True).then_inc(summed, 1)

            pipeline(pe, NC, (turn, 1), (to_edges, 1), (sums, 0))


def plain_sums(nc, g, table, weight, tag):
    w = D + 2 if weight else D
    with Space(nc, tag) as s:
        index_ok, gathered = s.sem("index_ok"), [s.sem(f"gathered{b}") for b in (0, 1)]
        staged, hot, summed, added, put = (s.sem(x) for x in ("staged", "hot", "summed", "added", "put"))
        G = s.sb("G", [P, 2, CH, D + H])
        idx = s.sb("idx", [P, 2, CH], U32)
        loc = s.sb("loc", [P, 2, CH])
        O = s.sb("O", [P, 2, CH, P])
        pa = s.ps("pa", [P, 2, 3, 512])
        waited = s.sem("waited")
        block = s.block()
        k = 1

        @block.gpsimd
        def _(pool):
            passed = Passed(pool, waited)

            def chunk(c, i, b, first):
                pool.wait_ge(index_ok, c + 1)
                if not first:
                    pool.wait_ge(summed, c - 1)
                passed()
                for j in range(CH):
                    pool.indirect_dma_start(
                        out=G[:, b, j, 0:D], out_offset=None, in_=table,
                        in_offset=bass.IndirectOffsetOnAxis(ap=idx[:, b, j:j + 1], axis=0)).then_inc(gathered[b], 16)

            pairs(pool, NI, chunk)

        @block.scalar
        def _(act):
            def chunk(c, i, b, first):
                if not first:
                    act.wait_ge(gathered[b], i * (16 * CH))
                act.activation(idx[:, b, :], g.OTHER[:, k, ds(c * CH, CH)], ACT.Copy).then_inc(index_ok, 1)
                if weight:
                    if not first:
                        act.wait_ge(summed, c - 1)
                    act.activation(G[:, b, :, D:D + 2], cols3(g.WEIGHT[:, ds(c * CH, CH)]).to_broadcast([P, CH, 2]),
                                   ACT.Copy).then_inc(put, 1)

            pairs(act, NI, chunk)

        @block.vector
        def _(v):
            def one_hots(c, b, first):
                move(v, loc[:, b, :], g.LOCAL[:, k, ds(c * CH, CH)]).then_inc(staged, 1)
                v.wait_ge(staged, c + 1)
                if not first:
                    v.wait_ge(summed, c - 1)
                for j in range(CH):
                    last = v.tensor_scalar(O[:, b, j, :], g.iota[:, :], loc[:, b, j:j + 1], None, ALU.is_equal)
                last.then_inc(hot, 1)

            def add_up(c, b):
                bins = nc.values_load_multi_w_load_instructions(
                    g.BINI[0:1, k, ds(c * CH, CH)], engines=[v.engine], min_val=0, max_val=NB - 1,
                    skip_runtime_bounds_check_because="the table is cut at the last bin")[1]
                v.wait_ge(summed, c + 1)
                for j in range(CH):
                    if not (isinstance(c, int) and c == 0 and j == 0):
                        v.wait_ge(added, c * CH + j)
                    a = g.ACC[:, ds(bins[j], 1), 0:w]
                    v.tensor_tensor(a, a, agg_cell(pa, b, j)[:, 0:w], ALU.add).then_inc(added, 1)

            def chunk(c, i, b, first):
                one_hots(c, b, first)
                if not (first and b == 0):
                    add_up(c - 1, 1 - b)

            pairs(v, NI, chunk)
            add_up(2 * NI - 1, 1)
            v.wait_ge(added, NT)

        @block.tensor
        def _(pe):
            def chunk(c, i, b, first):
                pe.wait_ge(hot, c + 1)
                pe.wait_ge(gathered[b], i * (16 * CH) + 16 * CH)
                if weight:
                    pe.wait_ge(put, c + 1)
                if not first:
                    pe.wait_ge(added, (c - 1) * CH)
                for j in range(CH):
                    last = pe.matmul(agg_cell(pa, b, j)[:, 0:w], O[:, b, j, :], G[:, b, j, 0:w], start=True, stop=True)
                last.then_inc(summed, 1)

            pairs(pe, NI, chunk)



def load_rows(sp, sem, pairs_):
    for dst, src in pairs_:
        sp.dma_start(dst, src).then_inc(sem, 16)
    sp.wait_ge(sem, 16 * len(pairs_))


def attention_tables(nc, g, a, table, tag):
    with Space(nc, tag) as s:
        loaded, cleared = s.sem("loaded"), s.sem("cleared")
        held, turned, copied, made, scored, evac, packed = (s.sem(x) for x in (
            "held", "turned", "copied", "made", "scored", "evac", "packed"))
        W = s.sb("W", [P, 2, D])
        A = s.sb("A", [P, 4 * H])
        xs = s.sb("xs", [P, 2, D])
        xt = s.sb("xt", [P, 2, P])
        ht = s.sb("ht", [P, 2, P])
        row = s.sb("row", [P, 2, W0])
        pt = s.ps("pt", [P, 2, 512])
        pb = s.ps("pb", [P, 2, 512])
        pc = s.ps("pc", [P, 2, 512])
        stored = [s.sem(f"stored{b}") for b in (0, 1)]
        block = s.block()

        @block.sync
        def _(sp):
            sp.wait_ge(cleared, 1)
            with nc.allow_non_contiguous_dma(reason="attention vectors into a block diagonal, once"):
                for v_, vec in enumerate((a.a_in, a.a_out)):
                    for h in range(H):
                        for half in (0, 1):
                            col = (half * 2 + v_) * H + h
                            sp.dma_start(A[h * HD:(h + 1) * HD, col:col + 1],
                                         vec[h:h + 1, half * HD:(half + 1) * HD].rearrange("o d -> d o")).then_inc(loaded, 16)
            sp.dma_start(W[:, 0, :], a.W).then_inc(loaded, 16)
            sp.dma_start(W[:, 1, :], a.W_self).then_inc(loaded, 16)

            def tile(n, i, b, first):
                sp.wait_ge(packed, n + 1)
                sp.dma_start(table[ds(n * P, P), :], row[:, b, :]).then_inc(stored[b], 16)

            tiles(sp, NB, tile)
            sp.wait_ge(stored[0], 16 * (NB - NB // 2))
            sp.wait_ge(stored[1], 16 * (NB // 2))

        @block.vector
        def _(v):
            v.memset(A[:, :], 0.0).then_inc(cleared, 1)

            def tile(n, i, b, first):
                if not first:
                    v.wait_ge(turned, n - 1)
                move(v, xs[:, b, :], g.X[:, ds(n, 1), :]).then_inc(held, 1)
                v.wait_ge(scored, n + 1)
                if not first:
                    v.wait_ge(stored[b], i * 16)
                v.tensor_copy(row[:, b, 0:D], pb[:, b, P:P + D])
                move(v, g.HH[:, ds(n, 1), :], pb[:, b, P + D:P + 2 * D])
                move(v, g.NS[:, ds(n, 1), :], pc[:, b, 2 * H:4 * H])
                v.tensor_copy(row[:, b, D:D + 2 * H], pc[:, b, 0:2 * H]).then_inc(packed, 1)

            tiles(v, NB, tile)

        @block.scalar
        def _(act):
            def tile(n, i, b, first):
                act.wait_ge(turned, n + 1)
                act.activation(xt[:, b, :], pt[:, b, 0:P], ACT.Copy).then_inc(copied, 1)
                act.wait_ge(made, n + 1)
                act.activation(ht[:, b, :], pb[:, b, 0:P], ACT.Copy).then_inc(evac, 1)

            tiles(act, NB, tile)

        @block.tensor
        def _(pe):
            pe.wait_ge(loaded, 16 * 18)

            def tile(n, i, b, first):
                pe.wait_ge(held, n + 1)
                pe.transpose(pt[:, b, 0:P], xs[:, b, :], g.ident[:, :]).then_inc(turned, 1)
                pe.wait_ge(copied, n + 1)
                if not first:
                    pe.wait_ge(packed, n - 1)
                pe.matmul(pb[:, b, 0:P], W[:, 0, :], xt[:, b, :], start=True, stop=True)
                pe.matmul(pb[:, b, P:P + 2 * D], xt[:, b, :], W[:, :, :].rearrange("p a d -> p (a d)"),
                          start=True, stop=True).then_inc(made, 1)
                pe.wait_ge(evac, n + 1)
                pe.matmul(pc[:, b, 0:4 * H], ht[:, b, :], A[:, :], start=True, stop=True).then_inc(scored, 1)

            tiles(pe, NB, tile)


def typed_product(nc, g, W, B, src, dst, tag):
    with Space(nc, tag) as s:
        loaded, masked, turned, copied, made, stored = (s.sem(x) for x in ("loaded", "masked", "turned", "copied", "made", "stored"))
        w = s.sb("w", [P, T, D])
        bias = s.sb("bias", [T, D])
        tm = s.sb("tm", [P, 2, T])
        xm = s.sb("xm", [P, 2, T, D])
        xt = s.sb("xt", [P, 2, T, P])
        mt = s.sb("mt", [T, 2, P])
        tms = s.sem("tms")
        pt = s.ps("pt", [P, 2, 512])
        pb = s.ps("pb", [P, 2, 512])
        block = s.block()

        @block.sync
        def _(sp):
            load_rows(sp, loaded, [(w[:, :, :], W.rearrange("t i o -> i t o")), (bias[:, :], B)])

        @block.vector
        def _(v):
            def tile(n, i, b, first):
                if not first:
                    v.wait_ge(turned, n - 1)
                move(v, tm[:, b, :], g.TM[:, ds(n, 1), :]).then_inc(tms, 1)
                v.wait_ge(tms, n + 1)
                for t in range(T):
                    last = v.tensor_scalar(xm[:, b, t, :], src[:, ds(n, 1), 0:D], tm[:, b, t:t + 1], None, ALU.mult)
                last.then_inc(masked, 1)
                v.wait_ge(made, n + 1)
                move(v, dst[:, ds(n, 1), 0:D], pb[:, b, 0:D]).then_inc(stored, 1)

            tiles(v, NB, tile)

        @block.scalar
        def _(act):
            def tile(n, i, b, first):
                act.wait_ge(turned, n + 1)
                if not first:
                    act.wait_ge(made, n - 1)
                act.activation(xt[:, b, :, :].rearrange("p t n -> p (t n)"), pt[:, b, 0:T * P], ACT.Copy)
                act.activation(mt[:, b, :], pt[0:T, b, T * P:(T + 1) * P], ACT.Copy).then_inc(copied, 1)

            tiles(act, NB, tile)

        @block.tensor
        def _(pe):
            pe.wait_ge(loaded, 32)

            def tile(n, i, b, first):
                pe.wait_ge(masked, n + 1)
                if not first:
                    pe.wait_ge(copied, n - 1)
                for t in range(T):
                    pe.transpose(pt[:, b, t * P:(t + 1) * P], xm[:, b, t, :], g.ident[:, :])
                pe.transpose(pt[0:T, b, T * P:(T + 1) * P], tm[:, b, :], g.ident[:, :]).then_inc(turned, 1)
                pe.wait_ge(copied, n + 1)
                if not first:
                    pe.wait_ge(stored, n - 1)
                for t in range(T):
                    pe.matmul(pb[:, b, 0:D], xt[:, b, t, :], w[:, t, :], start=(t == 0), stop=False)
                pe.matmul(pb[:, b, 0:D], mt[:, b, :], bias[:, :], start=False, stop=True).then_inc(made, 1)

            tiles(pe, NB, tile)


def hgt_tables(nc, g, a, l, table, tag):
    with Space(nc, tag) as s:
        loaded, cleared, scaled = s.sem("loaded"), s.sem("cleared"), s.sem("scaled")
        masked, turned, copied, made, evac, spread, packed, tms, qdone = (s.sem(x) for x in (
            "masked", "turned", "copied", "made", "evac", "spread", "packed", "tms", "qdone"))
        w = s.sb("w", [P, 3, T, D])
        bias = s.sb("bias", [T, 3, D])
        bd = s.sb("bd", [P, 2, R, D])
        mu = s.sb("mu", [P, R * H])
        tm = s.sb("tm", [P, 2, T])
        xm = s.sb("xm", [P, 2, T, D])
        xt = s.sb("xt", [P, 2, T, P])
        mt = s.sb("mt", [T, 2, P])
        kv = s.sb("kv", [P, 2, 2, P])
        row = s.sb("row", [P, 2, R, 2 * D])
        pt = s.ps("pt", [P, 2, 512])
        pb = s.ps("pb", [P, 2, 512])
        pk = s.ps("pk", [P, 4, 512])
        stored = [s.sem(f"stored{b}") for b in (0, 1)]
        block = s.block()

        @block.sync
        def _(sp):
            for m, (Wm, Bm) in enumerate(((a.Wk, a.bk), (a.Wv, a.bv), (a.Wq, a.bq))):
                sp.dma_start(w[:, m, :, :], Wm[l].rearrange("t i o -> i t o")).then_inc(loaded, 16)
                sp.dma_start(bias[:, m, :], Bm[l]).then_inc(loaded, 16)
            sp.dma_start(mu[:, :], a.mu[l].rearrange("(o r) h -> o (r h)", o=1).to_broadcast([P, R * H])).then_inc(loaded, 16)
            sp.wait_ge(cleared, 1)
            for m, rel in enumerate((a.a_rel, a.m_rel)):
                for h in range(H):
                    sp.dma_start(bd[h * HD:(h + 1) * HD, m, :, h * HD:(h + 1) * HD],
                                 rel[l, :, h].rearrange("r d e -> d r e")).then_inc(loaded, 16)

            def tile(n, i, b, first):
                sp.wait_ge(packed, 2 * n + 2)
                sp.dma_start(table[ds(n * P, P), :, :].rearrange("p r w -> p (r w)"),
                             row[:, b, :, :].rearrange("p r w -> p (r w)")).then_inc(stored[b], 16)

            tiles(sp, NB, tile)
            sp.wait_ge(stored[0], 16 * (NB - NB // 2))
            sp.wait_ge(stored[1], 16 * (NB // 2))

        @block.vector
        def _(v):
            v.memset(bd[:, :, :, :], 0.0).then_inc(cleared, 1)
            v.wait_ge(loaded, 16 * 15)
            v.tensor_scalar(mu[:, :], mu[:, :], float(HD) ** -0.5, None, ALU.mult).then_inc(scaled, 1)
            v.wait_ge(scaled, 1)
            flat = bd[:, 0, :, :].rearrange("p r (h e) -> p (r h) e", h=H)
            v.tensor_tensor(flat, flat, cols3(mu[:, :]).to_broadcast([P, R * H, HD]), ALU.mult).then_inc(scaled, 1)

            def tile(n, i, b, first):
                if not first:
                    v.wait_ge(turned, n - 1)
                move(v, tm[:, b, :], g.TM[:, ds(n, 1), :]).then_inc(tms, 1)
                v.wait_ge(tms, n + 1)
                for t in range(T):
                    last = v.tensor_scalar(xm[:, b, t, :], g.HH[:, ds(n, 1), :], tm[:, b, t:t + 1], None, ALU.mult)
                last.then_inc(masked, 1)
                v.wait_ge(spread, n + 1)
                if not first:
                    v.wait_ge(stored[b], i * 16)
                v.tensor_copy(row[:, b, :, 0:D], pk[:, 2 * b, :].rearrange("p (r w) -> p r w", r=R)).then_inc(packed, 1)

            tiles(v, NB, tile)

        @block.scalar
        def _(act):
            def tile(n, i, b, first):
                act.wait_ge(turned, n + 1)
                if not first:
                    act.wait_ge(made, n - 1)
                act.activation(xt[:, b, :, :].rearrange("p t n -> p (t n)"), pt[:, b, 0:T * P], ACT.Copy)
                act.activation(mt[:, b, :], pt[0:T, b, T * P:(T + 1) * P], ACT.Copy).then_inc(copied, 1)
                act.wait_ge(made, n + 1)
                if not first:
                    act.wait_ge(spread, n - 1)
                act.activation(kv[:, b, :, :].rearrange("p m n -> p (m n)"), pb[:, b, 0:2 * P], ACT.Copy).then_inc(evac, 1)
                act.activation(g.QQ[:, ds(n, 1), :], pb[:, b, 2 * P:2 * P + D], ACT.Copy).then_inc(qdone, 1)
                act.wait_ge(spread, n + 1)
                if not first:
                    act.wait_ge(stored[b], i * 16)
                act.activation(row[:, b, :, D:2 * D], pk[:, 2 * b + 1, :].rearrange("p (r w) -> p r w", r=R),
                               ACT.Copy).then_inc(packed, 1)

            tiles(act, NB, tile)

        @block.tensor
        def _(pe):
            pe.wait_ge(loaded, 16 * 15)
            pe.wait_ge(scaled, 2)

            def tile(n, i, b, first):
                pe.wait_ge(masked, n + 1)
                if not first:
                    pe.wait_ge(copied, n - 1)
                for t in range(T):
                    pe.transpose(pt[:, b, t * P:(t + 1) * P], xm[:, b, t, :], g.ident[:, :])
                pe.transpose(pt[0:T, b, T * P:(T + 1) * P], tm[:, b, :], g.ident[:, :]).then_inc(turned, 1)
                pe.wait_ge(copied, n + 1)
                if not first:
                    pe.wait_ge(qdone, n - 1)
                    pe.wait_ge(evac, n - 1)
                for m in (0, 1):
                    o = pb[:, b, m * P:(m + 1) * P]
                    for t in range(T):
                        pe.matmul(o, w[:, m, t, :], xt[:, b, t, :], start=(t == 0), stop=False)
                    pe.matmul(o, bias[:, m, :], mt[:, b, :], start=False, stop=True)
                o = pb[:, b, 2 * P:2 * P + D]
                for t in range(T):
                    pe.matmul(o, xt[:, b, t, :], w[:, 2, t, :], start=(t == 0), stop=False)
                pe.matmul(o, mt[:, b, :], bias[:, 2, :], start=False, stop=True).then_inc(made, 1)
                pe.wait_ge(evac, n + 1)
                if not first:
                    pe.wait_ge(packed, 2 * n - 2)
                for m in (0, 1):
                    last = pe.matmul(pk[:, 2 * b + m, :], kv[:, b, m, :],
                                     bd[:, m, :, :].rearrange("p r d -> p (r d)"), start=True, stop=True)
                last.then_inc(spread, 1)

            tiles(pe, NB, tile)


class Rows:

    def __init__(self, v, act, g, s):
        self.v, self.act, self.g = v, act, g
        self.s = s


def layer_norm(link, v, buf, sq, st, eps_ap, act_ask, wait_act):
    full = [P, NB, D]
    link(v.tensor_reduce(st[:, 0, :], buf, AX.X, ALU.add))
    link(v.tensor_scalar(st[:, 0, :], st[:, 0, :], -1.0 / D, None, ALU.mult))
    link(v.tensor_tensor(buf, buf, cols3(st[:, 0, :]).to_broadcast(full), ALU.add))
    link(v.tensor_tensor(sq, buf, buf, ALU.mult))
    link(v.tensor_reduce(st[:, 1, :], sq, AX.X, ALU.add))
    link(v.tensor_scalar(st[:, 1, :], st[:, 1, :], 1.0 / D, 1e-5, ALU.mult, ALU.add))
    act_ask()
    wait_act()
    link(v.reciprocal(st[:, 2, :], st[:, 2, :]))
    link(v.tensor_tensor(buf, buf, cols3(st[:, 2, :]).to_broadcast(full), ALU.mult))


class Wide:

    def __init__(self, nc, g, s):
        self.nc, self.g, self.s = nc, g, s
        self.chain, self.ask, self.ans = s.sem("chain"), s.sem("ask"), s.sem("ans")
        self.loaded = s.sem("loaded")
        self.jobs = []

    def run(self, loads, body, stores=()):
        s = self.s
        block = s.block()
        stored = s.sem("stored")
        count = {}

        @block.sync
        def _(sp):
            if loads:
                load_rows(sp, self.loaded, loads)

        @block.vector
        def _(v):
            link = Chain(v, self.chain)
            if loads:
                v.wait_ge(self.loaded, 16 * len(loads))

            def fn(job):
                self.jobs.append((link.n, job))
                v.wait_ge(self.ans, len(self.jobs))

            body(v, link, fn)
            count["n"] = link.n

        @block.scalar
        def _(act):
            for n, (after, job) in enumerate(self.jobs):
                act.wait_ge(self.chain, after)
                job(act).then_inc(self.ans, 1)
            if stores:
                act.wait_ge(self.chain, count["n"])
                for dst, src in stores:
                    act.dma_start(dst, src).then_inc(stored, 16)
                act.wait_ge(stored, 16 * len(stores))


def norm_rows(v, link, fn, buf, sq, st):
    full = [P, NB, D]
    link(v.tensor_reduce(st[:, 0, :], buf, AX.X, ALU.add))
    link(v.tensor_scalar(st[:, 0, :], st[:, 0, :], -1.0 / D, None, ALU.mult))
    link(v.tensor_tensor(buf, buf, cols3(st[:, 0, :]).to_broadcast(full), ALU.add))
    link(v.tensor_tensor(sq, buf, buf, ALU.mult))
    link(v.tensor_reduce(st[:, 1, :], sq, AX.X, ALU.add))
    link(v.tensor_scalar(st[:, 1, :], st[:, 1, :], 1.0 / D, 1e-5, ALU.mult, ALU.add))
    fn(lambda act: act.activation(st[:, 2, :], st[:, 1, :], ACT.Sqrt))
    link(v.reciprocal(st[:, 2, :], st[:, 2, :]))
    link(v.tensor_tensor(buf, buf, cols3(st[:, 2, :]).to_broadcast(full), ALU.mult))


def row_of(ap):
    return ap.rearrange("(o d) -> o d", o=1).to_broadcast([P, D])


def by_tile(row):
    return row.rearrange("p (o d) -> p o d", o=1).to_broadcast([P, NB, D])


def attention_mean(v, link, g, eps, rec, dst):
    link(v.tensor_scalar(rec, g.ACC[:, :, D:D + H], eps, None, ALU.add))
    link(v.reciprocal(rec, rec))
    for h in range(H):
        last = v.tensor_tensor(dst[:, :, h * HD:(h + 1) * HD], g.ACC[:, :, h * HD:(h + 1) * HD],
                               rec[:, :, h:h + 1].to_broadcast([P, NB, HD]), ALU.mult)
    link(last)


def add_direction(nc, g, tag):
    with Space(nc, tag) as s:
        rec = s.sb("rec", [P, NB, H])
        sq = s.sb("sq", [P, NB, D])

        def body(v, link, fn):
            attention_mean(v, link, g, 1e-8, rec[:, :, :], sq)
            link(v.tensor_tensor(g.HH[:, :, :], g.HH[:, :, :], sq[:, :, :], ALU.add))

        Wide(nc, g, s).run([], body)


def close_l0(nc, g, a, tag):
    with Space(nc, tag) as s:
        sq = s.sb("sq", [P, NB, D])
        st = s.sb("st", [P, 3, NB])
        par = s.sb("par", [P, 3, D])

        def body(v, link, fn):
            hh = g.HH[:, :, :]
            link(v.tensor_tensor(hh, hh, by_tile(par[:, 0, :]), ALU.add))
            norm_rows(v, link, fn, hh, sq[:, :, :], st)
            link(v.tensor_tensor(hh, hh, by_tile(par[:, 1, :]), ALU.mult))
            link(v.tensor_tensor(hh, hh, by_tile(par[:, 2, :]), ALU.add))
            link(v.tensor_tensor(g.X[:, :, :], g.X[:, :, :], hh, ALU.add))
            norm_rows(v, link, fn, g.X[:, :, :], sq[:, :, :], st)

        Wide(nc, g, s).run([(par[:, 0, :], row_of(a.bias)), (par[:, 1, :], row_of(a.ln_gamma)),
                            (par[:, 2, :], row_of(a.ln_beta))], body)


def gelu_mean(nc, g, tag):
    c = 0.7978845608028654
    with Space(nc, tag) as s:
        rec = s.sb("rec", [P, NB, H])
        sq = s.sb("sq", [P, NB, D])

        def body(v, link, fn):
            x = g.ACC[:, :, 0:D]
            attention_mean(v, link, g, 1e-16, rec[:, :, :], g.ACC)
            link(v.tensor_tensor(sq[:, :, :], x, x, ALU.mult))
            link(v.tensor_scalar(sq[:, :, :], sq[:, :, :], 0.044715, 1.0, ALU.mult, ALU.add))
            link(v.tensor_tensor(sq[:, :, :], sq[:, :, :], x, ALU.mult))
            link(v.tensor_scalar(sq[:, :, :], sq[:, :, :], -2.0 * c, 80.0, ALU.mult, ALU.min))
            fn(lambda act: act.activation(sq[:, :, :], sq[:, :, :], ACT.Exp))
            link(v.tensor_scalar(sq[:, :, :], sq[:, :, :], 1.0, None, ALU.add))
            link(v.reciprocal(sq[:, :, :], sq[:, :, :]))
            link(v.tensor_tensor(x, x, sq[:, :, :], ALU.mult))

        Wide(nc, g, s).run([], body)


def blend_skip(nc, g, a, l, last_layer, tag):
    with Space(nc, tag) as s:
        sk = s.sb("sk", [P, T])
        gate = s.sb("gate", [P, 2, NB])
        sq = s.sb("sq", [P, NB, D])
        st = s.sb("st", [P, 3, NB])

        def body(v, link, fn):
            link(v.tensor_scalar(sk[:, :], sk[:, :], -1.0, None, ALU.mult))
            fn(lambda act: act.activation(sk[:, :], sk[:, :], ACT.Exp))
            link(v.tensor_scalar(sk[:, :], sk[:, :], 1.0, None, ALU.add))
            link(v.reciprocal(sk[:, :], sk[:, :]))
            link(v.tensor_scalar(gate[:, 0, :], g.TM[:, :, 0], sk[:, 0:1], None, ALU.mult))
            for t in range(1, T):
                link(v.scalar_tensor_tensor(out=gate[:, 0, :], in0=g.TM[:, :, t], scalar=sk[:, t:t + 1],
                                            in1=gate[:, 0, :], op0=ALU.mult, op1=ALU.add))
            link(v.tensor_scalar(gate[:, 1, :], gate[:, 0, :], -1.0, 1.0, ALU.mult, ALU.add))
            link(v.tensor_tensor(sq[:, :, :], g.ACC[:, :, 0:D], cols3(gate[:, 0, :]).to_broadcast([P, NB, D]), ALU.mult))
            link(v.tensor_tensor(g.HH[:, :, :], g.HH[:, :, :], cols3(gate[:, 1, :]).to_broadcast([P, NB, D]), ALU.mult))
            link(v.tensor_tensor(g.HH[:, :, :], g.HH[:, :, :], sq[:, :, :], ALU.add))
            if last_layer:
                link(v.tensor_tensor(g.X[:, :, :], g.X[:, :, :], g.HH[:, :, :], ALU.add))
                norm_rows(v, link, fn, g.X[:, :, :], sq[:, :, :], st)

        Wide(nc, g, s).run([(sk[:, :], a.skip[l].rearrange("(o t) -> o t", o=1).to_broadcast([P, T]))], body)


def gcn_table(nc, g, a, table, tag):
    with Space(nc, tag) as s:
        loaded, root, chain, held, turned, copied, made, packed, staged = (s.sem(x) for x in (
            "loaded", "root", "chain", "held", "turned", "copied", "made", "packed", "staged"))
        W = s.sb("W", [P, D])
        xs = s.sb("xs", [P, 2, D])
        xt = s.sb("xt", [P, 2, P])
        row = s.sb("row", [P, 2, D])
        dv = s.sb("dv", [P, 2, 1])
        pt = s.ps("pt", [P, 2, 512])
        pb = s.ps("pb", [P, 2, 512])
        stored = [s.sem(f"stored{b}") for b in (0, 1)]
        block = s.block()

        @block.sync
        def _(sp):
            sp.dma_start(W[:, :], a.W2).then_inc(loaded, 16)

            def tile(n, i, b, first):
                sp.wait_ge(packed, n + 1)
                sp.dma_start(table[ds(n * P, P), :], row[:, b, :]).then_inc(stored[b], 16)

            tiles(sp, NB, tile)
            sp.wait_ge(stored[0], 16 * (NB - NB // 2))
            sp.wait_ge(stored[1], 16 * (NB // 2))

        @block.vector
        def _(v):
            link = Chain(v, chain)
            link(v.tensor_scalar(g.DINV[:, :], g.CNT[:, 1, :], 1.0, None, ALU.add))
            v.wait_ge(root, 1)
            link(v.reciprocal(g.DINV[:, :], g.DINV[:, :]))

            def tile(n, i, b, first):
                if not first:
                    v.wait_ge(turned, n - 1)
                move(v, xs[:, b, :], g.X[:, ds(n, 1), :]).then_inc(held, 1)
                move(v, dv[:, b, :], g.DINV[:, ds(n, 1)]).then_inc(staged, 1)
                v.wait_ge(staged, n + 1)
                v.wait_ge(made, n + 1)
                if not first:
                    v.wait_ge(stored[b], i * 16)
                v.tensor_scalar(g.ACC[:, ds(n, 1), 0:D], pb[:, b, 0:D], dv[:, b, :], None, ALU.mult)
                v.tensor_scalar(row[:, b, :], pb[:, b, 0:D], dv[:, b, :], None, ALU.mult).then_inc(packed, 1)

            tiles(v, NB, tile)

        @block.scalar
        def _(act):
            act.wait_ge(chain, 1)
            act.activation(g.DINV[:, :], g.DINV[:, :], ACT.Sqrt).then_inc(root, 1)

            def tile(n, i, b, first):
                act.wait_ge(turned, n + 1)
                if not first:
                    act.wait_ge(made, n - 1)
                act.activation(xt[:, b, :], pt[:, b, 0:P], ACT.Copy).then_inc(copied, 1)

            tiles(act, NB, tile)

        @block.tensor
        def _(pe):
            pe.wait_ge(loaded, 16)

            def tile(n, i, b, first):
                pe.wait_ge(held, n + 1)
                pe.transpose(pt[:, b, 0:P], xs[:, b, :], g.ident[:, :]).then_inc(turned, 1)
                pe.wait_ge(copied, n + 1)
                if not first:
                    pe.wait_ge(packed, n - 1)
                pe.matmul(pb[:, b, 0:D], xt[:, b, :], W[:, :], start=True, stop=True).then_inc(made, 1)

            tiles(pe, NB, tile)


def close_l2(nc, g, a, table, tag):
    with Space(nc, tag) as s:
        sq = s.sb("sq", [P, NB, D])
        st = s.sb("st", [P, 3, NB])
        par = s.sb("par", [P, D])

        def body(v, link, fn):
            x, y = g.X[:, :, :], sq[:, :, :]
            link(v.tensor_tensor(y, g.ACC[:, :, 0:D], cols3(g.DINV[:, :]).to_broadcast([P, NB, D]), ALU.mult))
            link(v.tensor_tensor(y, y, by_tile(par[:, :]), ALU.add))
            link(v.scalar_tensor_tensor(out=y, in0=y, scalar=0.1, in1=y, op0=ALU.mult, op1=ALU.max))
            link(v.tensor_tensor(y, y, x, ALU.add))
            link(v.tensor_tensor(x, x, y, ALU.add))
            norm_rows(v, link, fn, x, y, st)
            link(v.memset(g.ACC[:, :, :], 0.0))

        Wide(nc, g, s).run([(par[:, :], row_of(a.b2g))], body, [(rows(table), g.X[:, :, :])])


def gine_input(nc, g, a, tag):
    with Space(nc, tag) as s:
        sq = s.sb("sq", [P, NB, D])
        cn = s.sb("cn", [P, NB])
        ew = s.sb("ew", [P, D])
        eb = s.sb("eb", [P, D])
        ep = s.sb("ep", [P, 1])

        def body(v, link, fn):
            full = [P, NB, D]
            y, hh = sq[:, :, :], g.HH[:, :, :]
            cnt = g.CNT[:, 1, :]
            link(v.tensor_tensor(y, g.ACC[:, :, D:D + 1].to_broadcast(full), by_tile(ew[:, :]), ALU.mult))
            link(v.tensor_tensor(hh, g.ACC[:, :, 0:D], y, ALU.add))
            link(v.tensor_tensor(y, cols3(cnt).to_broadcast(full), by_tile(eb[:, :]), ALU.mult))
            link(v.tensor_tensor(hh, hh, y, ALU.add))
            link(v.tensor_scalar(cn[:, :], cnt, 1.0, None, ALU.max))
            link(v.reciprocal(cn[:, :], cn[:, :]))
            link(v.tensor_tensor(hh, hh, cols3(cn[:, :]).to_broadcast(full), ALU.mult))
            link(v.tensor_scalar(ep[:, :], ep[:, :], 1.0, None, ALU.add))
            link(v.tensor_scalar(y, g.X[:, :, :], ep[:, 0:1], None, ALU.mult))
            link(v.tensor_tensor(hh, hh, y, ALU.add))

        Wide(nc, g, s).run([(ew[:, :], a.edge_w.to_broadcast([P, D])), (eb[:, :], row_of(a.edge_b)),
                            (ep[:, :], a.eps.rearrange("(o d) -> o d", o=1).to_broadcast([P, 1]))], body)


def gine_mlp(nc, g, a, tag):
    with Space(nc, tag) as s:
        loaded, held, turned, copied, made, relu, out, stored, b12 = (s.sem(x) for x in (
            "loaded", "held", "turned", "copied", "made", "relu", "out", "stored", "b12"))
        w = s.sb("w", [P, 3, D])
        b1 = s.sb("b1", [P, 1])
        b2 = s.sb("b2", [1, 2, D])
        xs = s.sb("xs", [P, 2, 2, D])
        xt = s.sb("xt", [P, 2, 2, P])
        zt = s.sb("zt", [P, 2, P])
        pt = s.ps("pt", [P, 2, 512])
        pz = s.ps("pz", [P, 2, 512])
        po = s.ps("po", [P, 2, 512])
        block = s.block()

        @block.sync
        def _(sp):
            with nc.allow_non_contiguous_dma(reason="one bias word a partition, once"):
                load_rows(sp, loaded, [(w[:, 0, :], a.w1), (w[:, 1, :], a.w2), (w[:, 2, :], a.res_w),
                                       (b1[:, :], a.b1.rearrange("(d o) -> d o", o=1)),
                                       (b2[:, 0, :], a.b2.rearrange("(o d) -> o d", o=1)),
                                       (b2[:, 1, :], a.res_b.rearrange("(o d) -> o d", o=1))])

        @block.vector
        def _(v):
            v.wait_ge(loaded, 96)

            def tile(n, i, b, first):
                if not first:
                    v.wait_ge(turned, n - 1)
                move(v, xs[:, b, 0, :], g.HH[:, ds(n, 1), :])
                move(v, xs[:, b, 1, :], g.X[:, ds(n, 1), :]).then_inc(held, 1)
                v.wait_ge(out, n + 1)
                move(v, g.HH[:, ds(n, 1), :], po[:, b, 0:D]).then_inc(stored, 1)

            tiles(v, NB, tile)

        @block.scalar
        def _(act):
            act.wait_ge(loaded, 96)

            def tile(n, i, b, first):
                act.wait_ge(turned, n + 1)
                if not first:
                    act.wait_ge(out, n - 1)
                act.activation(xt[:, b, :, :].rearrange("p t n -> p (t n)"), pt[:, b, 0:2 * P], ACT.Copy).then_inc(copied, 1)
                act.wait_ge(made, n + 1)
                act.activation(zt[:, b, :], pz[:, b, 0:P], ACT.Relu, bias=b1[:, 0:1]).then_inc(relu, 1)

            tiles(act, NB, tile)

        @block.tensor
        def _(pe):
            pe.wait_ge(loaded, 96)

            def tile(n, i, b, first):
                pe.wait_ge(held, n + 1)
                if not first:
                    pe.wait_ge(copied, n - 1)
                pe.transpose(pt[:, b, 0:P], xs[:, b, 0, :], g.ident[:, :])
                pe.transpose(pt[:, b, P:2 * P], xs[:, b, 1, :], g.ident[:, :]).then_inc(turned, 1)
                pe.wait_ge(copied, n + 1)
                if not first:
                    pe.wait_ge(relu, n - 1)
                pe.matmul(pz[:, b, 0:P], w[:, 0, :], xt[:, b, 0, :], start=True, stop=True).then_inc(made, 1)
                pe.wait_ge(relu, n + 1)
                if not first:
                    pe.wait_ge(stored, n - 1)
                o = po[:, b, 0:D]
                pe.matmul(o, zt[:, b, :], w[:, 1, :], start=True, stop=False)
                pe.matmul(o, xt[:, b, 1, :], w[:, 2, :], start=False, stop=False)
                pe.matmul(o, g.ones[0:1, :], b2[:, 0, :], start=False, stop=False)
                pe.matmul(o, g.ones[0:1, :], b2[:, 1, :], start=False, stop=True).then_inc(out, 1)

            tiles(pe, NB, tile)


def close_l3(nc, g, a, out, tag):
    with Space(nc, tag) as s:
        chain, ask, ans, loaded, stored, made = (s.sem(x) for x in ("chain", "ask", "ans", "loaded", "stored", "made"))
        sq = s.sb("sq", [P, NB, D])
        st = s.sb("st", [P, 3, NB])
        valid = s.sb("valid", [P, NB])
        part = s.sb("part", [P, D])
        stat = s.sb("stat", [P, 2, D])
        par = s.sb("par", [P, 2, D])
        ps = s.ps("ps", [P, 512])
        block = s.block()
        jobs, sums, ends = [], [], []

        @block.gpsimd
        def _(pool):
            pool.iota(valid[:, :], pattern=[[P, NB]], base=0, channel_multiplier=1,
                      allow_small_or_imprecise_dtypes=True).then_inc(made, 1)

        @block.vector
        def _(v):
            link = Chain(v, chain)
            hh, y = g.HH[:, :, :], sq[:, :, :]
            v.wait_ge(made, 1)
            v.wait_ge(loaded, 32)
            link(v.tensor_scalar(valid[:, :], valid[:, :], float(N), None, ALU.is_lt))

            def mean_of(src, dst):
                link(v.tensor_reduce(part[:, :], src.rearrange("p n d -> p d n"), AX.X, ALU.add))
                sums.append(link.n)
                v.wait_ge(ask, len(sums))
                link(v.tensor_scalar(dst, ps[:, 0:D], 1.0 / N, None, ALU.mult))

            def fn(job):
                jobs.append((link.n, job))
                v.wait_ge(ans, len(jobs))

            mask = cols3(valid[:, :]).to_broadcast([P, NB, D])
            link(v.tensor_tensor(hh, hh, mask, ALU.mult))
            mean_of(hh, stat[:, 0, :])
            link(v.tensor_tensor(hh, hh, by_tile(stat[:, 0, :]), ALU.subtract))
            link(v.tensor_tensor(y, hh, hh, ALU.mult))
            link(v.tensor_tensor(y, y, mask, ALU.mult))
            mean_of(y, stat[:, 1, :])
            link(v.tensor_scalar(stat[:, 1, :], stat[:, 1, :], 1e-5, None, ALU.add))
            fn(lambda act: act.activation(stat[:, 1, :], stat[:, 1, :], ACT.Sqrt))
            link(v.reciprocal(stat[:, 1, :], stat[:, 1, :]))
            link(v.tensor_tensor(stat[:, 1, :], stat[:, 1, :], par[:, 0, :], ALU.mult))
            link(v.tensor_tensor(hh, hh, by_tile(stat[:, 1, :]), ALU.mult))
            link(v.tensor_tensor(hh, hh, by_tile(par[:, 1, :]), ALU.add))
            link(v.scalar_tensor_tensor(out=g.X[:, :, :], in0=hh, scalar=0.0, in1=g.X[:, :, :], op0=ALU.max, op1=ALU.add))
            norm_rows(v, link, fn, g.X[:, :, :], y, st)
            ends.append(link.n)

        @block.scalar
        def _(act):
            for after, job in jobs:
                act.wait_ge(chain, after)
                job(act).then_inc(ans, 1)

        @block.tensor
        def _(pe):
            for after in sums:
                pe.wait_ge(chain, after)
                pe.matmul(ps[:, 0:D], g.ones[:, :], part[:, :], start=True, stop=True).then_inc(ask, 1)

        @block.sync
        def _(sp):
            sp.dma_start(par[:, 0, :], row_of(a.gamma)).then_inc(loaded, 16)
            sp.dma_start(par[:, 1, :], row_of(a.beta)).then_inc(loaded, 16)
            sp.wait_ge(chain, ends[0])
            sp.dma_start(out[0:(NB - 1) * P, :].rearrange("(n p) w -> p n w", p=P), g.X[:, 0:NB - 1, :]).then_inc(stored, 16)
            sp.dma_start(out[(NB - 1) * P:N, :], g.X[0:N - (NB - 1) * P, NB - 1, :]).then_inc(stored, 16)
            sp.wait_ge(stored, 32)
            sp.wait_ge(loaded, 32)


class Args:
    pass


def gnn_kernel(nc, a, out):
    g = Args()
    with ExitStack() as ctx:
        def sb(name, shape, dt=F32):
            return ctx.enter_context(nc.sbuf_tensor(name, shape, dt))

        def dram(name, shape, dt=F32):
            return nc.dram_tensor(name, shape, dt, kind="Internal").ap()

        g.X = sb("X", [P, NB, D])
        g.ident = sb("ident", [P, P])
        g.ident_b = sb("ident_b", [P, P], BF16)
        g.iota = sb("iota", [P, P])
        g.iota_b = sb("iota_b", [P, P], BF16)
        g.before = sb("before", [P, P])
        g.ones = sb("ones", [P, P])
        g.zeros = sb("zeros", [P, P])
        g.TM = sb("TM", [P, NB, T])
        g.CNT = sb("CNT", [P, 2, NB])
        g.START = sb("START", [P, 2, NB])
        g.DINV = sb("DINV", [P, NB])
        g.BINI = sb("BINI", [1, 2, NT], I32)
        g.TF = sb("TF", [P, 2, 2, NT])
        g.LOCAL = sb("LOCAL", [P, 2, NTP])
        g.LAST = sb("LAST", [P, 2, NTP])
        g.OTHER = sb("OTHER", [P, 2, NTP])
        g.KVROW = sb("KVROW", [P, NTP])
        g.WEIGHT = sb("WEIGHT", [P, NTP])

        slots = [[dram(f"slots{k}{q}", (P * NT, RW)) for q in range(4)] for k in (0, 1)]
        flags = [dram(f"flags{k}", (P, TB * P)) for k in (0, 1)]
        stash = [dram(f"stash{k}", (NT // CH, P, CH * D)) for k in (0, 1)]
        table0 = dram("table0", (NP, W0))
        table1 = dram("table1", (NP, R, 2 * D))
        table2 = dram("table2", (NP, D))
        table3 = dram("table3", (NP, D))

        with ExitStack() as sort:
            def sbs(name, shape, dt=F32):
                return sort.enter_context(nc.sbuf_tensor(name, shape, dt))

            g.NODE = sbs("NODE", [P, 2, EC])
            g.DIG = sbs("DIG", [P, 2, EC, 2])
            g.ET = sbs("ET", [P, EC])
            g.EW = sbs("EW", [P, EC])
            g.BIN = sbs("BIN", [P, 2, NT])
            load_inputs(nc, g, a)
            for k in (0, 1):
                count_keys(nc, g, k, f"cnt{k}")
                place_edges(nc, g, k, slots[k], f"plc{k}")
        for k in (0, 1):
            slot_tables(nc, g, k, slots[k], flags[k], f"tab{k}")

        g.HH = sb("HH", [P, NB, D])
        g.NS = sb("NS", [P, NB, 2 * H])

        def attention(k, tag, *gather):
            with nc.sbuf_tensor(f"{tag}_LG", [P, NTP, H], F32) as lg, nc.sbuf_tensor(f"{tag}_MX", [P, NTP, H], F32) as mx:
                g.LG, g.MX = lg, mx
                clear_tail(nc, g, f"{tag}_clr")
                if gather[0] is table0:
                    edge_logits(nc, g, k, *gather, stash[k], f"{tag}_log")
                else:
                    g.QQ = g.ACC[:, :, 0:D]
                    hgt_tables(nc, g, a, gather[1], table1, f"{tag}_kv")
                    edge_logits(nc, g, k, table1.rearrange("n r w -> (n r) w"), 2 * D, g.KVROW, g.QQ, D, 0, D,
                                stash[k], f"{tag}_log")
                segment_max(nc, g, k, flags[k], f"{tag}_max")
                edge_sums(nc, g, k, stash[k], f"{tag}_sum")

        attention_tables(nc, g, a, table0, "l0t")
        with nc.sbuf_tensor("ACC0", [P, NB, D + H], F32) as acc:
            g.ACC = acc
            attention(1, "l0i", table0, W0, g.OTHER[:, 1, :], g.NS[:, :, 0:H], H, D, 0)
            add_direction(nc, g, "l0ia")
            attention(0, "l0o", table0, W0, g.OTHER[:, 0, :], g.NS[:, :, H:2 * H], H, D + H, 0)
            add_direction(nc, g, "l0oa")
        close_l0(nc, g, a, "l0c")

        typed_product(nc, g, a.W_in, a.b_in, g.X, g.HH, "l1i")
        for l in (0, 1):
            with nc.sbuf_tensor(f"ACC1{l}", [P, NB, D + H], F32) as acc:
                g.ACC = acc
                attention(1, f"l1{l}", table1, l)
                gelu_mean(nc, g, f"l1{l}g")
                typed_product(nc, g, a.Wa[l], a.ba[l], acc, acc, f"l1{l}a")
                blend_skip(nc, g, a, l, l == 1, f"l1{l}b")

        with nc.sbuf_tensor("ACC2", [P, NB, D + H], F32) as acc:
            g.ACC = acc
            gcn_table(nc, g, a, table2, "l2t")
            plain_sums(nc, g, table2, False, "l2s")
            close_l2(nc, g, a, table3, "l2c")
            plain_sums(nc, g, table3, True, "l3s")
            gine_input(nc, g, a, "l3i")
            gine_mlp(nc, g, a, "l3m")
            close_l3(nc, g, a, out, "l3c")


def clear_tail(nc, g, tag):
    with Space(nc, tag) as s:
        done = s.sem("done")
        block = s.block()

        @block.vector
        def _(v):
            v.memset(g.LG[:, NT:NTP, :], -BIG).then_inc(done, 1)
            v.wait_ge(done, 1)


_NAMES = {
    "x": "x", "src": "src", "dst": "dst", "edge_type_4": "edge_type", "edge_weight1": "edge_weight",
    "node_type_3": "node_type",
    "L0_gnn_W": "W", "L0_gnn_W_self": "W_self", "L0_gnn_a_in": "a_in", "L0_gnn_a_out": "a_out",
    "L0_gnn_bias": "bias", "L0_gnn_ln_gamma": "ln_gamma", "L0_gnn_ln_beta": "ln_beta",
    "L1_gnn_W_in": "W_in", "L1_gnn_b_in": "b_in", "L1_gnn_Wk": "Wk", "L1_gnn_bk": "bk", "L1_gnn_Wq": "Wq",
    "L1_gnn_bq": "bq", "L1_gnn_Wv": "Wv", "L1_gnn_bv": "bv", "L1_gnn_Wa": "Wa", "L1_gnn_ba": "ba",
    "L1_gnn_a_rel": "a_rel", "L1_gnn_m_rel": "m_rel", "L1_gnn_mu": "mu", "L1_gnn_skip": "skip",
    "L2_gnn_W": "W2", "L2_gnn_b": "b2g",
    "L3_gnn_edge_w": "edge_w", "L3_gnn_edge_b": "edge_b", "L3_gnn_w1": "w1", "L3_gnn_b1": "b1", "L3_gnn_w2": "w2",
    "L3_gnn_b2": "b2", "L3_gnn_res_w": "res_w", "L3_gnn_res_b": "res_b", "L3_gnn_eps": "eps",
    "L3_gnn_gamma": "gamma", "L3_gnn_beta": "beta",
}


def kernel(**inputs):
    import numpy as _np
    import concourse.bacc as _bacc
    from concourse import mybir as _mybir
    from concourse.bass_utils import run_bass_kernel_spmd as _run

    nc = _bacc.Bacc("TRN2", target_bir_lowering=False, num_devices=1)
    arrays, a = {}, Args()
    for name, short in _NAMES.items():
        v = _np.ascontiguousarray(inputs[name])
        arrays[f"in_{name}"] = v
        a.__dict__[short] = nc.dram_tensor(f"in_{name}", v.shape, _mybir.dt.from_np(v.dtype), kind="ExternalInput").ap()
    out = nc.dram_tensor("out_dram", (N, D), F32, kind="ExternalOutput").ap()
    gnn_kernel(nc, a, out)
    r = _run(nc, [arrays], core_ids=[0])
    return r.results[0]["out_dram"]
```

```python
from contextlib import ExitStack

import concourse.bass as bass
from concourse import mybir

P = 128
N = 6250
E = 106250
D = 128
H = 4
HD = D // H
R = 4
T = 3
NB = -(-N // P)
NP = NB * P
EC = -(-E // (P * 16)) * 16
NT = 880
assert (P * EC + NB * (P - 1)) // P <= NT and P * EC >= E
NTP = 896
TB = NTP // 32
CH = 8
NI = NT // CH // 2
EI = EC // CH // 2
BIG = 1.0e30
RW = 4
W0 = D + 2 * H

ALU = mybir.AluOpType
ACT = mybir.ActivationFunctionType
AX = mybir.AxisListType
F32 = mybir.dt.float32
BF16 = mybir.dt.bfloat16
I32 = mybir.dt.int32
U32 = mybir.dt.uint32
ds = bass.ds


class Space:

    def __init__(self, nc, tag):
        self.nc, self.tag, self.ctx, self.sems = nc, tag, ExitStack(), []

    def __enter__(self):
        self.ctx.__enter__()
        return self

    def __exit__(self, *a):
        self.ctx.__exit__(*a)
        if a[0] is None:
            self.nc.clear_and_free_semaphores(self.sems)
            self.nc.all_engine_barrier()

    def sb(self, name, shape, dt=F32):
        return self.ctx.enter_context(self.nc.sbuf_tensor(f"{self.tag}_{name}", shape, dt))

    def ps(self, name, shape, dt=F32):
        return self.ctx.enter_context(self.nc.psum_tensor(f"{self.tag}_{name}", shape, dt))

    def sem(self, name):
        self.sems.append(self.nc.alloc_semaphore(f"{self.tag}_{name}"))
        return self.sems[-1]

    def block(self):
        return self.ctx.enter_context(self.nc.Block())


class Passed:

    def __init__(self, pool, sem):
        self.pool, self.sem = pool, sem

    def __call__(self):
        self.pool.sem_inc(self.sem, 1)


class Chain:

    def __init__(self, eng, sem):
        self.eng, self.sem, self.n = eng, sem, 0

    def __call__(self, ins):
        self.n += 1
        ins.then_inc(self.sem, 1)
        self.eng.wait_ge(self.sem, self.n)


def pairs(eng, count, chunk):
    for b in (0, 1):
        chunk(b, 0, b, True)
    with eng.Fori(1, count) as i:
        for b in (0, 1):
            chunk(i * 2 + b, i, b, False)


def old(c, by=2):
    return not isinstance(c, int) or c >= by


def pipeline(eng, n, *stages):
    leads = [lead for _, lead in stages]
    first, last = -max(leads), n - min(leads)
    begin = (2 - min(leads) + 1) // 2
    end = max((n - max(leads)) // 2, begin)

    def step(s, i, b):
        for stage, lead in stages:
            if not isinstance(s, int) or 0 <= s + lead < n:
                stage(s + lead, i + (b + lead) // 2, (b + lead) % 2)

    for t in range(first, 2 * begin):
        step(t, t // 2, t % 2)
    if end > begin:
        with eng.Fori(begin, end) as i:
            for b in (0, 1):
                step(i * 2 + b, i, b)
    for t in range(2 * end, last):
        step(t, t // 2, t % 2)


def rows(dram):
    return dram.rearrange("(n p) w -> p n w", p=P)


def move(v, out, in_):
    return v.tensor_scalar(out, in_, 1.0, None, ALU.mult)


def split_exactly(link, v, parts, rest):
    for q in range(3):
        link(v.tensor_copy(parts[q], rest))
        if q < 2:
            link(v.tensor_tensor(rest, rest, parts[q], ALU.subtract))


def compare(v, out, iota, number):
    full = [P, out.shape[1], out.shape[2]]
    return v.tensor_tensor(out, iota.rearrange("p (o w) -> p o w", o=1).to_broadcast(full),
                           number.to_broadcast(full), ALU.is_equal)


def cols3(ap):
    return ap.rearrange("p (a b) -> p a b", b=1)



def load_inputs(nc, g, a):
    with Space(nc, "ld") as s:
        loaded, made, chain, cast = s.sem("loaded"), s.sem("made"), s.sem("chain"), s.sem("cast")
        keys = s.sb("keys", [P, 3, EC], I32)
        types = s.sb("types", [P, NB], I32)
        lo = s.sb("lo", [P, EC], I32)
        hi = s.sb("hi", [P, EC], I32)
        full = E // EC
        block = s.block()

        @block.sync
        def _(sp):
            sp.wait_ge(chain, 3)
            sp.dma_start(g.X[:, 0:NB - 1, :], a.x[0:(NB - 1) * P, :].rearrange("(n p) w -> p n w", p=P)).then_inc(loaded, 16)
            sp.dma_start(g.X[0:N - (NB - 1) * P, NB - 1, :], a.x[(NB - 1) * P:N, :]).then_inc(loaded, 16)
            for k, src in enumerate((a.src, a.dst, a.edge_type)):
                sp.dma_start(keys[0:full, k, :], src[0:full * EC].rearrange("(p c) -> p c", c=EC)).then_inc(loaded, 16)
                sp.dma_start(keys[full:full + 1, k, 0:E - full * EC],
                             src[full * EC:E].rearrange("(p c) -> p c", p=1)).then_inc(loaded, 16)
            w = a.edge_weight.rearrange("e o -> (e o)")
            sp.dma_start(g.EW[0:full, :], w[0:full * EC].rearrange("(p c) -> p c", c=EC)).then_inc(loaded, 16)
            sp.dma_start(g.EW[full:full + 1, 0:E - full * EC],
                         w[full * EC:E].rearrange("(p c) -> p c", p=1)).then_inc(loaded, 16)
            with nc.allow_non_contiguous_dma(reason="one word a node, once"):
                sp.dma_start(types[:, 0:NB - 1], a.node_type[0:(NB - 1) * P].rearrange("(n p) -> p n", p=P)).then_inc(loaded, 16)
                sp.dma_start(types[0:N - (NB - 1) * P, NB - 1:NB],
                             a.node_type[(NB - 1) * P:N].rearrange("(p o) -> p o", o=1)).then_inc(loaded, 16)
            sp.wait_ge(loaded, 12 * 16)

        @block.gpsimd
        def _(pool):
            pool.memset(g.ident[:, :], 0.0).then_inc(made, 1)
            pool.iota(g.iota[:, :], pattern=[[1, P]], base=0, channel_multiplier=0,
                      allow_small_or_imprecise_dtypes=True).then_inc(made, 1)
            pool.memset(g.before[:, :], 1.0).then_inc(made, 1)
            pool.wait_ge(made, 3)
            pool.affine_select(out=g.ident[:, :], in_=g.ident[:, :], compare_op=ALU.not_equal, fill=1.0,
                               base=0, pattern=[[-1, P]], channel_multiplier=1).then_inc(made, 1)
            pool.affine_select(out=g.before[:, :], in_=g.before[:, :], compare_op=ALU.is_gt, fill=0.0,
                               base=0, pattern=[[1, P]], channel_multiplier=-1).then_inc(made, 1)

        @block.vector
        def _(v):
            link = Chain(v, chain)
            link(v.memset(keys[:, :, :], 0))
            link(v.memset(types[:, :], 0))
            v.memset(g.EW[:, :], 0.0)
            v.memset(g.X[:, :, :], 0.0)
            v.memset(g.ones[:, :], 1.0)
            v.memset(g.zeros[:, :], 0.0)
            link(v.memset(keys[:, 0:2, :], NP - 1))
            v.wait_ge(made, 5)
            v.tensor_copy(g.iota_b[:, :], g.iota[:, :])
            v.tensor_copy(g.ident_b[:, :], g.ident[:, :])
            v.wait_ge(loaded, 12 * 16)
            for k in (0, 1):
                v.tensor_copy(g.NODE[:, k, :], keys[:, k, :])
                v.tensor_scalar(lo[:, :], keys[:, k, :], P - 1, None, ALU.bitwise_and)
                link(v.tensor_scalar(hi[:, :], keys[:, k, :], 7, None, ALU.arith_shift_right))
                v.tensor_copy(g.DIG[:, k, :, 0], lo[:, :])
                link(v.tensor_copy(g.DIG[:, k, :, 1], hi[:, :]))
            for t in range(T):
                v.tensor_scalar(g.TM[:, :, t], types[:, :], float(t), None, ALU.is_equal)
            link(v.tensor_copy(g.ET[:, :], keys[:, 2, :]))



def count_keys(nc, g, k, tag):
    with Space(nc, tag) as s:
        staged, hot, counted = s.sem("staged"), s.sem("hot"), s.sem("counted")
        chain, summed, made = s.sem("chain"), s.sem("summed"), s.sem("made")
        dig = s.sb("dig", [P, 2, CH, 2])
        olo = s.sb("olo", [P, 2, CH, P], BF16)
        ohi = s.sb("ohi", [P, 2, CH, NB], BF16)
        zero = s.sb("zero", [P, P], BF16)
        tot = s.sb("tot", [P, NB])
        toti = s.sb("toti", [P, NB], I32)
        end = s.sb("end", [P, NB])
        diag = s.sb("diag", [NB, NB])
        endc = s.sb("endc", [NB, 1])
        first = s.sb("first", [NB, NT])
        full = s.sb("full", [NB, NT])
        pc = s.ps("pc", [P, 512])
        pt = s.ps("pt", [P, 512])
        pu = s.ps("pu", [P, 512])
        pn = s.ps("pn", [P, 2, 512])
        block = s.block()
        HT = NT // 2

        @block.gpsimd
        def _(pool):
            pool.iota(first[:, :], pattern=[[P, NT]], base=0, channel_multiplier=0,
                      allow_small_or_imprecise_dtypes=True).then_inc(made, 1)

        @block.vector
        def _(v):
            v.memset(zero[:, :], 0.0).then_inc(hot, 1)

            def stage(c, i, b):
                if old(c):
                    v.wait_ge(hot, c)
                move(v, dig[:, b, :, :], g.DIG[:, k, ds(c * CH, CH), :]).then_inc(staged, 1)

            def one_hots(c, i, b):
                v.wait_ge(staged, c + 1)
                if old(c):
                    v.wait_ge(counted, c - 1)
                compare(v, olo[:, b, :, :], g.iota_b[:, :], dig[:, b, :, 0:1])
                compare(v, ohi[:, b, :, :], g.iota_b[:, 0:NB], dig[:, b, :, 1:2]).then_inc(hot, 1)

            pipeline(v, 2 * EI, (one_hots, 0), (stage, 1))
            link = Chain(v, chain)
            v.wait_ge(counted, 2 * EI + 1)
            link(v.tensor_copy(g.CNT[:, k, :], pc[:, 0:NB]))
            v.wait_ge(summed, 2)
            link(v.tensor_scalar(tot[:, :], pt[:, 0:NB], float(P - 1), None, ALU.add))
            link(v.tensor_copy(toti[:, :], tot[:, :]))
            link(v.tensor_scalar(toti[:, :], toti[:, :], 7, 7, ALU.arith_shift_right, ALU.logical_shift_left))
            link(v.tensor_copy(tot[:, :], toti[:, :]))
            link(v.tensor_tensor_scan(end[:, :], tot[:, :], g.zeros[:, 0:NB], 0.0, ALU.add, ALU.add))
            link(v.tensor_tensor(tot[:, :], end[:, :], tot[:, :], ALU.subtract))
            link(v.tensor_tensor(g.START[:, k, :], pu[:, 0:NB], tot[:, :], ALU.add))
            link(v.tensor_tensor(diag[:, :], end[0:NB, :], g.ident[0:NB, 0:NB], ALU.mult))
            link(v.tensor_reduce(endc[:, :], diag[:, :], AX.X, ALU.add))
            v.wait_ge(made, 1)
            v.tensor_scalar(full[:, :], first[:, :], endc[:, 0:1], None, ALU.is_ge).then_inc(summed, 1)
            v.wait_ge(summed, 5)
            for q in (0, 1):
                link(v.tensor_scalar(g.BIN[:, k, q * HT:(q + 1) * HT], pn[:, q, 0:HT], float(NB - 1), None, ALU.min))
            link(v.tensor_copy(g.BINI[:, k, :], g.BIN[0:1, k, :]))
            v.tensor_tensor(g.TF[:, k, 0, 1:NT], g.BIN[:, k, 1:NT], g.BIN[:, k, 0:NT - 1], ALU.not_equal)
            link(v.memset(g.TF[:, k, 0, 0:1], 1.0))
            link(v.memset(g.TF[:, k, 1, NT - 1:NT], 1.0))
            link(v.tensor_copy(g.TF[:, k, 1, 0:NT - 1], g.TF[:, k, 0, 1:NT]))
            link(v.tensor_scalar(g.TF[:, k, :, :], g.TF[:, k, :, :], -BIG, None, ALU.mult))

        @block.tensor
        def _(pe):
            pe.wait_ge(hot, 1)
            pe.matmul(pc[:, 0:NB], zero[:, :], zero[:, 0:NB], start=True, stop=False, skip_group_check=True)

            def chunk(c, i, b, first):
                pe.wait_ge(hot, c + 2)
                for j in range(CH):
                    last = pe.matmul(pc[:, 0:NB], olo[:, b, j, :], ohi[:, b, j, :], start=False, stop=False,
                                     skip_group_check=True)
                last.then_inc(counted, 1)

            pairs(pe, EI, chunk)
            pe.matmul(pc[:, 0:NB], zero[:, :], zero[:, 0:NB], start=False, stop=True,
                      skip_group_check=True).then_inc(counted, 1)
            pe.wait_ge(chain, 1)
            pe.matmul(pt[:, 0:NB], g.ones[:, :], g.CNT[:, k, :], start=True, stop=True).then_inc(summed, 1)
            pe.matmul(pu[:, 0:NB], g.before[:, :], g.CNT[:, k, :], start=True, stop=True).then_inc(summed, 1)
            pe.wait_ge(summed, 3)
            for q in (0, 1):
                pe.matmul(pn[:, q, 0:HT], g.ones[0:NB, :], full[:, q * HT:(q + 1) * HT],
                          start=True, stop=True).then_inc(summed, 1)


def place_edges(nc, g, k, slots, tag):
    with Space(nc, tag) as s:
        staged, hot_lo, hot_hi, turned, copied_b = (s.sem(x) for x in ("staged", "hot_lo", "hot_hi", "turned", "copied_b"))
        copied_f, equal, kept, tally = s.sem("copied_f"), s.sem("equal"), s.sem("kept"), s.sem("tally")
        tallied, carried, seen_ok, found = s.sem("tallied"), s.sem("carried"), s.sem("seen_ok"), s.sem("found")
        picked, ranked, index_ok, small = s.sem("picked"), s.sem("ranked"), s.sem("index_ok"), s.sem("small")
        sent = [s.sem(f"sent{q}") for q in range(4)]
        cleared, reset_ok, zeroed = s.sem("cleared"), s.sem("reset_ok"), s.sem("zeroed")
        dig = s.sb("dig", [P, 2, CH, 2])
        rec = s.sb("rec", [P, 2, CH, RW])
        olo = s.sb("olo", [P, 2, CH, P], BF16)
        ohi = s.sb("ohi", [P, 2, CH, NB], BF16)
        otb = s.sb("otb", [P, 2, CH, P], BF16)
        otf = s.sb("otf", [P, 2, CH, P])
        bm = s.sb("bm", [P, 2, CH, P], BF16)
        before = s.sb("before", [P, CH, P])
        reset = s.sb("reset", [P, NB, CH + 1])
        seq = s.sb("seq", [P, 2, NB, CH + 1])
        seen = s.sb("seen", [P, 2, NB, CH + 1])
        hits = s.sb("hits", [P, 2, CH, NB])
        pos = s.sb("pos", [P, 2, CH])
        posi = s.sb("posi", [P, 2, 3, CH], I32)
        idx = s.sb("idx", [P, 2, CH], U32)
        zrow = s.sb("zrow", [P, NT * RW])
        pt = s.ps("pt", [P, 1, CH, P], BF16)
        pe_q = s.ps("pe_q", [P, CH, P])
        pd = s.ps("pd", [P, 2, 512])
        pr = s.ps("pr", [P, 2, 512])
        waited = s.sem("waited")
        block = s.block()

        @block.sync
        def _(sp):
            sp.wait_ge(zeroed, 1)
            for q in range(4):
                sp.dma_start(slots[q].rearrange("(p c) w -> p (c w)", p=P), zrow[:, :]).then_inc(cleared, 16)
            sp.wait_ge(cleared, 64)

        @block.vector
        def _(v):
            v.memset(zrow[:, :], 0.0).then_inc(zeroed, 1)
            v.memset(reset[:, :, :], 1.0).then_inc(reset_ok, 1)
            v.wait_ge(reset_ok, 1)
            v.memset(reset[:, :, 0:1], 0.0)
            for j in range(CH):
                v.tensor_copy(before[:, j, :], g.before[:, :])
            v.tensor_copy(seen[:, 1, :, CH], g.START[:, k, :]).then_inc(seen_ok, 1)

            def stage(c, i, b):
                move(v, dig[:, b, :, :], g.DIG[:, k, ds(c * CH, CH), :]).then_inc(staged, 1)

            def low_digits(c, i, b):
                v.wait_ge(staged, c + 1)
                if old(c):
                    v.wait_ge(tally, c - 1)
                compare(v, olo[:, b, :, :], g.iota_b[:, :], dig[:, b, :, 0:1]).then_inc(hot_lo, 1)

            def high_digits(c, i, b):
                if old(c):
                    v.wait_ge(found, c - 1)
                compare(v, ohi[:, b, :, :], g.iota_b[:, 0:NB], dig[:, b, :, 1:2]).then_inc(hot_hi, 1)

            def keep_earlier(c, i, b):
                v.wait_ge(equal, c + 1)
                v.tensor_tensor(bm[:, b, :, :], pe_q[:, :, :], before[:, :, :], ALU.mult).then_inc(kept, 1)

            def count_up(c, i, b):
                v.wait_ge(seen_ok, c + 1)
                v.tensor_copy(seq[:, b, :, 0], seen[:, 1 - b, :, CH])
                v.wait_ge(tally, c + 1)
                v.tensor_copy(seq[:, b, :, 1:CH + 1],
                              pd[:, b, 0:CH * NB].rearrange("p (j h) -> p h j", j=CH)).then_inc(carried, 1)
                v.wait_ge(carried, c + 1)
                v.tensor_tensor_scan(seen[:, b, :, :].rearrange("p h j -> p (h j)"),
                                     reset[:, :, :].rearrange("p h j -> p (h j)"),
                                     seq[:, b, :, :].rearrange("p h j -> p (h j)"), 0.0,
                                     ALU.mult, ALU.add).then_inc(seen_ok, 1)

            def finish(c, i, b):
                v.wait_ge(found, c + 1)
                v.tensor_tensor(hits[:, b, :, :], pr[:, b, 0:CH * NB].rearrange("p (j h) -> p j h", j=CH),
                                ohi[:, b, :, :], ALU.mult).then_inc(picked, 1)
                if old(c):
                    for q in range(4):
                        v.wait_ge(sent[q], (c - 1) * (CH // 4 * 16))
                move(v, rec[:, b, :, 0], g.NODE[:, 1 - k, ds(c * CH, CH)])
                v.wait_ge(picked, c + 1)
                v.tensor_reduce(pos[:, b, :], hits[:, b, :, :], AX.X, ALU.add).then_inc(ranked, 1)
                v.tensor_scalar(rec[:, b, :, 1], g.DIG[:, k, ds(c * CH, CH), 0], 1.0, None, ALU.add)
                v.wait_ge(ranked, c + 1)
                v.tensor_copy(posi[:, b, 0, :], pos[:, b, :]).then_inc(small, 1)
                move(v, rec[:, b, :, 2], g.ET[:, ds(c * CH, CH)])
                v.wait_ge(small, c * 2 + 1)
                v.tensor_scalar(posi[:, b, 1, :], posi[:, b, 0, :], P - 1, None, ALU.bitwise_and)
                v.tensor_scalar(posi[:, b, 2, :], posi[:, b, 0, :], 7, None, ALU.arith_shift_right).then_inc(small, 1)
                move(v, rec[:, b, :, 3], g.EW[:, ds(c * CH, CH)])
                v.wait_ge(small, c * 2 + 2)
                v.scalar_tensor_tensor(out=idx[:, b, :], in0=posi[:, b, 1, :], scalar=float(NT),
                                       in1=posi[:, b, 2, :], op0=ALU.mult, op1=ALU.add).then_inc(index_ok, 1)

            pipeline(v, 2 * EI, (low_digits, 1), (keep_earlier, 0), (finish, -1), (high_digits, 1), (count_up, 0), (stage, 2))

        @block.tensor
        def _(pe):
            def turn(c, i, b):
                pe.wait_ge(hot_lo, c + 1)
                if old(c, 1):
                    pe.wait_ge(copied_f, c)
                    pe.wait_ge(copied_b, c)
                for j in range(CH):
                    last = pe.transpose(pt[:, 0, j, :], olo[:, b, j, :], g.ident_b[:, :])
                last.then_inc(turned, 1)

            def count(c, i, b):
                pe.wait_ge(hot_hi, c + 1)
                if old(c):
                    pe.wait_ge(carried, c - 1)
                for j in range(CH):
                    last = pe.matmul(pd[:, b, j * NB:(j + 1) * NB], olo[:, b, j, :], ohi[:, b, j, :],
                                     start=True, stop=True)
                last.then_inc(tally, 1)

            def equal_digits(c, i, b):
                pe.wait_ge(copied_b, c + 1)
                if old(c, 1):
                    pe.wait_ge(kept, c)
                for j in range(CH):
                    last = pe.matmul(pe_q[:, j, :], otb[:, b, j, :], otb[:, b, j, :], start=True, stop=True)
                last.then_inc(equal, 1)

            def find(c, i, b):
                pe.wait_ge(copied_f, c + 1)
                pe.wait_ge(kept, c + 1)
                pe.wait_ge(seen_ok, c + 2)
                if old(c):
                    pe.wait_ge(picked, c - 1)
                for j in range(CH):
                    pe.matmul(pr[:, b, j * NB:(j + 1) * NB], otf[:, b, j, :], seen[:, b, :, j],
                              start=True, stop=False)
                    last = pe.matmul(pr[:, b, j * NB:(j + 1) * NB], bm[:, b, j, :], ohi[:, b, j, :],
                                     start=False, stop=True)
                last.then_inc(found, 1)

            pipeline(pe, 2 * EI, (turn, 1), (equal_digits, 1), (count, 1), (find, 0))

        @block.scalar
        def _(act):
            def chunk(c, i, b, first):
                act.wait_ge(turned, c + 1)
                if not first:
                    act.wait_ge(found, c - 1)
                act.activation(otb[:, b, :, :], pt[:, 0, :, :], ACT.Copy).then_inc(copied_b, 1)
                act.activation(otf[:, b, :, :], pt[:, 0, :, :], ACT.Copy).then_inc(copied_f, 1)

            pairs(act, EI, chunk)

        @block.gpsimd
        def _(pool):
            pool.wait_ge(cleared, 64)
            passed = Passed(pool, waited)

            def chunk(c, i, b, first):
                pool.wait_ge(index_ok, c + 1)
                for j in range(CH):
                    q = j % 4
                    pool.wait_ge(sent[q], (c * 2 + j // 4) * 16)
                    passed()
                    pool.indirect_dma_start(
                        out=slots[q], out_offset=bass.IndirectOffsetOnAxis(ap=idx[:, b, j:j + 1], axis=0),
                        in_=rec[:, b, j, :], in_offset=None).then_inc(sent[q], 16)

            pairs(pool, EI, chunk)
            for q in range(4):
                pool.wait_ge(sent[q], EC // 4 * 16)


def slot_tables(nc, g, k, slots, flags, tag):
    with Space(nc, tag) as s:
        loaded, chain, turned, back, out = s.sem("loaded"), s.sem("chain"), s.sem("turned"), s.sem("back"), s.sem("out")
        copied = s.sem("copied")
        part = [s.sb(f"part{q}", [P, NTP * RW]) for q in range(4)]
        xl = s.sb("xl", [P, TB * P])
        fl = s.sb("fl", [P, TB, P])
        pt = s.ps("pt", [P, 2, 512])
        block = s.block()
        local4 = part[1]
        lastx = part[2][:, :].rearrange("p (t e) -> p t e", e=P)

        @block.sync
        def _(sp):
            for q in range(4):
                sp.dma_start(part[q][:, 0:NT * RW], slots[q].rearrange("(p c) w -> p (c w)", p=P)).then_inc(loaded, 16)
            sp.wait_ge(chain, 9)
            sp.dma_start(flags, fl[:, :, :].rearrange("p t e -> p (t e)")).then_inc(out, 16)
            sp.wait_ge(loaded, 64)
            sp.wait_ge(out, 16)

        @block.vector
        def _(v):
            link = Chain(v, chain)
            v.wait_ge(loaded, 64)
            w = NT * RW
            v.tensor_tensor(part[0][:, 0:w], part[0][:, 0:w], part[1][:, 0:w], ALU.add)
            link(v.tensor_tensor(part[2][:, 0:w], part[2][:, 0:w], part[3][:, 0:w], ALU.add))
            link(v.tensor_tensor(part[0][:, 0:w], part[0][:, 0:w], part[2][:, 0:w], ALU.add))
            r = part[0][:, 0:w].rearrange("p (t w) -> p t w", w=RW)
            v.tensor_copy(g.OTHER[:, k, 0:NT], r[:, :, 0])
            v.memset(g.LOCAL[:, k, NT:NTP], -1.0)
            link(v.tensor_scalar(g.LOCAL[:, k, 0:NT], r[:, :, 1], -1.0, None, ALU.add))
            if k == 1:
                v.scalar_tensor_tensor(out=g.KVROW[:, 0:NT], in0=r[:, :, 0], scalar=float(R), in1=r[:, :, 2],
                                       op0=ALU.mult, op1=ALU.add)
                link(v.tensor_copy(g.WEIGHT[:, 0:NT], r[:, :, 3]))
            else:
                link(v.memset(fl[:, :, 0:1], 0.0))
            link(v.tensor_copy(local4[:, :].rearrange("p (t h) -> p t h", h=H),
                               cols3(g.LOCAL[:, k, :]).to_broadcast([P, NTP, H])))
            v.wait_ge(copied, TB // 4)
            x3 = xl[:, :].rearrange("p (t e) -> p t e", e=P)
            v.tensor_tensor(fl[:, :, 1:P], x3[:, :, 1:P], x3[:, :, 0:P - 1], ALU.not_equal)
            v.memset(lastx[:, :, P - 1:P], 1.0)
            link(v.memset(fl[:, :, 0:1], 1.0))
            link(v.tensor_copy(lastx[:, :, 0:P - 1], fl[:, :, 1:P]))
            link(v.scalar_tensor_tensor(out=part[2][:, :], in0=xl[:, :], scalar=1.0, in1=part[2][:, :],
                                        op0=ALU.add, op1=ALU.mult))
            v.tensor_scalar(part[2][:, :], part[2][:, :], -1.0, None, ALU.add).then_inc(back, 1)
            v.wait_ge(back, 1)
            link(v.tensor_scalar(fl[:, :, :], fl[:, :, :], -BIG, None, ALU.mult))
            assert link.n == 9
            for m in range(TB // 4):
                v.wait_ge(back, 2 + m)
                o = pt[:, m % 2, :].rearrange("p (t h) -> p t h", h=H)
                v.tensor_copy(g.LAST[:, k, m * P:(m + 1) * P], o[:, :, 0]).then_inc(copied, 1)

        @block.scalar
        def _(act):
            for m in range(TB // 4):
                act.wait_ge(turned, m + 1)
                act.activation(xl[:, m * 512:(m + 1) * 512], pt[:, m % 2, :], ACT.Copy).then_inc(copied, 1)

        @block.tensor
        def _(pe):
            pe.wait_ge(chain, 5)
            for m in range(TB // 4):
                if m >= 2:
                    pe.wait_ge(copied, m - 1)
                for q in range(4):
                    last = pe.transpose(pt[:, m % 2, q * P:(q + 1) * P], local4[:, (4 * m + q) * P:(4 * m + q + 1) * P],
                                        g.ident[:, :])
                last.then_inc(turned, 1)
            pe.wait_ge(back, 1)
            for m in range(TB // 4):
                pe.wait_ge(copied, TB // 4 if m < 2 else TB // 4 + m - 1)
                for q in range(4):
                    last = pe.transpose(pt[:, m % 2, q * P:(q + 1) * P], part[2][:, (4 * m + q) * P:(4 * m + q + 1) * P],
                                        g.ident[:, :])
                last.then_inc(back, 1)



def edge_logits(nc, g, k, table, width, rowidx, node, nw, score, voff, stash, tag):
    with Space(nc, tag) as s:
        index_ok, gathered = s.sem("index_ok"), [s.sem(f"gathered{b}") for b in (0, 1)]
        stored = [s.sem(f"stored{b}") for b in (0, 1)]
        staged, hot, turned, copied, spread = (s.sem(x) for x in ("staged", "hot", "turned", "copied", "spread"))
        raw, kinked, logit = s.sem("raw"), s.sem("kinked"), s.sem("logit")
        G = s.sb("G", [P, 2, CH, width])
        idx = s.sb("idx", [P, 2, CH], U32)
        loc = s.sb("loc", [P, 2, CH])
        neg = s.sb("neg", [P, 2, CH])
        O = s.sb("O", [P, 2, CH, P], BF16)
        OT = s.sb("OT", [P, 2, CH, P], BF16)
        parts = s.sb("parts", [P, 3, NB, nw], BF16)
        split = s.sem("split")
        prod = s.sb("prod", [P, CH, nw])
        red = s.sb("red", [P, 2, CH, H])
        pt = s.ps("pt", [P, 2, CH, P], BF16)
        pe_b = s.ps("pe_x", [P, 2, max(CH * nw, 512)])
        pe_x = pe_b[:, :, 0:CH * nw].rearrange("p b (j w) -> p b j w", w=nw)
        waited = s.sem("waited")
        block = s.block()

        @block.gpsimd
        def _(pool):
            passed = Passed(pool, waited)

            def chunk(c, i, b, first):
                pool.wait_ge(index_ok, c + 1)
                if not first:
                    pool.wait_ge(logit, c - 1)
                    pool.wait_ge(stored[b], i * 16)
                passed()
                for j in range(CH):
                    pool.indirect_dma_start(
                        out=G[:, b, j, :], out_offset=None, in_=table,
                        in_offset=bass.IndirectOffsetOnAxis(ap=idx[:, b, j:j + 1], axis=0)).then_inc(gathered[b], 16)

            pairs(pool, NI, chunk)

        @block.sync
        def _(sp):
            def chunk(c, i, b, first):
                sp.wait_ge(gathered[b], i * (16 * CH) + 16 * CH)
                sp.dma_start(stash[ds(c, 1), :, :].rearrange("o p (j w) -> (o p) j w", j=CH),
                             G[:, b, :, voff:voff + D]).then_inc(stored[b], 16)

            pairs(sp, NI, chunk)
            for b in (0, 1):
                sp.wait_ge(stored[b], NI * 16)

        @block.scalar
        def _(act):
            def index(c, i, b):
                if old(c):
                    act.wait_ge(gathered[b], i * (16 * CH))
                act.activation(idx[:, b, :], rowidx[:, ds(c * CH, CH)], ACT.Copy).then_inc(index_ok, 1)

            def copy(c, i, b):
                act.wait_ge(turned, c + 1)
                if old(c):
                    act.wait_ge(spread, c - 1)
                act.activation(OT[:, b, :, :], pt[:, b, :, :], ACT.Copy).then_inc(copied, 1)

            pipeline(act, 2 * NI, (copy, 0), (index, 2))

        @block.vector
        def _(v):
            split_exactly(Chain(v, split), v, [parts[:, q, :, :] for q in range(3)], node)

            def stage(c, i, b):
                move(v, loc[:, b, :], g.LOCAL[:, k, ds(c * CH, CH)]).then_inc(staged, 1)

            def one_hots(c, i, b):
                v.wait_ge(staged, c + 1)
                if old(c):
                    v.wait_ge(turned, c - 1)
                v.tensor_scalar(neg[:, b, :], loc[:, b, :], 0.0, BIG, ALU.min, ALU.mult)
                for j in range(CH):
                    last = v.tensor_scalar(O[:, b, j, :], g.iota_b[:, :], loc[:, b, j:j + 1], None, ALU.is_equal)
                last.then_inc(hot, 1)

            def logits(c, i, b):
                v.wait_ge(spread, c + 1)
                v.wait_ge(gathered[b], i * (16 * CH) + 16 * CH)
                sc = G[:, b, :, score:score + nw]
                if nw == H:
                    v.tensor_tensor(prod[:, :, :], pe_x[:, b, :, :], sc, ALU.add).then_inc(raw, 1)
                    v.wait_ge(raw, c + 1)
                    v.scalar_tensor_tensor(out=red[:, b, :, :], in0=prod[:, :, :], scalar=0.2, in1=prod[:, :, :],
                                           op0=ALU.mult, op1=ALU.max).then_inc(kinked, 1)
                else:
                    v.tensor_tensor(prod[:, :, :], pe_x[:, b, :, :], sc, ALU.mult).then_inc(raw, 1)
                    v.wait_ge(raw, c + 1)
                    v.tensor_reduce(red[:, b, :, :], prod[:, :, :].rearrange("p j (h d) -> p j h d", h=H),
                                    AX.X, ALU.add).then_inc(kinked, 1)
                v.wait_ge(kinked, c + 1)
                v.tensor_tensor(g.LG[:, ds(c * CH, CH), :], red[:, b, :, :],
                                cols3(neg[:, b, :]).to_broadcast([P, CH, H]), ALU.add).then_inc(logit, 1)

            pipeline(v, 2 * NI, (one_hots, 1), (logits, 0), (stage, 2))

        @block.tensor
        def _(pe):
            pe.wait_ge(split, 5)

            def turn(c, i, b):
                pe.wait_ge(hot, c + 1)
                if old(c):
                    pe.wait_ge(copied, c - 1)
                for j in range(CH):
                    last = pe.transpose(pt[:, b, j, :], O[:, b, j, :], g.ident_b[:, :])
                last.then_inc(turned, 1)

            def to_edges(c, i, b):
                bins = nc.values_load_multi_w_load_instructions(
                    g.BINI[0:1, k, ds(c * CH, CH)], engines=[pe.engine], min_val=0, max_val=NB - 1,
                    skip_runtime_bounds_check_because="the table is cut at the last bin")[1]
                pe.wait_ge(copied, c + 1)
                if old(c):
                    pe.wait_ge(logit, c - 1)
                for j in range(CH):
                    for q in range(3):
                        last = pe.matmul(pe_x[:, b, j, :], OT[:, b, j, :], parts[:, q, ds(bins[j], 1), :],
                                         start=(q == 0), stop=(q == 2))
                last.then_inc(spread, 1)

            pipeline(pe, 2 * NI, (to_edges, 0), (turn, 1))


def segment_max(nc, g, k, flags, tag):
    with Space(nc, tag) as s:
        loaded, turned, copied, scanned, back, taken = (s.sem(x) for x in ("loaded", "turned", "copied", "scanned", "back", "taken"))
        staged, hot, moved, kept, chain, init = (s.sem(x) for x in ("staged", "hot", "moved", "kept", "chain", "init"))
        fl = g.MX[:, :, :].rearrange("p t h -> p (t h)")
        mt = g.ACC[:, :, :].rearrange("p n w -> p (n w)")[:, 0:NT * (H + 1)].rearrange("p (t h) -> p t h", h=H + 1)
        xt = s.sb("xt", [P, TB * P])
        fw = g.MXP
        loc = s.sb("loc", [P, 2, CH])
        OL = s.sb("OL", [P, 2, CH, P], BF16)
        fs = s.sb("fs", [P, 2, 3, CH, H + 1], BF16)
        pt = s.ps("pt", [P, 2, 512])
        pm = s.ps("pm", [P, 2, 512])
        block = s.block()
        lg = g.LG[:, :, :].rearrange("p t h -> p (t h)")
        M4 = TB // 4

        @block.sync
        def _(sp):
            sp.dma_start(fl, flags).then_inc(loaded, 16)
            sp.wait_ge(loaded, 16)

        @block.scalar
        def _(act):
            for m in range(M4):
                act.wait_ge(turned, m + 1)
                act.activation(xt[:, m * 512:(m + 1) * 512], pt[:, m % 2, :], ACT.Copy).then_inc(copied, 1)
            for m in range(M4):
                act.wait_ge(back, m + 1)
                act.activation(fl[:, m * 512:(m + 1) * 512], pt[:, m % 2, :], ACT.Copy).then_inc(taken, 1)

        @block.vector
        def _(v):
            link = Chain(v, chain)
            v.memset(fw[:, 0, :, H:H + 1], 1.0)
            v.memset(fw[:, 1:3, :, H:H + 1], 0.0).then_inc(init, 1)
            v.wait_ge(loaded, 16)
            v.wait_ge(copied, M4)
            v.tensor_tensor_scan(xt[:, :], fl, xt[:, :], -BIG, ALU.add, ALU.max).then_inc(scanned, 1)
            v.wait_ge(taken, M4)
            v.wait_ge(init, 1)
            split_exactly(link, v, [fw[:, q, :, 0:H] for q in range(3)], g.MX[:, :, :])

            def stage(c, i, b):
                move(v, loc[:, b, :], g.LAST[:, k, ds(c * CH, CH)]).then_inc(staged, 1)

            def one_hots(c, i, b):
                v.wait_ge(staged, c + 1)
                if old(c):
                    v.wait_ge(moved, c - 1)
                move(v, fs[:, b, :, :, :], fw[:, :, ds(c * CH, CH), :])
                compare(v, OL[:, b, :, :], g.iota_b[:, :], cols3(loc[:, b, :])).then_inc(hot, 1)

            def keep(c, i, b):
                v.wait_ge(moved, c + 1)
                move(v, mt[:, ds(c * CH, CH), :],
                     pm[:, b, 0:CH * (H + 1)].rearrange("p (j h) -> p j h", j=CH)).then_inc(kept, 1)

            pipeline(v, 2 * NI, (one_hots, 1), (keep, 0), (stage, 2))
            v.wait_ge(kept, 2 * NI)
            link(v.tensor_scalar(mt[:, :, H], mt[:, :, H], -1.0, BIG, ALU.add, ALU.mult))
            link(v.tensor_tensor(mt[:, :, 0:H], mt[:, :, 0:H],
                                 mt[:, :, H:H + 1].to_broadcast([P, NT, H]), ALU.add))
            for h in range(H):
                v.tensor_tensor_scan(g.MX[:, 0:NT, h], g.TF[:, k, 0, :], mt[:, :, h], -BIG, ALU.add, ALU.max)
            link(v.memset(loc[:, :, :], 0.0))
            for h in range(H):
                last = v.tensor_tensor_scan(mt[:, ::-1, h], g.TF[:, k, 1, ::-1], mt[:, ::-1, h], -BIG, ALU.add, ALU.max)
            link(last)
            link(v.tensor_tensor(g.MX[:, 0:NT, :], g.MX[:, 0:NT, :], mt[:, :, 0:H], ALU.max))
            split_exactly(link, v, [g.MXP[:, q, 0:NT, 0:H] for q in range(3)], g.MX[:, 0:NT, :])

        @block.tensor
        def _(pe):
            for m in range(M4):
                if m >= 2:
                    pe.wait_ge(copied, m - 1)
                for q in range(4):
                    last = pe.transpose(pt[:, m % 2, q * P:(q + 1) * P], lg[:, (4 * m + q) * P:(4 * m + q + 1) * P],
                                        g.ident[:, :])
                last.then_inc(turned, 1)
            pe.wait_ge(scanned, 1)
            for m in range(M4):
                if m >= 2:
                    pe.wait_ge(taken, m - 1)
                for q in range(4):
                    last = pe.transpose(pt[:, m % 2, q * P:(q + 1) * P], xt[:, (4 * m + q) * P:(4 * m + q + 1) * P],
                                        g.ident[:, :])
                last.then_inc(back, 1)

            def chunk(c, i, b, first):
                pe.wait_ge(hot, c + 1)
                if not first:
                    pe.wait_ge(kept, c - 1)
                for j in range(CH):
                    for q in range(3):
                        last = pe.matmul(pm[:, b, j * (H + 1):(j + 1) * (H + 1)], OL[:, b, j, :], fs[:, b, q, j, :],
                                         start=(q == 0), stop=(q == 2))
                last.then_inc(moved, 1)

            pairs(pe, NI, chunk)


def agg_cell(pa, b, j):
    return pa[:, b, j // 3, (j % 3) * (D + H):(j % 3 + 1) * (D + H)]


def edge_sums(nc, g, k, stash, tag):
    with Space(nc, tag) as s:
        arrived = [s.sem(f"arrived{b}") for b in (0, 1)]
        staged, hot, turned, copied, spread, wide = (s.sem(x) for x in ("staged", "hot", "turned", "copied", "spread", "wide"))
        shifted, powered, weighted, summed, added, init = (s.sem(x) for x in ("shifted", "powered", "weighted", "summed", "added", "init"))
        mx_ok = s.sem("mx_ok")
        V = s.sb("V", [P, 2, CH, D])
        WV = s.sb("WV", [P, 2, CH, D + H])
        loc = s.sb("loc", [P, 2, CH])
        O = s.sb("O", [P, 2, CH, P])
        OB = s.sb("OB", [P, 2, CH, P], BF16)
        OT = s.sb("OT", [P, 2, CH, P], BF16)
        sh = s.sb("sh", [P, 2, CH, H])
        mx = s.sb("mx", [P, 2, 3, CH, H], BF16)
        pt = s.ps("pt", [P, 1, CH, P], BF16)
        pe_x = s.ps("pe_x", [P, 512])
        pa = s.ps("pa", [P, 2, 3, 512])
        block = s.block()
        NC = 2 * NI

        @block.sync
        def _(sp):
            def load(c, i, b):
                if old(c):
                    sp.wait_ge(weighted, c - 1)
                sp.dma_start(V[:, b, :, :].rearrange("p j w -> p (j w)"),
                             stash[ds(c, 1), :, :].rearrange("o p w -> (o p) w")).then_inc(arrived[b], 16)

            pipeline(sp, NC, (load, 0))

        @block.scalar
        def _(act):
            def copies(c, i, b):
                if old(c):
                    act.wait_ge(spread, c - 1)
                act.activation(mx[:, b, :, :, :], g.MXP[:, :, ds(c * CH, CH), 0:H], ACT.Copy).then_inc(mx_ok, 1)
                act.wait_ge(turned, c + 1)
                act.activation(OT[:, b, :, :], pt[:, 0, :, :], ACT.Copy).then_inc(copied, 1)
                if old(c):
                    act.wait_ge(summed, (c - 1) * CH)
                act.activation(O[:, b, :, :], OB[:, b, :, :], ACT.Copy).then_inc(wide, 1)

            def power(c, i, b):
                act.wait_ge(shifted, c + 1)
                if old(c):
                    act.wait_ge(summed, (c - 1) * CH)
                act.activation(WV[:, b, :, D:D + H], sh[:, b, :, :], ACT.Exp).then_inc(powered, 1)

            pipeline(act, NC, (power, 1), (copies, 2))

        @block.vector
        def _(v):
            v.memset(g.ACC[:, :, :], 0.0).then_inc(init, 1)
            v.wait_ge(init, 1)

            def stage(c, i, b):
                move(v, loc[:, b, :], g.LOCAL[:, k, ds(c * CH, CH)]).then_inc(staged, 1)

            def shift(c, i, b):
                v.wait_ge(spread, c + 1)
                if old(c):
                    v.wait_ge(powered, c - 1)
                v.tensor_tensor(sh[:, b, :, :], g.LG[:, ds(c * CH, CH), :],
                                pe_x[:, 0:CH * H].rearrange("p (j h) -> p j h", j=CH), ALU.subtract).then_inc(shifted, 1)

            def weigh(c, i, b):
                v.wait_ge(arrived[b], i * 16 + 16)
                v.wait_ge(powered, c + 1)
                if old(c):
                    v.wait_ge(summed, (c - 1) * CH)
                v.tensor_tensor(WV[:, b, :, 0:D].rearrange("p j (h d) -> p j h d", h=H),
                                V[:, b, :, :].rearrange("p j (h d) -> p j h d", h=H),
                                WV[:, b, :, D:D + H].rearrange("p j (h o) -> p j h o", o=1).to_broadcast([P, CH, H, HD]),
                                ALU.mult).then_inc(weighted, 1)

            def one_hots_and_add(c, i, b):
                new, sum_up = not isinstance(c, int) or c < NC, old(c, 4)
                if sum_up:
                    bins = nc.values_load_multi_w_load_instructions(
                        g.BINI[0:1, k, ds((c - 4) * CH, CH)], engines=[v.engine], min_val=0, max_val=NB - 1,
                        skip_runtime_bounds_check_because="the table is cut at the last bin")[1]
                if new:
                    v.wait_ge(staged, c + 1)
                    if old(c):
                        v.wait_ge(turned, c - 1)
                        v.wait_ge(wide, c - 1)
                for j in range(CH):
                    if new:
                        last = v.tensor_scalar(OB[:, b, j, :], g.iota_b[:, :], loc[:, b, j:j + 1], None, ALU.is_equal)
                    if sum_up:
                        if j % 3 == 0:
                            v.wait_ge(summed, (c - 4) * CH + min(j + 3, CH))
                        if old(c, 5) or j:
                            v.wait_ge(added, (c - 4) * CH + j)
                        a = g.ACC[:, ds(bins[j], 1), :]
                        v.tensor_tensor(a, a, agg_cell(pa, b, j), ALU.add).then_inc(added, 1)
                if new:
                    last.then_inc(hot, 1)

            pipeline(v, NC, (weigh, 0), (shift, 1), (one_hots_and_add, 3), (stage, 4))
            for c in range(NC, NC + 4):
                one_hots_and_add(c, c // 2, c % 2)
            v.wait_ge(added, NT)

        @block.tensor
        def _(pe):
            def turn(c, i, b):
                pe.wait_ge(hot, c + 1)
                if old(c, 1):
                    pe.wait_ge(copied, c)
                for j in range(CH):
                    last = pe.transpose(pt[:, 0, j, :], OB[:, b, j, :], g.ident_b[:, :])
                last.then_inc(turned, 1)

            def to_edges(c, i, b):
                pe.wait_ge(copied, c + 1)
                pe.wait_ge(mx_ok, c + 1)
                if old(c, 1):
                    pe.wait_ge(shifted, c)
                for j in range(CH):
                    for q in range(3):
                        last = pe.matmul(pe_x[:, j * H:(j + 1) * H], OT[:, b, j, :], mx[:, b, q, j, :],
                                         start=(q == 0), stop=(q == 2))
                last.then_inc(spread, 1)

            def sums(c, i, b):
                pe.wait_ge(wide, c + 1)
                pe.wait_ge(weighted, c + 1)
                for j in range(CH):
                    if old(c) and j % 3 == 0:
                        pe.wait_ge(added, (c - 2) * CH + min(j + 3, CH))
                    pe.matmul(agg_cell(pa, b, j), O[:, b, j, :], WV[:, b, j, :], start=True, stop=True).then_inc(summed, 1)

            pipeline(pe, NC, (to_edges, 1), (turn, 2), (sums, 0))


def plain_sums(nc, g, table, weight, tag):
    w = D + 2 if weight else D
    with Space(nc, tag) as s:
        index_ok, gathered = s.sem("index_ok"), [s.sem(f"gathered{b}") for b in (0, 1)]
        staged, hot, summed, added, put = (s.sem(x) for x in ("staged", "hot", "summed", "added", "put"))
        G = s.sb("G", [P, 2, CH, D + H])
        idx = s.sb("idx", [P, 2, CH], U32)
        loc = s.sb("loc", [P, 2, CH])
        O = s.sb("O", [P, 2, CH, P])
        pa = s.ps("pa", [P, 2, 3, 512])
        waited = s.sem("waited")
        block = s.block()
        k = 1

        @block.gpsimd
        def _(pool):
            passed = Passed(pool, waited)

            def chunk(c, i, b, first):
                pool.wait_ge(index_ok, c + 1)
                if not first:
                    pool.wait_ge(summed, c - 1)
                passed()
                for j in range(CH):
                    pool.indirect_dma_start(
                        out=G[:, b, j, 0:D], out_offset=None, in_=table,
                        in_offset=bass.IndirectOffsetOnAxis(ap=idx[:, b, j:j + 1], axis=0)).then_inc(gathered[b], 16)

            pairs(pool, NI, chunk)

        @block.scalar
        def _(act):
            def chunk(c, i, b, first):
                if not first:
                    act.wait_ge(gathered[b], i * (16 * CH))
                act.activation(idx[:, b, :], g.OTHER[:, k, ds(c * CH, CH)], ACT.Copy).then_inc(index_ok, 1)
                if weight:
                    if not first:
                        act.wait_ge(summed, c - 1)
                    act.activation(G[:, b, :, D:D + 2], cols3(g.WEIGHT[:, ds(c * CH, CH)]).to_broadcast([P, CH, 2]),
                                   ACT.Copy).then_inc(put, 1)

            pairs(act, NI, chunk)

        @block.vector
        def _(v):
            def one_hots(c, b, first):
                move(v, loc[:, b, :], g.LOCAL[:, k, ds(c * CH, CH)]).then_inc(staged, 1)
                v.wait_ge(staged, c + 1)
                if not first:
                    v.wait_ge(summed, c - 1)
                for j in range(CH):
                    last = v.tensor_scalar(O[:, b, j, :], g.iota[:, :], loc[:, b, j:j + 1], None, ALU.is_equal)
                last.then_inc(hot, 1)

            def add_up(c, b):
                bins = nc.values_load_multi_w_load_instructions(
                    g.BINI[0:1, k, ds(c * CH, CH)], engines=[v.engine], min_val=0, max_val=NB - 1,
                    skip_runtime_bounds_check_because="the table is cut at the last bin")[1]
                v.wait_ge(summed, c + 1)
                for j in range(CH):
                    if not (isinstance(c, int) and c == 0 and j == 0):
                        v.wait_ge(added, c * CH + j)
                    a = g.ACC[:, ds(bins[j], 1), 0:w]
                    v.tensor_tensor(a, a, agg_cell(pa, b, j)[:, 0:w], ALU.add).then_inc(added, 1)

            def chunk(c, i, b, first):
                one_hots(c, b, first)
                if not (first and b == 0):
                    add_up(c - 1, 1 - b)

            pairs(v, NI, chunk)
            add_up(2 * NI - 1, 1)
            v.wait_ge(added, NT)

        @block.tensor
        def _(pe):
            def chunk(c, i, b, first):
                pe.wait_ge(hot, c + 1)
                pe.wait_ge(gathered[b], i * (16 * CH) + 16 * CH)
                if weight:
                    pe.wait_ge(put, c + 1)
                if not first:
                    pe.wait_ge(added, (c - 1) * CH)
                for j in range(CH):
                    last = pe.matmul(agg_cell(pa, b, j)[:, 0:w], O[:, b, j, :], G[:, b, j, 0:w], start=True, stop=True)
                last.then_inc(summed, 1)

            pairs(pe, NI, chunk)



def load_rows(sp, sem, pairs_):
    for dst, src in pairs_:
        sp.dma_start(dst, src).then_inc(sem, 16)
    sp.wait_ge(sem, 16 * len(pairs_))


def attention_tables(nc, g, a, table, tag):
    with Space(nc, tag) as s:
        loaded, cleared = s.sem("loaded"), s.sem("cleared")
        held, turned, copied, made, scored, evac, packed = (s.sem(x) for x in (
            "held", "turned", "copied", "made", "scored", "evac", "packed"))
        W = s.sb("W", [P, 2, D])
        A = s.sb("A", [P, 4 * H])
        xs = s.sb("xs", [P, 2, D])
        xt = s.sb("xt", [P, 2, P])
        ht = s.sb("ht", [P, 2, P])
        row = s.sb("row", [P, 2, W0])
        pt = s.ps("pt", [P, 2, 512])
        pb = s.ps("pb", [P, 2, 512])
        pc = s.ps("pc", [P, 2, 512])
        stored = [s.sem(f"stored{b}") for b in (0, 1)]
        block = s.block()

        @block.sync
        def _(sp):
            sp.wait_ge(cleared, 1)
            with nc.allow_non_contiguous_dma(reason="attention vectors into a block diagonal, once"):
                for v_, vec in enumerate((a.a_in, a.a_out)):
                    for h in range(H):
                        for half in (0, 1):
                            col = (half * 2 + v_) * H + h
                            sp.dma_start(A[h * HD:(h + 1) * HD, col:col + 1],
                                         vec[h:h + 1, half * HD:(half + 1) * HD].rearrange("o d -> d o")).then_inc(loaded, 16)
            sp.dma_start(W[:, 0, :], a.W).then_inc(loaded, 16)
            sp.dma_start(W[:, 1, :], a.W_self).then_inc(loaded, 16)

            def store(n, i, b):
                sp.wait_ge(packed, n + 1)
                sp.dma_start(table[ds(n * P, P), :], row[:, b, :]).then_inc(stored[b], 16)

            pipeline(sp, NB, (store, 0))
            sp.wait_ge(stored[0], 16 * (NB - NB // 2))
            sp.wait_ge(stored[1], 16 * (NB // 2))

        @block.vector
        def _(v):
            v.memset(A[:, :], 0.0).then_inc(cleared, 1)

            def hold(n, i, b):
                if old(n):
                    v.wait_ge(turned, n - 1)
                move(v, xs[:, b, :], g.X[:, ds(n, 1), :]).then_inc(held, 1)

            def pack(n, i, b):
                v.wait_ge(scored, n + 1)
                if old(n):
                    v.wait_ge(stored[b], i * 16)
                v.tensor_copy(row[:, b, 0:D], pb[:, b, P:P + D])
                move(v, g.HH[:, ds(n, 1), :], pb[:, b, P + D:P + 2 * D])
                move(v, g.NS[:, ds(n, 1), :], pc[:, b, 2 * H:4 * H])
                v.tensor_copy(row[:, b, D:D + 2 * H], pc[:, b, 0:2 * H]).then_inc(packed, 1)

            pipeline(v, NB, (pack, 0), (hold, 3))

        @block.scalar
        def _(act):
            def copy(n, i, b):
                act.wait_ge(turned, n + 1)
                act.activation(xt[:, b, :], pt[:, b, 0:P], ACT.Copy).then_inc(copied, 1)

            def keep_projected(n, i, b):
                act.wait_ge(made, n + 1)
                act.activation(ht[:, b, :], pb[:, b, 0:P], ACT.Copy).then_inc(evac, 1)

            pipeline(act, NB, (keep_projected, 1), (copy, 2))

        @block.tensor
        def _(pe):
            pe.wait_ge(loaded, 16 * 18)

            def turn(n, i, b):
                pe.wait_ge(held, n + 1)
                pe.transpose(pt[:, b, 0:P], xs[:, b, :], g.ident[:, :]).then_inc(turned, 1)

            def products(n, i, b):
                pe.wait_ge(copied, n + 1)
                if old(n):
                    pe.wait_ge(packed, n - 1)
                pe.matmul(pb[:, b, 0:P], W[:, 0, :], xt[:, b, :], start=True, stop=True)
                pe.matmul(pb[:, b, P:P + 2 * D], xt[:, b, :], W[:, :, :].rearrange("p a d -> p (a d)"),
                          start=True, stop=True).then_inc(made, 1)

            def scores(n, i, b):
                pe.wait_ge(evac, n + 1)
                pe.matmul(pc[:, b, 0:4 * H], ht[:, b, :], A[:, :], start=True, stop=True).then_inc(scored, 1)

            pipeline(pe, NB, (products, 1), (scores, 0), (turn, 2))


def typed_product(nc, g, W, B, src, dst, tag):
    with Space(nc, tag) as s:
        loaded, masked, turned, copied, made, stored = (s.sem(x) for x in ("loaded", "masked", "turned", "copied", "made", "stored"))
        w = s.sb("w", [P, T, D])
        bias = s.sb("bias", [T, D])
        tm = s.sb("tm", [P, 2, T])
        xm = s.sb("xm", [P, 2, T, D])
        xt = s.sb("xt", [P, 2, T, P])
        mt = s.sb("mt", [T, 2, P])
        tms = s.sem("tms")
        pt = s.ps("pt", [P, 2, 512])
        pb = s.ps("pb", [P, 2, 512])
        block = s.block()

        @block.sync
        def _(sp):
            load_rows(sp, loaded, [(w[:, :, :], W.rearrange("t i o -> i t o")), (bias[:, :], B)])

        @block.vector
        def _(v):
            def stage(n, i, b):
                if old(n):
                    v.wait_ge(turned, n - 1)
                move(v, tm[:, b, :], g.TM[:, ds(n, 1), :]).then_inc(tms, 1)

            def mask(n, i, b):
                v.wait_ge(tms, n + 1)
                if old(n):
                    v.wait_ge(turned, n - 1)
                for t in range(T):
                    last = v.tensor_scalar(xm[:, b, t, :], src[:, ds(n, 1), 0:D], tm[:, b, t:t + 1], None, ALU.mult)
                last.then_inc(masked, 1)

            def store(n, i, b):
                v.wait_ge(made, n + 1)
                move(v, dst[:, ds(n, 1), 0:D], pb[:, b, 0:D]).then_inc(stored, 1)

            pipeline(v, NB, (mask, 2), (store, 0), (stage, 3))

        @block.scalar
        def _(act):
            def copy(n, i, b):
                act.wait_ge(turned, n + 1)
                if old(n):
                    act.wait_ge(made, n - 1)
                act.activation(xt[:, b, :, :].rearrange("p t n -> p (t n)"), pt[:, b, 0:T * P], ACT.Copy)
                act.activation(mt[:, b, :], pt[0:T, b, T * P:(T + 1) * P], ACT.Copy).then_inc(copied, 1)

            pipeline(act, NB, (copy, 0))

        @block.tensor
        def _(pe):
            pe.wait_ge(loaded, 32)

            def turn(n, i, b):
                pe.wait_ge(masked, n + 1)
                if old(n):
                    pe.wait_ge(copied, n - 1)
                for t in range(T):
                    pe.transpose(pt[:, b, t * P:(t + 1) * P], xm[:, b, t, :], g.ident[:, :])
                pe.transpose(pt[0:T, b, T * P:(T + 1) * P], tm[:, b, :], g.ident[:, :]).then_inc(turned, 1)

            def products(n, i, b):
                pe.wait_ge(copied, n + 1)
                if old(n):
                    pe.wait_ge(stored, n - 1)
                for t in range(T):
                    pe.matmul(pb[:, b, 0:D], xt[:, b, t, :], w[:, t, :], start=(t == 0), stop=False)
                pe.matmul(pb[:, b, 0:D], mt[:, b, :], bias[:, :], start=False, stop=True).then_inc(made, 1)

            pipeline(pe, NB, (turn, 1), (products, 0))


def hgt_tables(nc, g, a, l, table, tag):
    with Space(nc, tag) as s:
        loaded, cleared, scaled = s.sem("loaded"), s.sem("cleared"), s.sem("scaled")
        masked, turned, copied, made, evac, spread, packed_k, packed_v, tms, qdone = (s.sem(x) for x in (
            "masked", "turned", "copied", "made", "evac", "spread", "packed_k", "packed_v", "tms", "qdone"))
        w = s.sb("w", [P, 3, T, D])
        bias = s.sb("bias", [T, 3, D])
        bd = s.sb("bd", [P, 2, R, D])
        mu = s.sb("mu", [P, R * H])
        tm = s.sb("tm", [P, 2, T])
        xm = s.sb("xm", [P, 2, T, D])
        xt = s.sb("xt", [P, 2, T, P])
        mt = s.sb("mt", [T, 2, P])
        kv = s.sb("kv", [P, 2, 2, P])
        row = s.sb("row", [P, 2, R, 2 * D])
        pt = s.ps("pt", [P, 2, 512])
        pb = s.ps("pb", [P, 2, 512])
        pk = s.ps("pk", [P, 4, 512])
        stored = [s.sem(f"stored{b}") for b in (0, 1)]
        block = s.block()

        @block.sync
        def _(sp):
            for m, (Wm, Bm) in enumerate(((a.Wk, a.bk), (a.Wv, a.bv), (a.Wq, a.bq))):
                sp.dma_start(w[:, m, :, :], Wm[l].rearrange("t i o -> i t o")).then_inc(loaded, 16)
                sp.dma_start(bias[:, m, :], Bm[l]).then_inc(loaded, 16)
            sp.dma_start(mu[:, :], a.mu[l].rearrange("(o r) h -> o (r h)", o=1).to_broadcast([P, R * H])).then_inc(loaded, 16)
            sp.wait_ge(cleared, 1)
            for m, rel in enumerate((a.a_rel, a.m_rel)):
                for h in range(H):
                    sp.dma_start(bd[h * HD:(h + 1) * HD, m, :, h * HD:(h + 1) * HD],
                                 rel[l, :, h].rearrange("r d e -> d r e")).then_inc(loaded, 16)

            def store(n, i, b):
                sp.wait_ge(packed_k, n + 1)
                sp.wait_ge(packed_v, n + 1)
                sp.dma_start(table[ds(n * P, P), :, :].rearrange("p r w -> p (r w)"),
                             row[:, b, :, :].rearrange("p r w -> p (r w)")).then_inc(stored[b], 16)

            pipeline(sp, NB, (store, 0))
            sp.wait_ge(stored[0], 16 * (NB - NB // 2))
            sp.wait_ge(stored[1], 16 * (NB // 2))

        @block.vector
        def _(v):
            v.memset(bd[:, :, :, :], 0.0).then_inc(cleared, 1)
            v.wait_ge(loaded, 16 * 15)
            v.tensor_scalar(mu[:, :], mu[:, :], float(HD) ** -0.5, None, ALU.mult).then_inc(scaled, 1)
            v.wait_ge(scaled, 1)
            flat = bd[:, 0, :, :].rearrange("p r (h e) -> p (r h) e", h=H)
            v.tensor_tensor(flat, flat, cols3(mu[:, :]).to_broadcast([P, R * H, HD]), ALU.mult).then_inc(scaled, 1)

            def stage(n, i, b):
                if old(n):
                    v.wait_ge(turned, n - 1)
                move(v, tm[:, b, :], g.TM[:, ds(n, 1), :]).then_inc(tms, 1)

            def mask(n, i, b):
                v.wait_ge(tms, n + 1)
                if old(n):
                    v.wait_ge(turned, n - 1)
                for t in range(T):
                    last = v.tensor_scalar(xm[:, b, t, :], g.HH[:, ds(n, 1), :], tm[:, b, t:t + 1], None, ALU.mult)
                last.then_inc(masked, 1)

            def pack_keys(n, i, b):
                v.wait_ge(spread, n + 1)
                if old(n):
                    v.wait_ge(stored[b], i * 16)
                v.tensor_copy(row[:, b, :, 0:D], pk[:, 2 * b, :].rearrange("p (r w) -> p r w", r=R)).then_inc(packed_k, 1)

            pipeline(v, NB, (mask, 3), (pack_keys, 0), (stage, 4))

        @block.scalar
        def _(act):
            def copy(n, i, b):
                act.wait_ge(turned, n + 1)
                if old(n):
                    act.wait_ge(made, n - 1)
                act.activation(xt[:, b, :, :].rearrange("p t n -> p (t n)"), pt[:, b, 0:T * P], ACT.Copy)
                act.activation(mt[:, b, :], pt[0:T, b, T * P:(T + 1) * P], ACT.Copy).then_inc(copied, 1)

            def keep_projected(n, i, b):
                act.wait_ge(made, n + 1)
                if old(n):
                    act.wait_ge(spread, n - 1)
                act.activation(kv[:, b, :, :].rearrange("p m n -> p (m n)"), pb[:, b, 0:2 * P], ACT.Copy).then_inc(evac, 1)
                act.activation(g.QQ[:, ds(n, 1), :], pb[:, b, 2 * P:2 * P + D], ACT.Copy).then_inc(qdone, 1)

            def pack_values(n, i, b):
                act.wait_ge(spread, n + 1)
                if old(n):
                    act.wait_ge(stored[b], i * 16)
                act.activation(row[:, b, :, D:2 * D], pk[:, 2 * b + 1, :].rearrange("p (r w) -> p r w", r=R),
                               ACT.Copy).then_inc(packed_v, 1)

            pipeline(act, NB, (keep_projected, 1), (copy, 2), (pack_values, 0))

        @block.tensor
        def _(pe):
            pe.wait_ge(loaded, 16 * 15)
            pe.wait_ge(scaled, 2)

            def turn(n, i, b):
                pe.wait_ge(masked, n + 1)
                if old(n):
                    pe.wait_ge(copied, n - 1)
                for t in range(T):
                    pe.transpose(pt[:, b, t * P:(t + 1) * P], xm[:, b, t, :], g.ident[:, :])
                pe.transpose(pt[0:T, b, T * P:(T + 1) * P], tm[:, b, :], g.ident[:, :]).then_inc(turned, 1)

            def project(n, i, b):
                pe.wait_ge(copied, n + 1)
                if old(n):
                    pe.wait_ge(qdone, n - 1)
                    pe.wait_ge(evac, n - 1)
                for m in (0, 1):
                    o = pb[:, b, m * P:(m + 1) * P]
                    for t in range(T):
                        pe.matmul(o, w[:, m, t, :], xt[:, b, t, :], start=(t == 0), stop=False)
                    pe.matmul(o, bias[:, m, :], mt[:, b, :], start=False, stop=True)
                o = pb[:, b, 2 * P:2 * P + D]
                for t in range(T):
                    pe.matmul(o, xt[:, b, t, :], w[:, 2, t, :], start=(t == 0), stop=False)
                pe.matmul(o, mt[:, b, :], bias[:, 2, :], start=False, stop=True).then_inc(made, 1)

            def relate(n, i, b):
                pe.wait_ge(evac, n + 1)
                if old(n):
                    pe.wait_ge(packed_k, n - 1)
                    pe.wait_ge(packed_v, n - 1)
                for m in (0, 1):
                    last = pe.matmul(pk[:, 2 * b + m, :], kv[:, b, m, :],
                                     bd[:, m, :, :].rearrange("p r d -> p (r d)"), start=True, stop=True)
                last.then_inc(spread, 1)

            pipeline(pe, NB, (project, 1), (turn, 2), (relate, 0))


class Wide:

    def __init__(self, nc, g, s):
        self.nc, self.g, self.s = nc, g, s
        self.chain, self.ask, self.ans = s.sem("chain"), s.sem("ask"), s.sem("ans")
        self.loaded = s.sem("loaded")
        self.jobs = []

    def run(self, loads, body, stores=()):
        s = self.s
        block = s.block()
        stored = s.sem("stored")
        count = {}

        @block.sync
        def _(sp):
            if loads:
                load_rows(sp, self.loaded, loads)

        @block.vector
        def _(v):
            link = Chain(v, self.chain)
            if loads:
                v.wait_ge(self.loaded, 16 * len(loads))

            def fn(job):
                self.jobs.append((link.n, job))
                v.wait_ge(self.ans, len(self.jobs))

            body(v, link, fn)
            count["n"] = link.n

        @block.scalar
        def _(act):
            for n, (after, job) in enumerate(self.jobs):
                act.wait_ge(self.chain, after)
                job(act).then_inc(self.ans, 1)
            if stores:
                act.wait_ge(self.chain, count["n"])
                for dst, src in stores:
                    act.dma_start(dst, src).then_inc(stored, 16)
                act.wait_ge(stored, 16 * len(stores))


def norm_rows(v, link, fn, buf, sq, st):
    full = [P, NB, D]
    link(v.tensor_reduce(st[:, 0, :], buf, AX.X, ALU.add))
    link(v.tensor_scalar(st[:, 0, :], st[:, 0, :], -1.0 / D, None, ALU.mult))
    link(v.tensor_tensor(buf, buf, cols3(st[:, 0, :]).to_broadcast(full), ALU.add))
    link(v.tensor_tensor(sq, buf, buf, ALU.mult))
    link(v.tensor_reduce(st[:, 1, :], sq, AX.X, ALU.add))
    link(v.tensor_scalar(st[:, 1, :], st[:, 1, :], 1.0 / D, 1e-5, ALU.mult, ALU.add))
    fn(lambda act: act.activation(st[:, 2, :], st[:, 1, :], ACT.Sqrt))
    link(v.reciprocal(st[:, 2, :], st[:, 2, :]))
    link(v.tensor_tensor(buf, buf, cols3(st[:, 2, :]).to_broadcast(full), ALU.mult))


def row_of(ap):
    return ap.rearrange("(o d) -> o d", o=1).to_broadcast([P, D])


def by_tile(row):
    return row.rearrange("p (o d) -> p o d", o=1).to_broadcast([P, NB, D])


def attention_mean(v, link, g, eps, rec, dst):
    link(v.tensor_scalar(rec, g.ACC[:, :, D:D + H], eps, None, ALU.add))
    link(v.reciprocal(rec, rec))
    for h in range(H):
        last = v.tensor_tensor(dst[:, :, h * HD:(h + 1) * HD], g.ACC[:, :, h * HD:(h + 1) * HD],
                               rec[:, :, h:h + 1].to_broadcast([P, NB, HD]), ALU.mult)
    link(last)


def add_direction(nc, g, tag):
    with Space(nc, tag) as s:
        rec = s.sb("rec", [P, NB, H])
        sq = s.sb("sq", [P, NB, D])

        def body(v, link, fn):
            attention_mean(v, link, g, 1e-8, rec[:, :, :], sq)
            link(v.tensor_tensor(g.HH[:, :, :], g.HH[:, :, :], sq[:, :, :], ALU.add))

        Wide(nc, g, s).run([], body)


def close_l0(nc, g, a, tag):
    with Space(nc, tag) as s:
        sq = s.sb("sq", [P, NB, D])
        st = s.sb("st", [P, 3, NB])
        par = s.sb("par", [P, 3, D])

        def body(v, link, fn):
            hh = g.HH[:, :, :]
            link(v.tensor_tensor(hh, hh, by_tile(par[:, 0, :]), ALU.add))
            norm_rows(v, link, fn, hh, sq[:, :, :], st)
            link(v.tensor_tensor(hh, hh, by_tile(par[:, 1, :]), ALU.mult))
            link(v.tensor_tensor(hh, hh, by_tile(par[:, 2, :]), ALU.add))
            link(v.tensor_tensor(g.X[:, :, :], g.X[:, :, :], hh, ALU.add))
            norm_rows(v, link, fn, g.X[:, :, :], sq[:, :, :], st)

        Wide(nc, g, s).run([(par[:, 0, :], row_of(a.bias)), (par[:, 1, :], row_of(a.ln_gamma)),
                            (par[:, 2, :], row_of(a.ln_beta))], body)


def gelu_mean(nc, g, tag):
    c = 0.7978845608028654
    with Space(nc, tag) as s:
        rec = s.sb("rec", [P, NB, H])
        sq = s.sb("sq", [P, NB, D])

        def body(v, link, fn):
            x = g.ACC[:, :, 0:D]
            attention_mean(v, link, g, 1e-16, rec[:, :, :], g.ACC)
            link(v.tensor_tensor(sq[:, :, :], x, x, ALU.mult))
            link(v.tensor_scalar(sq[:, :, :], sq[:, :, :], 0.044715, 1.0, ALU.mult, ALU.add))
            link(v.tensor_tensor(sq[:, :, :], sq[:, :, :], x, ALU.mult))
            link(v.tensor_scalar(sq[:, :, :], sq[:, :, :], -2.0 * c, 80.0, ALU.mult, ALU.min))
            fn(lambda act: act.activation(sq[:, :, :], sq[:, :, :], ACT.Exp))
            link(v.tensor_scalar(sq[:, :, :], sq[:, :, :], 1.0, None, ALU.add))
            link(v.reciprocal(sq[:, :, :], sq[:, :, :]))
            link(v.tensor_tensor(x, x, sq[:, :, :], ALU.mult))

        Wide(nc, g, s).run([], body)


def blend_skip(nc, g, a, l, last_layer, tag):
    with Space(nc, tag) as s:
        sk = s.sb("sk", [P, T])
        gate = s.sb("gate", [P, 2, NB])
        sq = s.sb("sq", [P, NB, D])
        st = s.sb("st", [P, 3, NB])

        def body(v, link, fn):
            link(v.tensor_scalar(sk[:, :], sk[:, :], -1.0, None, ALU.mult))
            fn(lambda act: act.activation(sk[:, :], sk[:, :], ACT.Exp))
            link(v.tensor_scalar(sk[:, :], sk[:, :], 1.0, None, ALU.add))
            link(v.reciprocal(sk[:, :], sk[:, :]))
            link(v.tensor_scalar(gate[:, 0, :], g.TM[:, :, 0], sk[:, 0:1], None, ALU.mult))
            for t in range(1, T):
                link(v.scalar_tensor_tensor(out=gate[:, 0, :], in0=g.TM[:, :, t], scalar=sk[:, t:t + 1],
                                            in1=gate[:, 0, :], op0=ALU.mult, op1=ALU.add))
            link(v.tensor_scalar(gate[:, 1, :], gate[:, 0, :], -1.0, 1.0, ALU.mult, ALU.add))
            link(v.tensor_tensor(sq[:, :, :], g.ACC[:, :, 0:D], cols3(gate[:, 0, :]).to_broadcast([P, NB, D]), ALU.mult))
            link(v.tensor_tensor(g.HH[:, :, :], g.HH[:, :, :], cols3(gate[:, 1, :]).to_broadcast([P, NB, D]), ALU.mult))
            link(v.tensor_tensor(g.HH[:, :, :], g.HH[:, :, :], sq[:, :, :], ALU.add))
            if last_layer:
                link(v.tensor_tensor(g.X[:, :, :], g.X[:, :, :], g.HH[:, :, :], ALU.add))
                norm_rows(v, link, fn, g.X[:, :, :], sq[:, :, :], st)

        Wide(nc, g, s).run([(sk[:, :], a.skip[l].rearrange("(o t) -> o t", o=1).to_broadcast([P, T]))], body)


def gcn_table(nc, g, a, table, tag):
    with Space(nc, tag) as s:
        loaded, root, chain, held, turned, copied, made, packed, staged = (s.sem(x) for x in (
            "loaded", "root", "chain", "held", "turned", "copied", "made", "packed", "staged"))
        W = s.sb("W", [P, D])
        xs = s.sb("xs", [P, 2, D])
        xt = s.sb("xt", [P, 2, P])
        row = s.sb("row", [P, 2, D])
        dv = s.sb("dv", [P, 2, 1])
        pt = s.ps("pt", [P, 2, 512])
        pb = s.ps("pb", [P, 2, 512])
        stored = [s.sem(f"stored{b}") for b in (0, 1)]
        block = s.block()

        @block.sync
        def _(sp):
            sp.dma_start(W[:, :], a.W2).then_inc(loaded, 16)

            def store(n, i, b):
                sp.wait_ge(packed, n + 1)
                sp.dma_start(table[ds(n * P, P), :], row[:, b, :]).then_inc(stored[b], 16)

            pipeline(sp, NB, (store, 0))
            sp.wait_ge(stored[0], 16 * (NB - NB // 2))
            sp.wait_ge(stored[1], 16 * (NB // 2))

        @block.vector
        def _(v):
            link = Chain(v, chain)
            link(v.tensor_scalar(g.DINV[:, :], g.CNT[:, 1, :], 1.0, None, ALU.add))
            v.wait_ge(root, 1)
            link(v.reciprocal(g.DINV[:, :], g.DINV[:, :]))

            def hold(n, i, b):
                if old(n):
                    v.wait_ge(turned, n - 1)
                move(v, xs[:, b, :], g.X[:, ds(n, 1), :]).then_inc(held, 1)

            def stage(n, i, b):
                if old(n):
                    v.wait_ge(packed, n - 1)
                move(v, dv[:, b, :], g.DINV[:, ds(n, 1)]).then_inc(staged, 1)

            def pack(n, i, b):
                v.wait_ge(staged, n + 1)
                v.wait_ge(made, n + 1)
                if old(n):
                    v.wait_ge(stored[b], i * 16)
                v.tensor_scalar(g.ACC[:, ds(n, 1), 0:D], pb[:, b, 0:D], dv[:, b, :], None, ALU.mult)
                v.tensor_scalar(row[:, b, :], pb[:, b, 0:D], dv[:, b, :], None, ALU.mult).then_inc(packed, 1)

            pipeline(v, NB, (stage, 1), (pack, 0), (hold, 3))

        @block.scalar
        def _(act):
            act.wait_ge(chain, 1)
            act.activation(g.DINV[:, :], g.DINV[:, :], ACT.Sqrt).then_inc(root, 1)

            def copy(n, i, b):
                act.wait_ge(turned, n + 1)
                if old(n):
                    act.wait_ge(made, n - 1)
                act.activation(xt[:, b, :], pt[:, b, 0:P], ACT.Copy).then_inc(copied, 1)

            pipeline(act, NB, (copy, 0))

        @block.tensor
        def _(pe):
            pe.wait_ge(loaded, 16)

            def turn(n, i, b):
                pe.wait_ge(held, n + 1)
                if old(n):
                    pe.wait_ge(copied, n - 1)
                pe.transpose(pt[:, b, 0:P], xs[:, b, :], g.ident[:, :]).then_inc(turned, 1)

            def product(n, i, b):
                pe.wait_ge(copied, n + 1)
                if old(n):
                    pe.wait_ge(packed, n - 1)
                pe.matmul(pb[:, b, 0:D], xt[:, b, :], W[:, :], start=True, stop=True).then_inc(made, 1)

            pipeline(pe, NB, (turn, 1), (product, 0))


def close_l2(nc, g, a, table, tag):
    with Space(nc, tag) as s:
        sq = s.sb("sq", [P, NB, D])
        st = s.sb("st", [P, 3, NB])
        par = s.sb("par", [P, D])

        def body(v, link, fn):
            x, y = g.X[:, :, :], sq[:, :, :]
            link(v.tensor_tensor(y, g.ACC[:, :, 0:D], cols3(g.DINV[:, :]).to_broadcast([P, NB, D]), ALU.mult))
            link(v.tensor_tensor(y, y, by_tile(par[:, :]), ALU.add))
            link(v.scalar_tensor_tensor(out=y, in0=y, scalar=0.1, in1=y, op0=ALU.mult, op1=ALU.max))
            link(v.tensor_tensor(y, y, x, ALU.add))
            link(v.tensor_tensor(x, x, y, ALU.add))
            norm_rows(v, link, fn, x, y, st)
            link(v.memset(g.ACC[:, :, :], 0.0))

        Wide(nc, g, s).run([(par[:, :], row_of(a.b2g))], body, [(rows(table), g.X[:, :, :])])


def gine_input(nc, g, a, tag):
    with Space(nc, tag) as s:
        sq = s.sb("sq", [P, NB, D])
        cn = s.sb("cn", [P, NB])
        ew = s.sb("ew", [P, D])
        eb = s.sb("eb", [P, D])
        ep = s.sb("ep", [P, 1])

        def body(v, link, fn):
            full = [P, NB, D]
            y, hh = sq[:, :, :], g.HH[:, :, :]
            cnt = g.CNT[:, 1, :]
            link(v.tensor_tensor(y, g.ACC[:, :, D:D + 1].to_broadcast(full), by_tile(ew[:, :]), ALU.mult))
            link(v.tensor_tensor(hh, g.ACC[:, :, 0:D], y, ALU.add))
            link(v.tensor_tensor(y, cols3(cnt).to_broadcast(full), by_tile(eb[:, :]), ALU.mult))
            link(v.tensor_tensor(hh, hh, y, ALU.add))
            link(v.tensor_scalar(cn[:, :], cnt, 1.0, None, ALU.max))
            link(v.reciprocal(cn[:, :], cn[:, :]))
            link(v.tensor_tensor(hh, hh, cols3(cn[:, :]).to_broadcast(full), ALU.mult))
            link(v.tensor_scalar(ep[:, :], ep[:, :], 1.0, None, ALU.add))
            link(v.tensor_scalar(y, g.X[:, :, :], ep[:, 0:1], None, ALU.mult))
            link(v.tensor_tensor(hh, hh, y, ALU.add))

        Wide(nc, g, s).run([(ew[:, :], a.edge_w.to_broadcast([P, D])), (eb[:, :], row_of(a.edge_b)),
                            (ep[:, :], a.eps.rearrange("(o d) -> o d", o=1).to_broadcast([P, 1]))], body)


def gine_mlp(nc, g, a, tag):
    with Space(nc, tag) as s:
        loaded, held, turned, copied, made, relu, out, stored = (s.sem(x) for x in (
            "loaded", "held", "turned", "copied", "made", "relu", "out", "stored"))
        w = s.sb("w", [P, 3, D])
        b1 = s.sb("b1", [P, 1])
        b2 = s.sb("b2", [1, 2, D])
        xs = s.sb("xs", [P, 2, 2, D])
        xt = s.sb("xt", [P, 2, 2, P])
        zt = s.sb("zt", [P, 2, P])
        pt = s.ps("pt", [P, 2, 512])
        pz = s.ps("pz", [P, 2, 512])
        po = s.ps("po", [P, 2, 512])
        block = s.block()

        @block.sync
        def _(sp):
            with nc.allow_non_contiguous_dma(reason="one bias word a partition, once"):
                load_rows(sp, loaded, [(w[:, 0, :], a.w1), (w[:, 1, :], a.w2), (w[:, 2, :], a.res_w),
                                       (b1[:, :], a.b1.rearrange("(d o) -> d o", o=1)),
                                       (b2[:, 0, :], a.b2.rearrange("(o d) -> o d", o=1)),
                                       (b2[:, 1, :], a.res_b.rearrange("(o d) -> o d", o=1))])

        @block.vector
        def _(v):
            v.wait_ge(loaded, 96)

            def hold(n, i, b):
                if old(n):
                    v.wait_ge(turned, n - 1)
                move(v, xs[:, b, 0, :], g.HH[:, ds(n, 1), :])
                move(v, xs[:, b, 1, :], g.X[:, ds(n, 1), :]).then_inc(held, 1)

            def store(n, i, b):
                v.wait_ge(out, n + 1)
                move(v, g.HH[:, ds(n, 1), :], po[:, b, 0:D]).then_inc(stored, 1)

            pipeline(v, NB, (store, 0), (hold, 3))

        @block.scalar
        def _(act):
            act.wait_ge(loaded, 96)

            def copy(n, i, b):
                act.wait_ge(turned, n + 1)
                if old(n):
                    act.wait_ge(out, n - 1)
                act.activation(xt[:, b, :, :].rearrange("p t n -> p (t n)"), pt[:, b, 0:2 * P], ACT.Copy).then_inc(copied, 1)

            def rectify(n, i, b):
                act.wait_ge(made, n + 1)
                act.activation(zt[:, b, :], pz[:, b, 0:P], ACT.Relu, bias=b1[:, 0:1]).then_inc(relu, 1)

            pipeline(act, NB, (rectify, 1), (copy, 2))

        @block.tensor
        def _(pe):
            pe.wait_ge(loaded, 96)

            def turn(n, i, b):
                pe.wait_ge(held, n + 1)
                if old(n):
                    pe.wait_ge(copied, n - 1)
                pe.transpose(pt[:, b, 0:P], xs[:, b, 0, :], g.ident[:, :])
                pe.transpose(pt[:, b, P:2 * P], xs[:, b, 1, :], g.ident[:, :]).then_inc(turned, 1)

            def first_layer(n, i, b):
                pe.wait_ge(copied, n + 1)
                if old(n):
                    pe.wait_ge(relu, n - 1)
                pe.matmul(pz[:, b, 0:P], w[:, 0, :], xt[:, b, 0, :], start=True, stop=True).then_inc(made, 1)

            def second_layer(n, i, b):
                pe.wait_ge(relu, n + 1)
                if old(n):
                    pe.wait_ge(stored, n - 1)
                o = po[:, b, 0:D]
                pe.matmul(o, zt[:, b, :], w[:, 1, :], start=True, stop=False)
                pe.matmul(o, xt[:, b, 1, :], w[:, 2, :], start=False, stop=False)
                pe.matmul(o, g.ones[0:1, :], b2[:, 0, :], start=False, stop=False)
                pe.matmul(o, g.ones[0:1, :], b2[:, 1, :], start=False, stop=True).then_inc(out, 1)

            pipeline(pe, NB, (first_layer, 1), (turn, 2), (second_layer, 0))


def close_l3(nc, g, a, out, tag):
    with Space(nc, tag) as s:
        chain, ask, ans, loaded, stored, made = (s.sem(x) for x in ("chain", "ask", "ans", "loaded", "stored", "made"))
        sq = s.sb("sq", [P, NB, D])
        st = s.sb("st", [P, 3, NB])
        valid = s.sb("valid", [P, NB])
        part = s.sb("part", [P, D])
        stat = s.sb("stat", [P, 2, D])
        par = s.sb("par", [P, 2, D])
        ps = s.ps("ps", [P, 512])
        block = s.block()
        jobs, sums, ends = [], [], []

        @block.gpsimd
        def _(pool):
            pool.iota(valid[:, :], pattern=[[P, NB]], base=0, channel_multiplier=1,
                      allow_small_or_imprecise_dtypes=True).then_inc(made, 1)

        @block.vector
        def _(v):
            link = Chain(v, chain)
            hh, y = g.HH[:, :, :], sq[:, :, :]
            v.wait_ge(made, 1)
            v.wait_ge(loaded, 32)
            link(v.tensor_scalar(valid[:, :], valid[:, :], float(N), None, ALU.is_lt))

            def mean_of(src, dst):
                link(v.tensor_reduce(part[:, :], src.rearrange("p n d -> p d n"), AX.X, ALU.add))
                sums.append(link.n)
                v.wait_ge(ask, len(sums))
                link(v.tensor_scalar(dst, ps[:, 0:D], 1.0 / N, None, ALU.mult))

            def fn(job):
                jobs.append((link.n, job))
                v.wait_ge(ans, len(jobs))

            mask = cols3(valid[:, :]).to_broadcast([P, NB, D])
            link(v.tensor_tensor(hh, hh, mask, ALU.mult))
            mean_of(hh, stat[:, 0, :])
            link(v.tensor_tensor(hh, hh, by_tile(stat[:, 0, :]), ALU.subtract))
            link(v.tensor_tensor(y, hh, hh, ALU.mult))
            link(v.tensor_tensor(y, y, mask, ALU.mult))
            mean_of(y, stat[:, 1, :])
            link(v.tensor_scalar(stat[:, 1, :], stat[:, 1, :], 1e-5, None, ALU.add))
            fn(lambda act: act.activation(stat[:, 1, :], stat[:, 1, :], ACT.Sqrt))
            link(v.reciprocal(stat[:, 1, :], stat[:, 1, :]))
            link(v.tensor_tensor(stat[:, 1, :], stat[:, 1, :], par[:, 0, :], ALU.mult))
            link(v.tensor_tensor(hh, hh, by_tile(stat[:, 1, :]), ALU.mult))
            link(v.tensor_tensor(hh, hh, by_tile(par[:, 1, :]), ALU.add))
            link(v.scalar_tensor_tensor(out=g.X[:, :, :], in0=hh, scalar=0.0, in1=g.X[:, :, :], op0=ALU.max, op1=ALU.add))
            norm_rows(v, link, fn, g.X[:, :, :], y, st)
            ends.append(link.n)

        @block.scalar
        def _(act):
            for after, job in jobs:
                act.wait_ge(chain, after)
                job(act).then_inc(ans, 1)

        @block.tensor
        def _(pe):
            for after in sums:
                pe.wait_ge(chain, after)
                pe.matmul(ps[:, 0:D], g.ones[:, :], part[:, :], start=True, stop=True).then_inc(ask, 1)

        @block.sync
        def _(sp):
            sp.dma_start(par[:, 0, :], row_of(a.gamma)).then_inc(loaded, 16)
            sp.dma_start(par[:, 1, :], row_of(a.beta)).then_inc(loaded, 16)
            sp.wait_ge(chain, ends[0])
            sp.dma_start(out[0:(NB - 1) * P, :].rearrange("(n p) w -> p n w", p=P), g.X[:, 0:NB - 1, :]).then_inc(stored, 16)
            sp.dma_start(out[(NB - 1) * P:N, :], g.X[0:N - (NB - 1) * P, NB - 1, :]).then_inc(stored, 16)
            sp.wait_ge(stored, 32)
            sp.wait_ge(loaded, 32)


class Args:
    pass


def gnn_kernel(nc, a, out):
    g = Args()
    with ExitStack() as ctx:
        def sb(name, shape, dt=F32):
            return ctx.enter_context(nc.sbuf_tensor(name, shape, dt))

        def dram(name, shape, dt=F32):
            return nc.dram_tensor(name, shape, dt, kind="Internal").ap()

        g.X = sb("X", [P, NB, D])
        g.ident = sb("ident", [P, P])
        g.ident_b = sb("ident_b", [P, P], BF16)
        g.iota = sb("iota", [P, P])
        g.iota_b = sb("iota_b", [P, P], BF16)
        g.ones = sb("ones", [P, P])
        g.TM = sb("TM", [P, NB, T])
        g.CNT = sb("CNT", [P, 2, NB])
        g.DINV = sb("DINV", [P, NB])
        g.BINI = sb("BINI", [1, 2, NT], I32)
        g.TF = sb("TF", [P, 2, 2, NT])
        g.LOCAL = sb("LOCAL", [P, 2, NTP])
        g.LAST = sb("LAST", [P, 2, NTP])
        g.OTHER = sb("OTHER", [P, 2, NTP])
        g.KVROW = sb("KVROW", [P, NTP])
        g.WEIGHT = sb("WEIGHT", [P, NTP])

        slots = [[dram(f"slots{k}{q}", (P * NT, RW)) for q in range(4)] for k in (0, 1)]
        flags = [dram(f"flags{k}", (P, TB * P)) for k in (0, 1)]
        stash = [dram(f"stash{k}", (NT // CH, P, CH * D)) for k in (0, 1)]
        table0 = dram("table0", (NP, W0))
        table1 = dram("table1", (NP, R, 2 * D))
        table2 = dram("table2", (NP, D))
        table3 = dram("table3", (NP, D))

        with ExitStack() as sort:
            def sbs(name, shape, dt=F32):
                return sort.enter_context(nc.sbuf_tensor(name, shape, dt))

            g.before = sbs("before", [P, P])
            g.zeros = sbs("zeros", [P, P])
            g.START = sbs("START", [P, 2, NB])
            g.NODE = sbs("NODE", [P, 2, EC])
            g.DIG = sbs("DIG", [P, 2, EC, 2])
            g.ET = sbs("ET", [P, EC])
            g.EW = sbs("EW", [P, EC])
            g.BIN = sbs("BIN", [P, 2, NT])
            load_inputs(nc, g, a)
            for k in (0, 1):
                count_keys(nc, g, k, f"cnt{k}")
                place_edges(nc, g, k, slots[k], f"plc{k}")
        for k in (0, 1):
            slot_tables(nc, g, k, slots[k], flags[k], f"tab{k}")

        g.HH = sb("HH", [P, NB, D])
        g.NS = sb("NS", [P, NB, 2 * H])

        def attention(k, tag, *gather):
            with nc.sbuf_tensor(f"{tag}_LG", [P, NTP, H], F32) as g.LG:
                clear_tail(nc, g, f"{tag}_clr")
                if gather[0] is table0:
                    edge_logits(nc, g, k, *gather, stash[k], f"{tag}_log")
                else:
                    g.QQ = g.ACC[:, :, 0:D]
                    hgt_tables(nc, g, a, gather[1], table1, f"{tag}_kv")
                    edge_logits(nc, g, k, table1.rearrange("n r w -> (n r) w"), 2 * D, g.KVROW, g.QQ, D, 0, D,
                                stash[k], f"{tag}_log")
                with nc.sbuf_tensor(f"{tag}_MXP", [P, 3, NTP, H + 1], BF16) as g.MXP:
                    with nc.sbuf_tensor(f"{tag}_MX", [P, NTP, H], F32) as g.MX:
                        segment_max(nc, g, k, flags[k], f"{tag}_max")
                    edge_sums(nc, g, k, stash[k], f"{tag}_sum")

        attention_tables(nc, g, a, table0, "l0t")
        with nc.sbuf_tensor("ACC0", [P, NB, D + H], F32) as acc:
            g.ACC = acc
            attention(1, "l0i", table0, W0, g.OTHER[:, 1, :], g.NS[:, :, 0:H], H, D, 0)
            add_direction(nc, g, "l0ia")
            attention(0, "l0o", table0, W0, g.OTHER[:, 0, :], g.NS[:, :, H:2 * H], H, D + H, 0)
            add_direction(nc, g, "l0oa")
        close_l0(nc, g, a, "l0c")

        typed_product(nc, g, a.W_in, a.b_in, g.X, g.HH, "l1i")
        for l in (0, 1):
            with nc.sbuf_tensor(f"ACC1{l}", [P, NB, D + H], F32) as acc:
                g.ACC = acc
                attention(1, f"l1{l}", table1, l)
                gelu_mean(nc, g, f"l1{l}g")
                typed_product(nc, g, a.Wa[l], a.ba[l], acc, acc, f"l1{l}a")
                blend_skip(nc, g, a, l, l == 1, f"l1{l}b")

        with nc.sbuf_tensor("ACC2", [P, NB, D + H], F32) as acc:
            g.ACC = acc
            gcn_table(nc, g, a, table2, "l2t")
            plain_sums(nc, g, table2, False, "l2s")
            close_l2(nc, g, a, table3, "l2c")
            plain_sums(nc, g, table3, True, "l3s")
            gine_input(nc, g, a, "l3i")
            gine_mlp(nc, g, a, "l3m")
            close_l3(nc, g, a, out, "l3c")


def clear_tail(nc, g, tag):
    with Space(nc, tag) as s:
        done = s.sem("done")
        block = s.block()

        @block.vector
        def _(v):
            v.memset(g.LG[:, NT:NTP, :], -BIG).then_inc(done, 1)
            v.wait_ge(done, 1)


_NAMES = {
    "x": "x", "src": "src", "dst": "dst", "edge_type_4": "edge_type", "edge_weight1": "edge_weight",
    "node_type_3": "node_type",
    "L0_gnn_W": "W", "L0_gnn_W_self": "W_self", "L0_gnn_a_in": "a_in", "L0_gnn_a_out": "a_out",
    "L0_gnn_bias": "bias", "L0_gnn_ln_gamma": "ln_gamma", "L0_gnn_ln_beta": "ln_beta",
    "L1_gnn_W_in": "W_in", "L1_gnn_b_in": "b_in", "L1_gnn_Wk": "Wk", "L1_gnn_bk": "bk", "L1_gnn_Wq": "Wq",
    "L1_gnn_bq": "bq", "L1_gnn_Wv": "Wv", "L1_gnn_bv": "bv", "L1_gnn_Wa": "Wa", "L1_gnn_ba": "ba",
    "L1_gnn_a_rel": "a_rel", "L1_gnn_m_rel": "m_rel", "L1_gnn_mu": "mu", "L1_gnn_skip": "skip",
    "L2_gnn_W": "W2", "L2_gnn_b": "b2g",
    "L3_gnn_edge_w": "edge_w", "L3_gnn_edge_b": "edge_b", "L3_gnn_w1": "w1", "L3_gnn_b1": "b1", "L3_gnn_w2": "w2",
    "L3_gnn_b2": "b2", "L3_gnn_res_w": "res_w", "L3_gnn_res_b": "res_b", "L3_gnn_eps": "eps",
    "L3_gnn_gamma": "gamma", "L3_gnn_beta": "beta",
}


def kernel(**inputs):
    import numpy as _np
    import concourse.bacc as _bacc
    from concourse import mybir as _mybir
    from concourse.bass_utils import run_bass_kernel_spmd as _run

    nc = _bacc.Bacc("TRN2", target_bir_lowering=False, num_devices=1)
    arrays, a = {}, Args()
    for name, short in _NAMES.items():
        v = _np.ascontiguousarray(inputs[name])
        arrays[f"in_{name}"] = v
        a.__dict__[short] = nc.dram_tensor(f"in_{name}", v.shape, _mybir.dt.from_np(v.dtype), kind="ExternalInput").ap()
    out = nc.dram_tensor("out_dram", (N, D), F32, kind="ExternalOutput").ap()
    gnn_kernel(nc, a, out)
    r = _run(nc, [arrays], core_ids=[0])
    return r.results[0]["out_dram"]
```
